# Optimizing a Trainium2 kernel written in Bass

```python
import numpy as np
import jax
import jax.numpy as jnp

def _softmax(x, axis=-1):
    return jax.nn.softmax(x, axis=axis)

def _gelu(x):
    return jax.nn.gelu(x, approximate=True)

def _silu(x):
    return jax.nn.silu(x)

def _sigmoid(x):
    return jax.nn.sigmoid(x)

def _layernorm(x, axis=-1, eps=1e-05):
    m = jnp.mean(x, axis=axis, keepdims=True)
    v = jnp.var(x, axis=axis, keepdims=True)
    return (x - m) / jnp.sqrt(v + eps)

def _scatter_add(tgt, idx, src, axis=0):
    return tgt.at[idx].add(src)

def _segment_sum(src, seg, n):
    return jax.ops.segment_sum(src, seg, n)
kernel_name = 'mk_flamingo_gated_d4_seqx_r8_5eaf88'

def setup_inputs(seed: int=0):
    np.random.seed(seed)
    _w = jnp.asarray

    def _rec_inputs():
        import jax
        import jax.numpy as jnp
        _rk = jax.random.key(seed)
        x = -0.0002928 + 1 * jax.random.normal(jax.random.fold_in(_rk, 1), (4, 256, 128), jnp.float32)
        _lenS = 256 - jax.random.randint(jax.random.fold_in(_rk, 7), (4,), 0, max(1, 256 // 4) + 1, jnp.int32)
        _lenS2 = 256 - jax.random.randint(jax.random.fold_in(_rk, 8), (4,), 0, max(1, 256 // 4) + 1, jnp.int32)
        _ctx_1024P = jax.random.normal(jax.random.fold_in(_rk, 11), (4, 16, 128), jnp.float32)
        _ctx_1024c = jax.random.dirichlet(jax.random.fold_in(_rk, 511), 0.3 * jnp.ones((16,), jnp.float32), (4, 256))
        _ctx_1024t = jnp.einsum('bsk,bkd->bsd', _ctx_1024c, _ctx_1024P)
        _ctx_1024t = _ctx_1024t * jax.lax.rsqrt(jnp.mean(jnp.square(_ctx_1024t)) + 1e-12) * 0.953939
        ctx_1024 = -1.39393e-06 + 0.999914 * (_ctx_1024t + 0.3 * jax.random.normal(jax.random.fold_in(_rk, 611), (4, 256, 128), jnp.float32))
        _validS = jnp.arange(256)[None, :] < _lenS[:, None]
        _validS2 = jnp.arange(256)[None, :] < _lenS2[:, None]
        _causal = jnp.tril(jnp.ones((256, 256), dtype=bool))
        mask_SxS2_ff1 = jnp.where(jnp.ones((256, 256), dtype=bool), 1.0, 0.0).astype(jnp.float32)
        _g = jax.random.normal(jax.random.fold_in(_rk, 9001), (2, 4), jnp.float32)
        _g = jnp.sign(_g) * jnp.maximum(jnp.abs(_g), 1.0) + (_g == 0) * 1.0
        g_xattn = _g[0]
        g_ffn = _g[1]
        return (x, ctx_1024, mask_SxS2_ff1, g_xattn, g_ffn)
    x, ctx_1024, mask_SxS2_ff1, g_xattn, g_ffn = _rec_inputs()

    def _L0_xattn_setup():
        import jax, jax.numpy as jnp
        import numpy as np
        B, N, M, D_MODEL, H, DH, D_OUT = (2, 256, 256, 128, 16, 64, 128)
        key0 = jax.random.key(seed)
        ks = jax.random.split(key0, 12)
        s_in = 1.0 / np.sqrt(D_MODEL)
        s_pr = 1.0 / np.sqrt(DH * H)
        return {'query': jax.random.normal(ks[0], (B, N, D_MODEL), jnp.float32), 'key': jax.random.normal(ks[1], (B, M, D_MODEL), jnp.float32), 'value': jax.random.normal(ks[2], (B, M, D_MODEL), jnp.float32), 'mask': jnp.ones((N, M), jnp.float32), 'Wq': jax.random.normal(ks[3], (H, D_MODEL, DH), jnp.float32) * s_in, 'bq': jnp.zeros((H, DH), jnp.float32), 'Wk': jax.random.normal(ks[4], (H, D_MODEL, DH), jnp.float32) * s_in, 'bk': jnp.zeros((H, DH), jnp.float32), 'Wv': jax.random.normal(ks[5], (H, D_MODEL, DH), jnp.float32) * s_in, 'bv': jnp.zeros((H, DH), jnp.float32), 'Wo': jax.random.normal(ks[6], (DH * H, D_OUT), jnp.float32) * s_pr, 'bo': jnp.zeros((D_OUT,), jnp.float32)}
    _L0_xattn_all = _L0_xattn_setup()
    _L0_xattn_in = {k: v for k, v in _L0_xattn_all.items() if k in ('Wq', 'bq', 'Wk', 'bk', 'Wv', 'bv', 'Wo', 'bo')}
    del _L0_xattn_all

    def _L0_ffn_setup():
        import jax, jax.numpy as jnp
        import numpy as np
        DIM = 128
        DEPTH = 6
        HEADS = 16
        DIM_HEAD = 64
        WINDOW = 32
        INNER = HEADS * DIM_HEAD
        DIM_INNER = int(DIM * 4 * 2 / 3)
        QK_SCALE = 8.0

        def shift_tokens(t):
            a, s = jnp.split(t, 2, -1)
            s = jnp.pad(s, ((0, 0), (1, 0), (0, 0)))[:, :-1]
            return jnp.concatenate([a, s], -1)

        def l2norm(t):
            return t / jnp.maximum(jnp.linalg.norm(t, axis=-1, keepdims=True), 1e-12)

        def rotate_half(x):
            x1, x2 = jnp.split(x, 2, -1)
            return jnp.concatenate([-x2, x1], -1)

        def rotary_tables(n):
            half = jnp.arange(0, DIM_HEAD, 2, dtype=jnp.float32)
            inv_freq = 1.0 / 10000.0 ** (half / DIM_HEAD)
            t = jnp.arange(n, dtype=jnp.float32)
            freqs = t[:, None] * inv_freq[None, :]
            freqs = jnp.concatenate([freqs, freqs], -1)
            base_scale = (half + 0.4 * DIM_HEAD) / (1.4 * DIM_HEAD)
            power = (t - n // 2) / (WINDOW // 2)
            scale = base_scale[None, :] ** power[:, None]
            scale = jnp.concatenate([scale, scale], -1)
            return (freqs, scale)

        def local_attention(q, k, v):
            b, h, n, d = q.shape
            w = WINDOW
            nw = n // w
            bq = q.reshape(b, h, nw, w, d)
            bk = k.reshape(b, h, nw, w, d)
            bv = v.reshape(b, h, nw, w, d)

            def look(t):
                p = jnp.pad(t, ((0, 0), (0, 0), (1, 0), (0, 0), (0, 0)))
                return jnp.concatenate([p[:, :, :nw], p[:, :, 1:]], axis=3)
            bk2, bv2 = (look(bk), look(bv))
            seq = jnp.arange(n).reshape(nw, w)
            seq_p = jnp.pad(seq, ((1, 0), (0, 0)), constant_values=-1)
            jt = jnp.concatenate([seq_p[:nw], seq_p[1:]], axis=1)
            it = seq[:, :, None]
            jb = jt[:, None, :]
            mask = (it < jb) | (it > jb + w) | (jb == -1)
            sim = jnp.einsum('bhwie,bhwje->bhwij', bq, bk2) * QK_SCALE
            sim = jnp.where(mask, -jnp.finfo(sim.dtype).max, sim)
            attn = jax.nn.softmax(sim, -1)
            out = jnp.einsum('bhwij,bhwje->bhwie', attn, bv2)
            return out.reshape(b, h, n, d)

        def attn_layer(x, Wqkv, qs, ksc, Wo):
            b, n, _ = x.shape
            qkv = x @ Wqkv
            q, k, v = jnp.split(qkv, 3, -1)
            sh = lambda t: t.reshape(b, n, HEADS, DIM_HEAD).transpose(0, 2, 1, 3)
            q, k, v = (sh(q), sh(k), sh(v))
            q = l2norm(q) * qs
            k = l2norm(k) * ksc
            freqs, scale = rotary_tables(n)
            cos, sin = (jnp.cos(freqs), jnp.sin(freqs))
            q = q * cos * scale + rotate_half(q) * sin * scale
            inv = 1.0 / scale
            k = k * cos * inv + rotate_half(k) * sin * inv
            out = local_attention(q, k, v)
            out = out.transpose(0, 2, 1, 3).reshape(b, n, INNER)
            return out @ Wo

        def ffn_layer(x, g, bln, W1, b1, W2, b2):
            mu = x.mean(-1, keepdims=True)
            var = ((x - mu) ** 2).mean(-1, keepdims=True)
            xn = (x - mu) / jnp.sqrt(var + 1e-05) * g + bln
            hg = xn @ W1 + b1
            a, gate = jnp.split(hg, 2, -1)
            return a * jax.nn.gelu(gate, approximate=False) @ W2 + b2
        key = jax.random.key(seed)
        ks = jax.random.split(key, 8)
        B, N = (2, 256)
        init = lambda k, shape: jax.random.normal(k, shape, jnp.float32) * 0.02
        return {'x': jax.random.normal(ks[0], (B, N, DIM), jnp.float32), 'Wqkv': init(ks[1], (DEPTH, DIM, 3 * INNER)), 'q_scale': jnp.ones((DEPTH, DIM_HEAD), jnp.float32), 'k_scale': jnp.ones((DEPTH, DIM_HEAD), jnp.float32), 'Wo': init(ks[2], (DEPTH, INNER, DIM)), 'ln_g': jnp.ones((DEPTH, DIM), jnp.float32), 'ln_b': jnp.zeros((DEPTH, DIM), jnp.float32), 'W1': init(ks[3], (DEPTH, DIM, 2 * DIM_INNER)), 'b1': jnp.zeros((DEPTH, 2 * DIM_INNER), jnp.float32), 'W2': init(ks[4], (DEPTH, DIM_INNER, DIM)), 'b2': jnp.zeros((DEPTH, DIM), jnp.float32)}
    _L0_ffn_all = _L0_ffn_setup()
    _L0_ffn_in = {k: v for k, v in _L0_ffn_all.items() if k in ('Wqkv', 'q_scale', 'k_scale', 'Wo', 'ln_g', 'ln_b', 'W1', 'b1', 'W2', 'b2')}
    del _L0_ffn_all

    def _L1_xattn_setup():
        import jax, jax.numpy as jnp
        import numpy as np
        H = 128
        B = 8
        L_CHAR = 256
        L_SUB = 128

        def _linear(x, W, b):
            return jnp.einsum('blh,oh->blo', x, W) + b

        def _interp_linear(x, out_len):
            L_in = x.shape[1]
            pos = (jnp.arange(out_len, dtype=x.dtype) + 0.5) * (L_in / out_len) - 0.5
            pos = jnp.clip(pos, 0.0, L_in - 1)
            lo = jnp.floor(pos).astype(jnp.int32)
            hi = jnp.minimum(lo + 1, L_in - 1)
            w = (pos - lo.astype(x.dtype))[None, :, None]
            return x[:, lo] * (1 - w) + x[:, hi] * w
        key = jax.random.key(seed)
        ks = jax.random.split(key, 18)
        s = 0.02
        inp = {'char_emb': jax.random.normal(ks[0], (B, L_CHAR, H), jnp.float32), 'subword_emb': jax.random.normal(ks[1], (B, L_SUB, H), jnp.float32)}
        names = ['Wq_c', 'Wk_s', 'Wv_s', 'Wq_s', 'Wk_c', 'Wv_c']
        for i, n in enumerate(names):
            inp[n] = jax.random.normal(ks[2 + 2 * i], (H, H), jnp.float32) * s
            inp['b' + n[1:]] = jax.random.normal(ks[3 + 2 * i], (H,), jnp.float32) * s
        inp['Wg'] = jax.random.normal(ks[14], (H, 2 * H), jnp.float32) * s
        inp['bg'] = jax.random.normal(ks[15], (H,), jnp.float32) * s
        return inp
    _L1_xattn_all = _L1_xattn_setup()
    _L1_xattn_in = {k: v for k, v in _L1_xattn_all.items() if k in ('Wq_c', 'bq_c', 'Wk_s', 'bk_s', 'Wv_s', 'bv_s', 'Wq_s', 'bq_s', 'Wk_c', 'bk_c', 'Wv_c', 'bv_c', 'Wg', 'bg')}
    del _L1_xattn_all

    def _L1_ffn_setup():
        import jax, jax.numpy as jnp
        import numpy as np
        LN_EPS = 1e-05

        def entmax15(z):
            z = z / 2.0
            z = z - jnp.max(z, axis=-1, keepdims=True)
            zs = -jnp.sort(-z, axis=-1)
            k = jnp.arange(1, z.shape[-1] + 1, dtype=z.dtype)
            mean = jnp.cumsum(zs, axis=-1) / k
            meansq = jnp.cumsum(zs * zs, axis=-1) / k
            ss = k * (meansq - jnp.square(mean))
            delta = (1.0 - ss) / k
            tau = mean - jnp.sqrt(jnp.clip(delta, 0.0))
            support = jnp.sum((tau <= zs).astype(jnp.int32), axis=-1, keepdims=True)
            tau_star = jnp.take_along_axis(tau, support - 1, axis=-1)
            return jnp.square(jnp.clip(z - tau_star, 0.0))

        def layernorm_noaffine(v):
            m = jnp.mean(v, axis=-1, keepdims=True)
            var = jnp.mean(jnp.square(v - m), axis=-1, keepdims=True)
            return (v - m) / jnp.sqrt(var + LN_EPS)

        def cp_mumoe(x, gate, Win, Wout):
            ones = jnp.ones(x.shape[:-1] + (1,), x.dtype)
            xb = jnp.concatenate([x, ones], axis=-1)
            z = jnp.einsum('btd,dr->btr', xb, Win) * gate
            return jnp.einsum('btr,or->bto', z, Wout)
        key = jax.random.key(seed)
        ks = jax.random.split(key, 8)
        B, T, D, O, D2, E, R = (8, 256, 128, 512, 128, 16, 64)
        s = lambda k, shape, scale: jax.random.normal(k, shape, jnp.float32) * scale
        return {'x': s(ks[0], (B, T, D), 1.0), 'proj': s(ks[1], (D, E), D ** (-0.5)), 'C1': s(ks[2], (E, R), E ** (-0.5)), 'Win1': s(ks[3], (D + 1, R), D ** (-0.5)), 'Wout1': s(ks[4], (O, R), R ** (-0.5)), 'C2': s(ks[5], (E, R), E ** (-0.5)), 'Win2': s(ks[6], (O + 1, R), O ** (-0.5)), 'Wout2': s(ks[7], (D2, R), R ** (-0.5))}
    _L1_ffn_all = _L1_ffn_setup()
    _L1_ffn_in = {k: v for k, v in _L1_ffn_all.items() if k in ('proj', 'C1', 'Win1', 'Wout1', 'C2', 'Win2', 'Wout2')}
    del _L1_ffn_all

    def _L2_xattn_setup():
        import jax, jax.numpy as jnp
        import numpy as np
        B, S, D = (4, 256, 128)
        EPS = 1e-06
        key = jax.random.key(seed)
        ks = jax.random.split(key, 9)
        scale = 1.0 / np.sqrt(D)
        return {'q': jax.random.normal(ks[0], (B, S, D), jnp.float32), 'k': jax.random.normal(ks[1], (B, S, D), jnp.float32), 'v': jax.random.normal(ks[2], (B, S, D), jnp.float32), 'Wq': jax.random.normal(ks[3], (D, D), jnp.float32) * scale, 'bq': jnp.zeros((D,), jnp.float32), 'Wk': jax.random.normal(ks[4], (D, D), jnp.float32) * scale, 'bk': jnp.zeros((D,), jnp.float32), 'Wv': jax.random.normal(ks[5], (D, D), jnp.float32) * scale, 'bv': jnp.zeros((D,), jnp.float32), 'gamma': jnp.ones((D,), jnp.float32), 'beta': jnp.zeros((D,), jnp.float32)}
    _L2_xattn_all = _L2_xattn_setup()
    _L2_xattn_in = {k: v for k, v in _L2_xattn_all.items() if k in ('Wq', 'bq', 'Wk', 'bk', 'Wv', 'bv', 'gamma', 'beta')}
    del _L2_xattn_all

    def _L2_ffn_setup():
        import jax, jax.numpy as jnp
        import numpy as np
        from jax import lax
        D = 128
        H = 176
        E = 8
        K = 2
        ROUTER_SCALE = 1.0

        def _expert(x, w1, b1, w3, b3, w2, b2):
            h = jax.nn.silu((x @ w1 + b1) * (x @ w3 + b3))
            return h @ w2 + b2
        key = jax.random.key(seed)
        ks = jax.random.split(key, 16)
        s = 0.02
        inp = {'x': jax.random.normal(ks[0], (2, 256, D), dtype=jnp.float32), 'gate_w': jax.random.normal(ks[1], (E, D), dtype=jnp.float32) * s, 'gate_b': jax.random.normal(ks[2], (E,), dtype=jnp.float32) * s, 'w1': jax.random.normal(ks[3], (E, D, H), dtype=jnp.float32) * s, 'b1': jax.random.normal(ks[4], (E, H), dtype=jnp.float32) * s, 'w3': jax.random.normal(ks[5], (E, D, H), dtype=jnp.float32) * s, 'b3': jax.random.normal(ks[6], (E, H), dtype=jnp.float32) * s, 'w2': jax.random.normal(ks[7], (E, H, D), dtype=jnp.float32) * s, 'b2': jax.random.normal(ks[8], (E, D), dtype=jnp.float32) * s, 'sw1': jax.random.normal(ks[9], (D, H), dtype=jnp.float32) * s, 'sb1': jax.random.normal(ks[10], (H,), dtype=jnp.float32) * s, 'sw3': jax.random.normal(ks[11], (D, H), dtype=jnp.float32) * s, 'sb3': jax.random.normal(ks[12], (H,), dtype=jnp.float32) * s, 'sw2': jax.random.normal(ks[13], (H, D), dtype=jnp.float32) * s, 'sb2': jax.random.normal(ks[14], (D,), dtype=jnp.float32) * s}
        return inp
    _L2_ffn_all = _L2_ffn_setup()
    _L2_ffn_in = {k: v for k, v in _L2_ffn_all.items() if k in ('gate_w', 'gate_b', 'w1', 'b1', 'w3', 'b3', 'w2', 'b2', 'sw1', 'sb1', 'sw3', 'sb3', 'sw2', 'sb2')}
    del _L2_ffn_all

    def _L3_xattn_setup():
        import jax, jax.numpy as jnp
        import numpy as np
        import math
        B, T, E, H = (2, 256, 128, 16)
        D = E // H
        key = jax.random.key(seed)
        ks = jax.random.split(key, 8)
        s = 1.0 / math.sqrt(E)
        return {'input': jax.random.normal(ks[0], (B, T, E), jnp.float32), 'encoded_features': jax.random.normal(ks[1], (B, T, E), jnp.float32), 'Wq': jax.random.normal(ks[2], (E, E), jnp.float32) * s, 'bq': jnp.zeros((E,), jnp.float32), 'Wkv': jax.random.normal(ks[3], (E, 2 * E), jnp.float32) * s, 'bkv': jnp.zeros((2 * E,), jnp.float32), 'Wo': jax.random.normal(ks[4], (E, E), jnp.float32) * s, 'bo': jnp.zeros((E,), jnp.float32)}
    _L3_xattn_all = _L3_xattn_setup()
    _L3_xattn_in = {k: v for k, v in _L3_xattn_all.items() if k in ('Wq', 'bq', 'Wkv', 'bkv', 'Wo', 'bo')}
    del _L3_xattn_all

    def _L3_ffn_setup():
        import jax, jax.numpy as jnp
        import numpy as np
        B, S, D, O, E, K = (4, 256, 128, 128, 8, 2)
        key = jax.random.key(seed)
        ks = jax.random.split(key, 5)
        scale_in = 1.0 / np.sqrt(D)
        x = jax.random.normal(ks[0], (B, S, D), dtype=jnp.float32)
        gate_w = jax.random.uniform(ks[1], (E, D), jnp.float32, -scale_in, scale_in)
        gate_b = jax.random.uniform(ks[2], (E,), jnp.float32, -scale_in, scale_in)
        expert_w = jax.random.uniform(ks[3], (E, D, O), jnp.float32, -scale_in, scale_in)
        expert_b = jax.random.uniform(ks[4], (E, O), jnp.float32, -scale_in, scale_in)
        return {'x': x, 'gate_w': gate_w, 'gate_b': gate_b, 'expert_w': expert_w, 'expert_b': expert_b}
    _L3_ffn_all = _L3_ffn_setup()
    _L3_ffn_in = {k: v for k, v in _L3_ffn_all.items() if k in ('gate_w', 'gate_b', 'expert_w', 'expert_b')}
    del _L3_ffn_all
    return {'x': x, 'ctx_1024': ctx_1024, 'mask_SxS2_ff1': mask_SxS2_ff1, 'g_xattn': g_xattn, 'g_ffn': g_ffn, 'L0_xattn_Wq': _L0_xattn_in['Wq'], 'L0_xattn_bq': _L0_xattn_in['bq'], 'L0_xattn_Wk': _L0_xattn_in['Wk'], 'L0_xattn_bk': _L0_xattn_in['bk'], 'L0_xattn_Wv': _L0_xattn_in['Wv'], 'L0_xattn_bv': _L0_xattn_in['bv'], 'L0_xattn_Wo': _L0_xattn_in['Wo'], 'L0_xattn_bo': _L0_xattn_in['bo'], 'L0_ffn_Wqkv': _L0_ffn_in['Wqkv'], 'L0_ffn_q_scale': _L0_ffn_in['q_scale'], 'L0_ffn_k_scale': _L0_ffn_in['k_scale'], 'L0_ffn_Wo': _L0_ffn_in['Wo'], 'L0_ffn_ln_g': _L0_ffn_in['ln_g'], 'L0_ffn_ln_b': _L0_ffn_in['ln_b'], 'L0_ffn_W1': _L0_ffn_in['W1'], 'L0_ffn_b1': _L0_ffn_in['b1'], 'L0_ffn_W2': _L0_ffn_in['W2'], 'L0_ffn_b2': _L0_ffn_in['b2'], 'L1_xattn_Wq_c': _L1_xattn_in['Wq_c'], 'L1_xattn_bq_c': _L1_xattn_in['bq_c'], 'L1_xattn_Wk_s': _L1_xattn_in['Wk_s'], 'L1_xattn_bk_s': _L1_xattn_in['bk_s'], 'L1_xattn_Wv_s': _L1_xattn_in['Wv_s'], 'L1_xattn_bv_s': _L1_xattn_in['bv_s'], 'L1_xattn_Wq_s': _L1_xattn_in['Wq_s'], 'L1_xattn_bq_s': _L1_xattn_in['bq_s'], 'L1_xattn_Wk_c': _L1_xattn_in['Wk_c'], 'L1_xattn_bk_c': _L1_xattn_in['bk_c'], 'L1_xattn_Wv_c': _L1_xattn_in['Wv_c'], 'L1_xattn_bv_c': _L1_xattn_in['bv_c'], 'L1_xattn_Wg': _L1_xattn_in['Wg'], 'L1_xattn_bg': _L1_xattn_in['bg'], 'L1_ffn_proj': _L1_ffn_in['proj'], 'L1_ffn_C1': _L1_ffn_in['C1'], 'L1_ffn_Win1': _L1_ffn_in['Win1'], 'L1_ffn_Wout1': _L1_ffn_in['Wout1'], 'L1_ffn_C2': _L1_ffn_in['C2'], 'L1_ffn_Win2': _L1_ffn_in['Win2'], 'L1_ffn_Wout2': _L1_ffn_in['Wout2'], 'L2_xattn_Wq': _L2_xattn_in['Wq'], 'L2_xattn_bq': _L2_xattn_in['bq'], 'L2_xattn_Wk': _L2_xattn_in['Wk'], 'L2_xattn_bk': _L2_xattn_in['bk'], 'L2_xattn_Wv': _L2_xattn_in['Wv'], 'L2_xattn_bv': _L2_xattn_in['bv'], 'L2_xattn_gamma': _L2_xattn_in['gamma'], 'L2_xattn_beta': _L2_xattn_in['beta'], 'L2_ffn_gate_w': _L2_ffn_in['gate_w'], 'L2_ffn_gate_b': _L2_ffn_in['gate_b'], 'L2_ffn_w1': _L2_ffn_in['w1'], 'L2_ffn_b1': _L2_ffn_in['b1'], 'L2_ffn_w3': _L2_ffn_in['w3'], 'L2_ffn_b3': _L2_ffn_in['b3'], 'L2_ffn_w2': _L2_ffn_in['w2'], 'L2_ffn_b2': _L2_ffn_in['b2'], 'L2_ffn_sw1': _L2_ffn_in['sw1'], 'L2_ffn_sb1': _L2_ffn_in['sb1'], 'L2_ffn_sw3': _L2_ffn_in['sw3'], 'L2_ffn_sb3': _L2_ffn_in['sb3'], 'L2_ffn_sw2': _L2_ffn_in['sw2'], 'L2_ffn_sb2': _L2_ffn_in['sb2'], 'L3_xattn_Wq': _L3_xattn_in['Wq'], 'L3_xattn_bq': _L3_xattn_in['bq'], 'L3_xattn_Wkv': _L3_xattn_in['Wkv'], 'L3_xattn_bkv': _L3_xattn_in['bkv'], 'L3_xattn_Wo': _L3_xattn_in['Wo'], 'L3_xattn_bo': _L3_xattn_in['bo'], 'L3_ffn_gate_w': _L3_ffn_in['gate_w'], 'L3_ffn_gate_b': _L3_ffn_in['gate_b'], 'L3_ffn_expert_w': _L3_ffn_in['expert_w'], 'L3_ffn_expert_b': _L3_ffn_in['expert_b']}

def reference(x, ctx_1024, mask_SxS2_ff1, g_xattn, g_ffn, L0_xattn_Wq, L0_xattn_bq, L0_xattn_Wk, L0_xattn_bk, L0_xattn_Wv, L0_xattn_bv, L0_xattn_Wo, L0_xattn_bo, L0_ffn_Wqkv, L0_ffn_q_scale, L0_ffn_k_scale, L0_ffn_Wo, L0_ffn_ln_g, L0_ffn_ln_b, L0_ffn_W1, L0_ffn_b1, L0_ffn_W2, L0_ffn_b2, L1_xattn_Wq_c, L1_xattn_bq_c, L1_xattn_Wk_s, L1_xattn_bk_s, L1_xattn_Wv_s, L1_xattn_bv_s, L1_xattn_Wq_s, L1_xattn_bq_s, L1_xattn_Wk_c, L1_xattn_bk_c, L1_xattn_Wv_c, L1_xattn_bv_c, L1_xattn_Wg, L1_xattn_bg, L1_ffn_proj, L1_ffn_C1, L1_ffn_Win1, L1_ffn_Wout1, L1_ffn_C2, L1_ffn_Win2, L1_ffn_Wout2, L2_xattn_Wq, L2_xattn_bq, L2_xattn_Wk, L2_xattn_bk, L2_xattn_Wv, L2_xattn_bv, L2_xattn_gamma, L2_xattn_beta, L2_ffn_gate_w, L2_ffn_gate_b, L2_ffn_w1, L2_ffn_b1, L2_ffn_w3, L2_ffn_b3, L2_ffn_w2, L2_ffn_b2, L2_ffn_sw1, L2_ffn_sb1, L2_ffn_sw3, L2_ffn_sb3, L2_ffn_sw2, L2_ffn_sb2, L3_xattn_Wq, L3_xattn_bq, L3_xattn_Wkv, L3_xattn_bkv, L3_xattn_Wo, L3_xattn_bo, L3_ffn_gate_w, L3_ffn_gate_b, L3_ffn_expert_w, L3_ffn_expert_b):
    import jax
    import jax.numpy as jnp

    def _L0_xattn_ref(query, key, value, mask, Wq, bq, Wk, bk, Wv, bv, Wo, bo):
        import jax, jax.numpy as jnp
        import numpy as np
        B, N, M, D_MODEL, H, DH, D_OUT = (2, 256, 256, 128, 16, 64, 128)
        q = jnp.einsum('bnd,hde->bhne', query, Wq) + bq[None, :, None, :]
        k = jnp.einsum('bmd,hde->bhme', key, Wk) + bk[None, :, None, :]
        v = jnp.einsum('bmd,hde->bhme', value, Wv) + bv[None, :, None, :]
        q = q / jnp.sqrt(jnp.asarray(q.shape[-1], q.dtype))
        logits = jnp.einsum('bhne,bhme->bhnm', q, k)
        logits = logits + -10000000000.0 * (1.0 - mask)
        attn = jax.nn.softmax(logits, axis=-1)
        ctx = jnp.einsum('bhnm,bhme->bhne', attn, v)
        ctx = jnp.transpose(ctx, (0, 2, 3, 1)).reshape(ctx.shape[0], ctx.shape[2], -1)
        return jnp.dot(ctx, Wo) + bo

    def _L0_ffn_ref(x, Wqkv, q_scale, k_scale, Wo, ln_g, ln_b, W1, b1, W2, b2):
        import jax, jax.numpy as jnp
        import numpy as np
        DIM = 128
        DEPTH = 6
        HEADS = 16
        DIM_HEAD = 64
        WINDOW = 32
        INNER = HEADS * DIM_HEAD
        DIM_INNER = int(DIM * 4 * 2 / 3)
        QK_SCALE = 8.0

        def shift_tokens(t):
            a, s = jnp.split(t, 2, -1)
            s = jnp.pad(s, ((0, 0), (1, 0), (0, 0)))[:, :-1]
            return jnp.concatenate([a, s], -1)

        def l2norm(t):
            return t / jnp.maximum(jnp.linalg.norm(t, axis=-1, keepdims=True), 1e-12)

        def rotate_half(x):
            x1, x2 = jnp.split(x, 2, -1)
            return jnp.concatenate([-x2, x1], -1)

        def rotary_tables(n):
            half = jnp.arange(0, DIM_HEAD, 2, dtype=jnp.float32)
            inv_freq = 1.0 / 10000.0 ** (half / DIM_HEAD)
            t = jnp.arange(n, dtype=jnp.float32)
            freqs = t[:, None] * inv_freq[None, :]
            freqs = jnp.concatenate([freqs, freqs], -1)
            base_scale = (half + 0.4 * DIM_HEAD) / (1.4 * DIM_HEAD)
            power = (t - n // 2) / (WINDOW // 2)
            scale = base_scale[None, :] ** power[:, None]
            scale = jnp.concatenate([scale, scale], -1)
            return (freqs, scale)

        def local_attention(q, k, v):
            b, h, n, d = q.shape
            w = WINDOW
            nw = n // w
            bq = q.reshape(b, h, nw, w, d)
            bk = k.reshape(b, h, nw, w, d)
            bv = v.reshape(b, h, nw, w, d)

            def look(t):
                p = jnp.pad(t, ((0, 0), (0, 0), (1, 0), (0, 0), (0, 0)))
                return jnp.concatenate([p[:, :, :nw], p[:, :, 1:]], axis=3)
            bk2, bv2 = (look(bk), look(bv))
            seq = jnp.arange(n).reshape(nw, w)
            seq_p = jnp.pad(seq, ((1, 0), (0, 0)), constant_values=-1)
            jt = jnp.concatenate([seq_p[:nw], seq_p[1:]], axis=1)
            it = seq[:, :, None]
            jb = jt[:, None, :]
            mask = (it < jb) | (it > jb + w) | (jb == -1)
            sim = jnp.einsum('bhwie,bhwje->bhwij', bq, bk2) * QK_SCALE
            sim = jnp.where(mask, -jnp.finfo(sim.dtype).max, sim)
            attn = jax.nn.softmax(sim, -1)
            out = jnp.einsum('bhwij,bhwje->bhwie', attn, bv2)
            return out.reshape(b, h, n, d)

        def attn_layer(x, Wqkv, qs, ksc, Wo):
            b, n, _ = x.shape
            qkv = x @ Wqkv
            q, k, v = jnp.split(qkv, 3, -1)
            sh = lambda t: t.reshape(b, n, HEADS, DIM_HEAD).transpose(0, 2, 1, 3)
            q, k, v = (sh(q), sh(k), sh(v))
            q = l2norm(q) * qs
            k = l2norm(k) * ksc
            freqs, scale = rotary_tables(n)
            cos, sin = (jnp.cos(freqs), jnp.sin(freqs))
            q = q * cos * scale + rotate_half(q) * sin * scale
            inv = 1.0 / scale
            k = k * cos * inv + rotate_half(k) * sin * inv
            out = local_attention(q, k, v)
            out = out.transpose(0, 2, 1, 3).reshape(b, n, INNER)
            return out @ Wo

        def ffn_layer(x, g, bln, W1, b1, W2, b2):
            mu = x.mean(-1, keepdims=True)
            var = ((x - mu) ** 2).mean(-1, keepdims=True)
            xn = (x - mu) / jnp.sqrt(var + 1e-05) * g + bln
            hg = xn @ W1 + b1
            a, gate = jnp.split(hg, 2, -1)
            return a * jax.nn.gelu(gate, approximate=False) @ W2 + b2
        for i in range(DEPTH):
            x = attn_layer(shift_tokens(x), Wqkv[i], q_scale[i], k_scale[i], Wo[i]) + x
            x = ffn_layer(shift_tokens(x), ln_g[i], ln_b[i], W1[i], b1[i], W2[i], b2[i]) + x
        return x

    def _L1_xattn_ref(char_emb, subword_emb, Wq_c, bq_c, Wk_s, bk_s, Wv_s, bv_s, Wq_s, bq_s, Wk_c, bk_c, Wv_c, bv_c, Wg, bg):
        import jax, jax.numpy as jnp
        import numpy as np
        H = 128
        B = 8
        L_CHAR = 256
        L_SUB = 128

        def _linear(x, W, b):
            return jnp.einsum('blh,oh->blo', x, W) + b

        def _interp_linear(x, out_len):
            L_in = x.shape[1]
            pos = (jnp.arange(out_len, dtype=x.dtype) + 0.5) * (L_in / out_len) - 0.5
            pos = jnp.clip(pos, 0.0, L_in - 1)
            lo = jnp.floor(pos).astype(jnp.int32)
            hi = jnp.minimum(lo + 1, L_in - 1)
            w = (pos - lo.astype(x.dtype))[None, :, None]
            return x[:, lo] * (1 - w) + x[:, hi] * w
        h = char_emb.shape[-1]
        scale = 1.0 / jnp.sqrt(jnp.asarray(h, char_emb.dtype))
        Q_char = _linear(char_emb, Wq_c, bq_c)
        K_sub = _linear(subword_emb, Wk_s, bk_s)
        V_sub = _linear(subword_emb, Wv_s, bv_s)
        scores = jnp.einsum('bqh,bkh->bqk', Q_char, K_sub) * scale
        char2sub = jnp.einsum('bqk,bkh->bqh', jax.nn.softmax(scores, axis=-1), V_sub)
        Q_sub = _linear(subword_emb, Wq_s, bq_s)
        K_char = _linear(char_emb, Wk_c, bk_c)
        V_char = _linear(char_emb, Wv_c, bv_c)
        scores2 = jnp.einsum('bqh,bkh->bqk', Q_sub, K_char) * scale
        sub2char = jnp.einsum('bqk,bkh->bqh', jax.nn.softmax(scores2, axis=-1), V_char)
        L_char = char_emb.shape[1]
        if sub2char.shape[1] != L_char:
            sub2char = _interp_linear(sub2char, L_char)
        gate_in = jnp.concatenate([char2sub, sub2char], axis=-1)
        gate = jax.nn.sigmoid(jnp.einsum('blh,oh->blo', gate_in, Wg) + bg)
        return gate * char2sub + (1 - gate) * sub2char

    def _L1_ffn_ref(x, proj, C1, Win1, Wout1, C2, Win2, Wout2):
        import jax, jax.numpy as jnp
        import numpy as np
        LN_EPS = 1e-05

        def entmax15(z):
            z = z / 2.0
            z = z - jnp.max(z, axis=-1, keepdims=True)
            zs = -jnp.sort(-z, axis=-1)
            k = jnp.arange(1, z.shape[-1] + 1, dtype=z.dtype)
            mean = jnp.cumsum(zs, axis=-1) / k
            meansq = jnp.cumsum(zs * zs, axis=-1) / k
            ss = k * (meansq - jnp.square(mean))
            delta = (1.0 - ss) / k
            tau = mean - jnp.sqrt(jnp.clip(delta, 0.0))
            support = jnp.sum((tau <= zs).astype(jnp.int32), axis=-1, keepdims=True)
            tau_star = jnp.take_along_axis(tau, support - 1, axis=-1)
            return jnp.square(jnp.clip(z - tau_star, 0.0))

        def layernorm_noaffine(v):
            m = jnp.mean(v, axis=-1, keepdims=True)
            var = jnp.mean(jnp.square(v - m), axis=-1, keepdims=True)
            return (v - m) / jnp.sqrt(var + LN_EPS)

        def cp_mumoe(x, gate, Win, Wout):
            ones = jnp.ones(x.shape[:-1] + (1,), x.dtype)
            xb = jnp.concatenate([x, ones], axis=-1)
            z = jnp.einsum('btd,dr->btr', xb, Win) * gate
            return jnp.einsum('btr,or->bto', z, Wout)
        a = entmax15(layernorm_noaffine(jnp.einsum('btd,de->bte', x, proj)))
        g1 = jnp.einsum('bte,er->btr', a, C1)
        h = cp_mumoe(x, g1, Win1, Wout1)
        h = jax.nn.gelu(h, approximate=False)
        g2 = jnp.einsum('bte,er->btr', a, C2)
        return cp_mumoe(h, g2, Win2, Wout2)

    def _L2_xattn_ref(q, k, v, Wq, bq, Wk, bk, Wv, bv, gamma, beta):
        import jax, jax.numpy as jnp
        import numpy as np
        B, S, D = (4, 256, 128)
        EPS = 1e-06
        residual = v
        Q = jnp.einsum('bsd,de->bse', q, Wq) + bq
        K = jnp.einsum('bsd,de->bse', k, Wk) + bk
        V = jnp.einsum('bsd,de->bse', v, Wv) + bv
        inv_scale = 1.0 / jnp.sqrt(jnp.asarray(D, Q.dtype))
        scores = jnp.einsum('bqd,bkd->bqk', Q, K) * inv_scale
        attn = jax.nn.softmax(scores, axis=-1)
        out = jnp.einsum('bqk,bkd->bqd', attn, V) + residual
        mu = jnp.mean(out, axis=-1, keepdims=True)
        var = jnp.var(out, axis=-1, keepdims=True)
        normed = (out - mu) * jax.lax.rsqrt(var + EPS)
        return normed * gamma + beta

    def _L2_ffn_ref(x, gate_w, gate_b, w1, b1, w3, b3, w2, b2, sw1, sb1, sw3, sb3, sw2, sb2):
        import jax, jax.numpy as jnp
        import numpy as np
        from jax import lax
        D = 128
        H = 176
        E = 8
        K = 2
        ROUTER_SCALE = 1.0

        def _expert(x, w1, b1, w3, b3, w2, b2):
            h = jax.nn.silu((x @ w1 + b1) * (x @ w3 + b3))
            return h @ w2 + b2
        shape = x.shape
        xf = x.reshape(-1, D)
        T = xf.shape[0]
        scores = jax.nn.softmax(xf @ gate_w.T, axis=-1)
        biased = scores + gate_b
        _, idx = lax.top_k(biased, K)
        w = jnp.take_along_axis(scores, idx, axis=-1) * ROUTER_SCALE
        rw = jnp.zeros((T, E), dtype=xf.dtype).at[jnp.arange(T)[:, None], idx].add(w)
        h = jax.nn.silu((jnp.einsum('td,edh->teh', xf, w1) + b1) * (jnp.einsum('td,edh->teh', xf, w3) + b3))
        oe = jnp.einsum('teh,ehd->ted', h, w2) + b2
        y = jnp.einsum('te,ted->td', rw, oe)
        z = _expert(xf, sw1, sb1, sw3, sb3, sw2, sb2)
        return (y + z).reshape(shape)

    def _L3_xattn_ref(input, encoded_features, Wq, bq, Wkv, bkv, Wo, bo):
        import jax, jax.numpy as jnp
        import numpy as np
        import math
        B, T, E, H = (2, 256, 128, 16)
        D = E // H
        b, tq, _ = input.shape
        tk = encoded_features.shape[1]
        q = (input @ Wq + bq).reshape(b, tq, H, D).transpose(0, 2, 1, 3)
        kv = (encoded_features @ Wkv + bkv).reshape(b, tk, 2, H, D).transpose(2, 0, 3, 1, 4)
        k, v = (kv[0], kv[1])
        scores = jnp.einsum('bhqd,bhkd->bhqk', q, k) / math.sqrt(D)
        attn = jax.nn.softmax(scores, axis=2)
        out = jnp.einsum('bhqk,bhkd->bhqd', attn, v)
        out = out.transpose(0, 2, 1, 3).reshape(b, tq, H * D)
        return out @ Wo + bo

    def _L3_ffn_ref(x, gate_w, gate_b, expert_w, expert_b):
        import jax, jax.numpy as jnp
        import numpy as np
        B, S, D, O, E, K = (4, 256, 128, 128, 8, 2)
        logits = jnp.einsum('bsd,ed->bse', x, gate_w) + gate_b
        if K < E:
            topv, topi = jax.lax.top_k(logits, K)
            keep = jax.nn.one_hot(topi, E, dtype=jnp.float32).sum(axis=-2)
            logits = jnp.where(keep > 0, logits, -jnp.inf)
        gate_score = jax.nn.softmax(logits, axis=-1)
        expert_out = jnp.einsum('bsd,edo->bseo', x, expert_w) + expert_b
        out = jnp.einsum('bseo,bse->bso', expert_out, gate_score)
        return out
    x = x + jnp.tanh(g_xattn[0]) * _L0_xattn_ref(_layernorm(x, axis=-1), ctx_1024, ctx_1024, mask_SxS2_ff1, L0_xattn_Wq, L0_xattn_bq, L0_xattn_Wk, L0_xattn_bk, L0_xattn_Wv, L0_xattn_bv, L0_xattn_Wo, L0_xattn_bo)
    x = x + jnp.tanh(g_ffn[0]) * _L0_ffn_ref(_layernorm(x, axis=-1), L0_ffn_Wqkv, L0_ffn_q_scale, L0_ffn_k_scale, L0_ffn_Wo, L0_ffn_ln_g, L0_ffn_ln_b, L0_ffn_W1, L0_ffn_b1, L0_ffn_W2, L0_ffn_b2)
    x = x + jnp.tanh(g_xattn[1]) * _L1_xattn_ref(_layernorm(x, axis=-1), ctx_1024, L1_xattn_Wq_c, L1_xattn_bq_c, L1_xattn_Wk_s, L1_xattn_bk_s, L1_xattn_Wv_s, L1_xattn_bv_s, L1_xattn_Wq_s, L1_xattn_bq_s, L1_xattn_Wk_c, L1_xattn_bk_c, L1_xattn_Wv_c, L1_xattn_bv_c, L1_xattn_Wg, L1_xattn_bg)
    x = x + jnp.tanh(g_ffn[1]) * _L1_ffn_ref(_layernorm(x, axis=-1), L1_ffn_proj, L1_ffn_C1, L1_ffn_Win1, L1_ffn_Wout1, L1_ffn_C2, L1_ffn_Win2, L1_ffn_Wout2)
    x = x + jnp.tanh(g_xattn[2]) * _L2_xattn_ref(_layernorm(x, axis=-1), ctx_1024, ctx_1024, L2_xattn_Wq, L2_xattn_bq, L2_xattn_Wk, L2_xattn_bk, L2_xattn_Wv, L2_xattn_bv, L2_xattn_gamma, L2_xattn_beta)
    x = x + jnp.tanh(g_ffn[2]) * _L2_ffn_ref(_layernorm(x, axis=-1), L2_ffn_gate_w, L2_ffn_gate_b, L2_ffn_w1, L2_ffn_b1, L2_ffn_w3, L2_ffn_b3, L2_ffn_w2, L2_ffn_b2, L2_ffn_sw1, L2_ffn_sb1, L2_ffn_sw3, L2_ffn_sb3, L2_ffn_sw2, L2_ffn_sb2)
    x = x + jnp.tanh(g_xattn[3]) * _L3_xattn_ref(_layernorm(x, axis=-1), ctx_1024, L3_xattn_Wq, L3_xattn_bq, L3_xattn_Wkv, L3_xattn_bkv, L3_xattn_Wo, L3_xattn_bo)
    x = x + jnp.tanh(g_ffn[3]) * _L3_ffn_ref(_layernorm(x, axis=-1), L3_ffn_gate_w, L3_ffn_gate_b, L3_ffn_expert_w, L3_ffn_expert_b)
    return x

_drawn_inputs = setup_inputs


def setup_inputs(seed=0):
    import zlib

    import numpy as np

    out = dict(_drawn_inputs(seed))
    spreads = {'mask_SxS2_ff1': (1.0, 0.2),
     'L0_xattn_bq': (0.0, 0.1),
     'L0_xattn_bk': (0.0, 0.1),
     'L0_xattn_bv': (0.0, 0.1),
     'L0_xattn_bo': (0.0, 0.1),
     'L0_ffn_q_scale': (1.0, 0.2),
     'L0_ffn_k_scale': (1.0, 0.539),
     'L0_ffn_ln_g': (1.0, 0.552),
     'L0_ffn_ln_b': (0.0, 0.348),
     'L0_ffn_b1': (0.0, 0.1),
     'L0_ffn_b2': (0.0, 0.1),
     'L2_xattn_bq': (0.0, 0.1),
     'L2_xattn_bk': (0.0, 2.0),
     'L2_xattn_bv': (0.0, 0.1),
     'L2_xattn_gamma': (1.0, 0.2),
     'L2_xattn_beta': (0.0, 0.1),
     'L3_xattn_bq': (0.0, 2.0),
     'L3_xattn_bkv': (0.0, 0.1),
     'L3_xattn_bo': (0.0, 0.1)}
    factors = {'g_ffn': 28.992,
     'L1_xattn_Wq_c': 3.849,
     'L1_xattn_bq_c': 8.0,
     'L1_xattn_Wk_s': 6.045,
     'L1_xattn_bk_s': 64.0,
     'L1_xattn_Wq_s': 8.0,
     'L1_xattn_bq_s': 8.0,
     'L1_xattn_Wk_c': 6.413,
     'L1_xattn_bk_c': 64.0,
     'L1_xattn_Wg': 4.244,
     'L1_xattn_bg': 6.109,
     'L2_ffn_gate_w': 4.892,
     'L2_ffn_gate_b': 5.154,
     'L2_ffn_w1': 5.172,
     'L2_ffn_b1': 8.0,
     'L2_ffn_w3': 5.858,
     'L2_ffn_b3': 8.0,
     'L2_ffn_w2': 4.665,
     'L2_ffn_b2': 3.927,
     'L2_ffn_sw1': 3.051,
     'L2_ffn_sb1': 8.0,
     'L2_ffn_sw3': 2.993,
     'L2_ffn_sb3': 7.674}
    for name, (base, spread) in spreads.items():
        noise = np.random.default_rng([zlib.crc32(name.encode()), seed]).standard_normal(out[name].shape)
        drawn = base * np.exp(spread * noise) if base else spread * noise
        out[name] = jnp.asarray(drawn.astype(out[name].dtype))
    for name, factor in factors.items():
        out[name] = (out[name] * factor).astype(out[name].dtype)
    return out
```

```python
from contextlib import ExitStack

import numpy as np

import concourse.bass as bass
from concourse import mybir

F32 = mybir.dt.float32
ALU = mybir.AluOpType
ACT = mybir.ActivationFunctionType
AX = mybir.AxisListType

B, N, D = 4, 256, 128
P = 128
NT = N // P
BANK = 512
H0, DH = 16, 64
PAIRS = H0 * DH // P
INNER = H0 * DH
DEPTH, WINDOW = 6, 32
FF = D * 4 * 2 // 3
FFC = [(i, min(P, FF - i)) for i in range(0, FF, P)]
E1, R1, O1 = 16, 64, 512
E2, HID2, K2 = 8, 176, 2
HH2 = HID2 // 2
H3, DH3 = 16, 8
E3 = 8
QK_SCALE = 8.0
MASKED = -1e30
LOWEST = -3.0e38
EPS, EPS_L2 = 1e-5, 1e-6


class Columns:

    def __init__(self, pieces):
        self.at, self.n = {}, 0
        for name, width in pieces:
            self.at[name] = (self.n, width)
            self.n += width

    def __call__(self, tile, name):
        start, width = self.at[name]
        return tile[:, start:start + width]


CONST = Columns([("ident", P), ("mean", P), ("ones", P), ("qcos", NT * DH), ("qsin", NT * DH),
                 ("kcos", NT * DH), ("ksin", NT * DH),
                 ("band", NT * P), ("tri", E2 * E2), ("k", E1), ("invk", E1), ("headmask", H3)])
L0X = Columns([("Wq", INNER), ("Wk", INNER), ("Wv", INNER), ("Wo", PAIRS * D), ("mask", NT * N),
               ("bq", PAIRS), ("bk", PAIRS), ("bv", PAIRS), ("bo", 1)])
L0F = Columns([("Wqkv", 3 * INNER), ("Wo", PAIRS * D), ("W1", 2 * FF), ("W2", len(FFC) * D),
               ("scales", 4 * DH), ("ln_g", 1), ("ln_b", 1), ("b1", 2 * len(FFC)), ("b2", 1)])
MIX1 = Columns([(n, D) for n in ("Wq_c", "Wk_s", "Wv_s", "Wq_s", "Wk_c", "Wv_c", "Wg_a", "Wg_b")]
               + [(n, 1) for n in ("bq_c", "bk_s", "bv_s", "bq_s", "bk_c", "bv_c", "bg")]
               + [("proj", E1), ("C1", R1), ("Win1", R1), ("Wout1", O1), ("C2", R1),
                  ("Win2", O1 // P * R1), ("Wout2", D), ("bin1", 1), ("bin2", 1)]
               + [("Wq", D), ("Wk", D), ("Wv", D), ("bq", 1), ("bk", 1), ("bv", 1),
                  ("gamma", 1), ("beta", 1)])
L2F = Columns([("w1", (E2 + 1) * HID2), ("w3", (E2 + 1) * HID2), ("w2", (E2 + 1) * 2 * D),
               ("b1", (E2 + 1) * 2), ("b3", (E2 + 1) * 2), ("b2", D), ("gate_w", E2),
               ("gate_b", E2), ("sb2", 1)])
L3 = Columns([("Wq", D), ("Wk", D), ("Wv", D), ("Wo", D), ("bq", 1), ("bk", 1), ("bv", D),
              ("bo", 1), ("gate_w", E3), ("gate_b", E3), ("expert_w", E3 * D), ("expert_b", D)])
STAGES = [L0X] + [L0F] * DEPTH + [MIX1, L2F, L3]
SLOT = max(s.n for s in STAGES)


class Queue:

    def __init__(self, sem):
        self.sem, self.count, self.ops, self.passed = sem, 0, [], {}

    def wait(self, *marks):
        for sem, value in marks:
            if self.passed.get(sem.name, 0) < value:
                self.passed[sem.name] = value
                self.ops.append((sem, value))

    def put(self, op):
        self.ops.append(op)

    def mark(self):
        op, sem = self.ops.pop(), self.sem
        self.ops.append(lambda e: op(e).then_inc(sem, 1))
        self.count += 1
        return (sem, self.count)

    def settle(self):
        self.wait((self.sem, self.count))

    def play(self, engine):
        for op in self.ops:
            if isinstance(op, tuple):
                engine.wait_ge(*op)
            else:
                op(engine)


class Tensor(Queue):
    def mm(self, out, lhsT, rhs, start=True, stop=True):
        self.put(lambda e: e.matmul(out, lhsT, rhs, start=start, stop=stop, skip_group_check=True))

    def turn(self, out, in_, ident):
        rows = in_.shape[0]
        self.put(lambda e: e.transpose(out, in_, ident[0:rows, 0:rows]))


class Scalar(Queue):
    def act(self, out, in_, func, bias=0.0, scale=1.0, total=None):
        if total is None:
            self.put(lambda e: e.activation(out, in_, func, bias=bias, scale=scale))
        else:
            self.put(lambda e: e.activation(out, in_, func, bias=bias, scale=scale, accum_out=total))


class Elementwise(Queue):
    def tt(self, out, a, b, op):
        self.put(lambda e: e.tensor_tensor(out, a, b, op))

    def ts(self, out, a, s1, s2, op0, op1=None):
        if op1 is None:
            self.put(lambda e: e.tensor_scalar(out, a, s1, None, op0))
        else:
            self.put(lambda e: e.tensor_scalar(out, a, s1, s2, op0, op1))

    def copy(self, out, a):
        self.put(lambda e: e.tensor_copy(out, a))

    def fill(self, out, value):
        self.put(lambda e: e.memset(out, value))

    def stt(self, out, a, s, b, op0, op1):
        self.put(lambda e: e.scalar_tensor_tensor(out=out, in0=a, scalar=s, in1=b, op0=op0, op1=op1))

    def reduce(self, out, a, op, negate=False):
        self.put(lambda e: e.tensor_reduce(out, a, AX.X, op, negate=negate))

    def add_max(self, out, a, b, largest):
        self.put(lambda e: e.tensor_tensor_reduce(out, a, b, 1.0, LOWEST, ALU.add, ALU.max, largest))

    def recip(self, out, a):
        self.put(lambda e: e.reciprocal(out, a))

    def top8(self, out, a):
        self.put(lambda e: e.max(out, a))

    def drop(self, out, values, a):
        self.put(lambda e: e.match_replace(out, values, a, LOWEST))

    def scan(self, out, a, b):
        self.put(lambda e: e.tensor_tensor_scan(out, a, b, 0.0, ALU.mult, ALU.add))


def split(ap, n):
    return ap.rearrange("p (n k) -> p n k", n=n)


def stretch(ap, k):
    return ap.unsqueeze(2).to_broadcast([ap.shape[0], ap.shape[1], k])


def repeat(ap, n):
    return ap.unsqueeze(1).to_broadcast([ap.shape[0], n, ap.shape[1]])


class Chip:
    pass


class Sequence:
    pass


def layernorm(c, s, src, ready, eps, out):
    centred, square, diag = s.w[:, 0:N], s.w[:, N:2 * N], s.w[:, 2 * N:3 * N]
    var, rstd = s.sm[:, 0:NT], s.sm[:, NT:2 * NT]
    b0, b1 = s.bank
    c.pe.wait(ready, s.free[0], c.const_ready)
    c.pe.mm(b0[:, 0:N], c.mean, src)
    mean_done = c.pe.mark()
    c.dve.wait(mean_done, ready)
    c.dve.tt(centred, src, b0[:, 0:N], ALU.subtract)
    centred_done = c.dve.mark()
    c.act.wait(centred_done)
    c.act.act(square, centred, ACT.Square)
    square_done = c.act.mark()
    yield
    c.pe.wait(square_done, s.free[1])
    for t in range(NT):
        c.pe.mm(b1[:, t:t + 1], square[:, t * P:(t + 1) * P], c.mean[:, 0:1])
    var_done = c.pe.mark()
    c.dve.wait(var_done)
    c.dve.ts(var, b1[:, 0:NT], eps, None, ALU.add)
    s.free[1] = c.dve.mark()
    c.pool.wait(s.free[1], c.powers_ready)
    c.pool.tt(rstd, var, c.minus_half[:, 0:NT], ALU.pow)
    rstd_done = c.pool.mark()
    c.dve.wait(rstd_done)
    for t in range(NT):
        c.dve.ts(diag[:, t * P:(t + 1) * P], c.ident, rstd[:, t:t + 1], None, ALU.mult)
    diag_done = c.dve.mark()
    yield
    c.pe.wait(diag_done)
    for t in range(NT):
        c.pe.mm(b0[:, t * P:(t + 1) * P], c.ones, diag[:, t * P:(t + 1) * P])
    spread = c.pe.mark()
    c.dve.wait(spread)
    c.dve.tt(out, centred, b0[:, 0:N], ALU.mult)
    s.free[0] = c.dve.mark()
    yield
    return s.free[0]


def cross_attention_0(c, s):
    b0, b1 = s.bank
    normed = yield from layernorm(c, s, s.x[:, :], s.ready, EPS, s.xn[:, :])
    s.normed = normed
    W = s.W
    qz = s.qz[:, :].rearrange("p (r z n) -> p r z n", r=4, z=2)
    kT = s.kT[:, 0:N]
    v = s.kT[:, N:2 * N].rearrange("p (t d) -> p t d", t=NT)
    mask = split(W("mask"), NT)
    bq8 = s.sm[:, 8:8 + PAIRS]
    c.dve.wait(s.weights)
    c.dve.ts(bq8, W("bq"), 0.125, None, ALU.mult)
    bq8_done = c.dve.mark()
    for pair in range(PAIRS):
        cols = slice(pair * P, (pair + 1) * P)
        c.pe.wait(normed, s.weights, s.x_ready, *s.free)
        c.pe.mm(b0[:, 0:N], W("Wq")[:, cols], s.xn[:, :])
        c.pe.mm(b0[:, N:2 * N], W("Wk")[:, cols], s.ctx[:, :])
        qk_done = c.pe.mark()
        for t in range(NT):
            c.pe.mm(b1[:, t * P:(t + 1) * P], s.ctx[:, t * P:(t + 1) * P], W("Wv")[:, cols])
        v_done = c.pe.mark()
        c.act.wait(qk_done, s.weights, bq8_done, s.qz_zero)
        for z in range(2):
            rows = slice(z * DH, (z + 1) * DH)
            c.act.act(qz[rows, 0:NT, z, :], split(b0[rows, 0:N], NT), ACT.Identity, bias=bq8[rows, pair:pair + 1], scale=0.125)
        c.act.act(kT, b0[:, N:2 * N], ACT.Identity, bias=W("bk")[:, pair:pair + 1])
        qk_kept = c.act.mark()
        c.dve.wait(v_done)
        c.dve.copy(v, b1[:, 0:N].rearrange("p (t d) -> p t d", t=NT))
        v_kept = c.dve.mark()
        yield
        most, least, total, over = (s.sm[:, 16 + 4 * i:20 + 4 * i] for i in range(4))
        c.pe.wait(qk_kept, v_kept)
        scored = []
        for z in range(2):
            for t in range(NT):
                c.pe.mm(s.bank[z][:, t * N:(t + 1) * N], qz[:, t, z, :], kT)
            scored.append(c.pe.mark())
        e = [s.w[:, z * BANK:(z + 1) * BANK] for z in range(2)]
        pT = [s.w[:, (2 + z) * BANK:(3 + z) * BANK] for z in range(2)]
        normalised = []
        for z in range(2):
            c.dve.wait(scored[z], c.mask_ready)
            for t in range(NT):
                i = 2 * z + t
                c.dve.add_max(e[z][:, t * N:(t + 1) * N], s.bank[z][:, t * N:(t + 1) * N], mask[:, t, :],
                              most[:, i:i + 1])
            c.dve.wait(c.dve.mark())
            c.dve.ts(least[:, 2 * z:2 * z + 2], most[:, 2 * z:2 * z + 2], -1.0, None, ALU.mult)
            shift_done = c.dve.mark()
            c.act.wait(shift_done)
            for t in range(NT):
                i = 2 * z + t
                c.act.act(e[z][:, t * N:(t + 1) * N], e[z][:, t * N:(t + 1) * N], ACT.Exp,
                          bias=least[:, i:i + 1], total=total[:, i:i + 1])
            exp_done = c.act.mark()
            c.dve.wait(exp_done)
            c.dve.recip(over[:, 2 * z:2 * z + 2], total[:, 2 * z:2 * z + 2])
            over_done = c.dve.mark()
            c.pool.wait(over_done)
            c.pool.tt(split(e[z], NT), split(e[z], NT), stretch(over[:, 2 * z:2 * z + 2], N), ALU.mult)
            normalised.append(c.pool.mark())
        yield
        kept = []
        for z in range(2):
            c.pe.wait(normalised[z])
            for m in range(NT):
                for t in range(NT):
                    c.pe.turn(s.bank[z][:, m * N + t * P:m * N + (t + 1) * P],
                              e[z][:, t * N + m * P:t * N + (m + 1) * P], c.ident)
            turned = c.pe.mark()
            q = c.dve if z else c.act
            q.wait(turned)
            if z:
                c.dve.copy(pT[z], s.bank[z][:, :])
            else:
                c.act.act(pT[z], s.bank[z][:, :], ACT.Copy)
            kept.append(q.mark())
        yield
        c.pe.wait(*kept)
        for m in range(NT):
            for z in range(2):
                c.pe.mm(b0[z * DH:(z + 1) * DH, 0:N], v[:, m, z * DH:(z + 1) * DH],
                        pT[z][:, m * N:(m + 1) * N], start=(m == 0), stop=(m == NT - 1))
        o_done = c.pe.mark()
        oT = (s.v if pair < 4 else s.oT)[:, (pair % 4) * N:(pair % 4 + 1) * N]
        c.act.wait(o_done)
        c.act.act(oT, b0[:, 0:N], ACT.Identity, bias=W("bv")[:, pair:pair + 1])
        s.free = [c.act.mark(), kept[1]]
        yield
    c.pe.wait(*s.free)
    for pair in range(PAIRS):
        oT = (s.v if pair < 4 else s.oT)[:, (pair % 4) * N:(pair % 4 + 1) * N]
        c.pe.mm(b0[:, 0:N], W("Wo")[:, pair * D:(pair + 1) * D], oT, start=(pair == 0), stop=(pair == PAIRS - 1))
    y_done = c.pe.mark()
    yield from update_stream(c, s, b0[:, 0:N], y_done, W("bo"), 0)


def update_stream(c, s, y, y_done, bias, gate, bank=0):
    tmp = s.w[:, 0:N]
    c.dve.wait(y_done, c.gates_ready, s.weights)
    c.dve.ts(tmp, y, bias, c.gates[:, gate:gate + 1], ALU.add, ALU.mult)
    s.free[bank] = c.dve.mark()
    c.dve.wait(s.free[bank])
    c.dve.tt(s.x[:, :], s.x[:, :], tmp, ALU.add)
    s.ready = c.dve.mark()
    yield


def shifted(c, s, ready):
    c.dve.wait(ready)
    c.dve.copy(s.zs[0:DH, :], s.z[0:DH, :])
    c.dve.copy(s.zs[DH:P, 1:N], s.z[DH:P, 0:N - 1])
    return c.dve.mark()


def local_layer(c, s, stage):
    b0, b1 = s.bank
    W = s.W
    if stage == 1:
        z_ready = yield from layernorm(c, s, s.x[:, :], s.ready, EPS, s.z[:, :])
        c.dve.fill(s.zs[DH:P, 0:1], 0.0)
    else:
        z_ready = s.z_ready
    zs_ready = shifted(c, s, z_ready)
    tab = c.tables[stage % 2][:, :].rearrange("p (a t d) -> p a t d", a=4, t=NT)
    qz = s.qz[:, :].rearrange("p (r z n) -> p r z n", r=4, z=2)
    kT = split(s.kT[:, :], 4)
    v = split(s.v[:, :], NT)
    oT = split(s.oT[:, :], 4)
    before = split(s.before[:, :], 8)
    w = [s.w[:, i * BANK:(i + 1) * BANK] for i in range(6)]
    sq_sum, norm, most, least, total, over = (s.sm[:, 64 + 16 * i:80 + 16 * i] for i in range(6))
    heads = 8
    for g in range(H0 // heads):
        for t in range(NT):
            tile = slice(t * P, (t + 1) * P)
            made = []
            for i in range(2):
                c.pe.wait(zs_ready, s.weights, s.free[i])
                c.pe.mm(s.bank[i][:, :], s.zs[:, tile], W("Wqkv")[:, i * INNER + g * BANK:i * INNER + (g + 1) * BANK])
                made.append(c.pe.mark())
            for i in range(2):
                c.act.wait(made[i], *s.free)
                c.act.act(w[i], s.bank[i][:, :], ACT.Square)
                squared = c.act.mark()
                c.dve.wait(squared)
                c.dve.reduce(sq_sum[:, i * heads:(i + 1) * heads], split(w[i], heads), ALU.add)
            summed = c.dve.mark()
            c.pool.wait(summed, c.powers_ready)
            c.pool.ts(norm, sq_sum, 1e-24, None, ALU.max)
            c.pool.wait(c.pool.mark())
            c.pool.tt(norm, norm, c.minus_half[:, 0:2 * heads], ALU.pow)
            norm_done = c.pool.mark()
            yield
            rotated = []
            for i in range(2):
                c.dve.wait(norm_done)
                c.dve.tt(split(w[i], heads), split(s.bank[i][:, :], heads), stretch(norm[:, i * heads:(i + 1) * heads], DH),
                         ALU.mult)
                s.free[i] = c.dve.mark()
                c.pool.wait(s.free[i], s.table_ready)
                here, turned, half = split(w[i], heads), split(w[2 + i], heads), DH // 2
                c.pool.tt(turned[:, :, 0:half], here[:, :, half:DH], repeat(tab[:, 2 * i + 1, t, 0:half], heads), ALU.mult)
                c.pool.tt(turned[:, :, half:DH], here[:, :, 0:half], repeat(tab[:, 2 * i + 1, t, half:DH], heads), ALU.mult)
                sine_done = c.pool.mark()
                c.dve.wait(s.free[i], s.table_ready)
                c.dve.tt(split(w[4 + i], heads), here, repeat(tab[:, 2 * i, t, :], heads), ALU.mult)
                c.dve.wait(c.dve.mark(), sine_done)
                c.dve.tt(w[4 + i], w[4 + i], w[2 + i], ALU.add)
                rotated.append(c.dve.mark())
            c.pe.wait(s.free[0])
            c.pe.mm(b0[:, :], s.zs[:, tile], W("Wqkv")[:, 2 * INNER + g * BANK:2 * INNER + (g + 1) * BANK])
            v_done = c.pe.mark()
            c.act.wait(v_done)
            c.act.act(v[:, t, :], b0[:, :], ACT.Copy)
            v_kept = c.act.mark()
            yield
            c.pe.wait(rotated[0], s.free[1])
            for r in range(4):
                c.pe.turn(b1[:, r * P:(r + 1) * P], w[4][:, r * P:(r + 1) * P], c.ident)
            turned_q = c.pe.mark()
            c.pe.wait(rotated[1], v_kept)
            for r in range(4):
                c.pe.turn(b0[:, r * P:(r + 1) * P], w[5][:, r * P:(r + 1) * P], c.ident)
            turned_k = c.pe.mark()
            c.act.wait(turned_q, s.qz_zero)
            c.act.act(qz[0:DH, :, 0, :], split(b1[0:DH, :], 4), ACT.Copy)
            q_kept_0 = c.act.mark()
            c.dve.wait(turned_q, s.qz_zero)
            c.dve.copy(qz[DH:P, :, 1, :], split(b1[DH:P, :], 4))
            q_kept_1 = c.dve.mark()
            c.act.wait(turned_k)
            c.act.act(kT[:, :, tile], split(b0[:, :], 4), ACT.Copy)
            k_kept = c.act.mark()
            yield
            scored = []
            c.pe.wait(q_kept_0, q_kept_1, k_kept)
            for j in range(2):
                for hh in range(4):
                    r, z = divmod(4 * j + hh, 2)
                    c.pe.mm(s.bank[j][:, hh * P:(hh + 1) * P], qz[:, r, z, :], kT[:, r, tile])
                    if t:
                        c.pe.mm(s.bank[j][0:WINDOW, (hh + 1) * P - WINDOW:(hh + 1) * P], qz[:, r, z, 0:WINDOW],
                                kT[:, r, P - WINDOW:P])
                scored.append(c.pe.mark())
            normalised = []
            for j in range(2):
                c.dve.wait(scored[j])
                for hh in range(4):
                    c.dve.add_max(w[j][:, hh * P:(hh + 1) * P], s.bank[j][:, hh * P:(hh + 1) * P],
                                  c.band[:, tile], most[:, 4 * j + hh:4 * j + hh + 1])
                s.free[j] = c.dve.mark()
                c.dve.wait(s.free[j])
                quad = slice(4 * j, 4 * j + 4)
                c.dve.ts(least[:, quad], most[:, quad], -1.0, None, ALU.mult)
                shift_done = c.dve.mark()
                c.act.wait(shift_done)
                for hh in range(4):
                    i = 4 * j + hh
                    c.act.act(w[j][:, hh * P:(hh + 1) * P], w[j][:, hh * P:(hh + 1) * P], ACT.Exp,
                              bias=least[:, i:i + 1], total=total[:, i:i + 1])
                exp_done = c.act.mark()
                c.dve.wait(exp_done)
                c.dve.recip(over[:, quad], total[:, quad])
                over_done = c.dve.mark()
                c.pool.wait(over_done)
                c.pool.tt(split(w[j], 4), split(w[j], 4), stretch(over[:, quad], P), ALU.mult)
                normalised.append(c.pool.mark())
            yield
            kept = []
            for j in range(2):
                c.pe.wait(normalised[j], s.free[j])
                for hh in range(4):
                    c.pe.turn(s.bank[j][:, hh * P:(hh + 1) * P], w[j][:, hh * P:(hh + 1) * P], c.ident)
                turned = c.pe.mark()
                q = c.dve if j else c.act
                q.wait(turned)
                if j:
                    c.dve.copy(w[2 + j], s.bank[j][:, :])
                else:
                    c.act.act(w[2 + j], s.bank[j][:, :], ACT.Copy)
                copied = q.mark()
                if t:
                    last, quad = slice(P - WINDOW, P), slice(4 * j, 4 * j + 4)
                    early = split(w[2 + j], 4)[last, :, 0:WINDOW]
                    c.dve.wait(copied, s.qz_zero)
                    c.dve.copy(before[last, quad, :], split(s.bank[j][:, :], 4)[last, :, 0:WINDOW])
                    kept.append(c.dve.mark())
                    c.dve.fill(early, 0.0)
                    kept.append(c.dve.mark())
                else:
                    kept.append(copied)
            yield
            c.pe.wait(*kept)
            for h in range(heads):
                r, z = divmod(h, 2)
                j, hh = divmod(h, 4)
                pT = w[2 + j][:, hh * P:(hh + 1) * P]
                rows, vh = slice(z * DH, (z + 1) * DH), slice(h * DH, (h + 1) * DH)
                c.pe.mm(b0[rows, r * P:(r + 1) * P], v[:, t, vh], pT, start=True, stop=(t == 0))
                if t:
                    c.pe.mm(b0[rows, r * P:r * P + WINDOW], v[:, 0, vh], before[:, h, :], start=False, stop=True)
            o_done = c.pe.mark()
            c.act.wait(o_done)
            c.act.act(oT[:, :, tile], split(b0[:, :], 4), ACT.Copy)
            s.free = [c.act.mark(), kept[-1]]
            yield
        c.pe.wait(*s.free)
        for r in range(4):
            c.pe.mm(b1[:, 0:N], W("Wo")[:, (4 * g + r) * D:(4 * g + r + 1) * D], oT[:, r, :], start=(r == 0), stop=(r == 3))
        y_done = c.pe.mark()
        c.dve.wait(y_done, zs_ready)
        c.dve.tt(s.z[:, :], s.z[:, :], b1[:, 0:N], ALU.add)
        s.free[1] = z_ready = c.dve.mark()
    zs_ready = shifted(c, s, z_ready)
    yield
    normed = yield from layernorm(c, s, s.zs[:, :], zs_ready, EPS, s.xn[:, :])
    c.dve.wait(normed, s.weights)
    c.dve.ts(s.xn[:, :], s.xn[:, :], W("ln_g"), W("ln_b"), ALU.mult, ALU.add)
    normed = c.dve.mark()
    yield
    hidden = []
    for i, (start, m) in enumerate(FFC):
        bank = s.bank[i % 2]
        c.pe.wait(normed, s.weights, s.free[i % 2])
        for z in range(2):
            c.pe.mm(bank[0:m, z * N:(z + 1) * N], W("W1")[:, z * FF + start:z * FF + start + m], s.xn[:, :])
        made = c.pe.mark()
        gelu, prod = w[i][0:m, 0:N], w[i][0:m, N:2 * N]
        bias = W("b1")
        c.act.wait(made, normed, s.weights)
        c.act.act(gelu, bank[0:m, N:2 * N], ACT.Gelu, bias=bias[0:m, len(FFC) + i:len(FFC) + i + 1])
        gelu_done = c.act.mark()
        c.dve.wait(gelu_done)
        c.dve.stt(prod, bank[0:m, 0:N], bias[0:m, i:i + 1], gelu, ALU.add, ALU.mult)
        s.free[i % 2] = c.dve.mark()
        hidden.append((prod, s.free[i % 2], m))
        if i == 1:
            yield
    yield
    for i, (prod, ready, m) in enumerate(hidden):
        c.pe.wait(ready, s.free[1])
        c.pe.mm(b1[:, 0:N], W("W2")[0:m, i * D:(i + 1) * D], prod, start=(i == 0), stop=(i == len(hidden) - 1))
    y_done = c.pe.mark()
    c.dve.wait(y_done)
    c.dve.stt(s.z[:, :], b1[:, 0:N], W("b2"), s.z[:, :], ALU.add, ALU.add)
    s.free[1] = s.z_ready = s.ready = c.dve.mark()
    yield
    if stage == DEPTH:
        c.dve.wait(s.z_ready, c.gates_ready)
        c.dve.stt(s.x[:, :], s.z[:, :], c.gates[:, B:B + 1], s.x[:, :], ALU.mult, ALU.add)
        s.ready = c.dve.mark()
        yield


def project(c, s, out, w, src, ready, bias, bank, half=0):
    dst = s.bank[bank][:, half * N:(half + 1) * N]
    c.pe.wait(ready, s.weights, s.free[bank])
    c.pe.mm(dst, w, src)
    made = c.pe.mark()
    c.act.wait(made, s.weights)
    c.act.act(out, dst, ACT.Identity, bias=bias)
    s.free[bank] = c.act.mark()
    return s.free[bank]


def attention(c, s, qT, kT, v, qk_ready, v_ready, scale):
    b0, b1 = s.bank
    e, pT = s.w[:, 0:BANK], s.w[:, BANK:2 * BANK]
    least, total, over = (s.sm[:, 160 + 2 * i:162 + 2 * i] for i in range(3))
    c.pe.wait(qk_ready, s.free[0])
    for t in range(NT):
        c.pe.mm(b0[:, t * N:(t + 1) * N], qT[:, t * P:(t + 1) * P], kT)
    scored = c.pe.mark()
    c.dve.wait(scored)
    c.dve.reduce(least, split(b0[:, :], NT), ALU.max, negate=True)
    c.dve.wait(c.dve.mark())
    c.dve.ts(least, least, scale, None, ALU.mult)
    shift_done = c.dve.mark()
    c.act.wait(shift_done)
    for t in range(NT):
        c.act.act(e[:, t * N:(t + 1) * N], b0[:, t * N:(t + 1) * N], ACT.Exp, bias=least[:, t:t + 1], scale=scale,
                  total=total[:, t:t + 1])
    s.free[0] = c.act.mark()
    c.dve.wait(s.free[0])
    c.dve.recip(over, total)
    over_done = c.dve.mark()
    c.pool.wait(over_done)
    c.pool.tt(split(e, NT), split(e, NT), stretch(over, N), ALU.mult)
    normalised = c.pool.mark()
    yield
    c.pe.wait(normalised, s.free[1])
    for m in range(NT):
        for t in range(NT):
            c.pe.turn(b1[:, m * N + t * P:m * N + (t + 1) * P], e[:, t * N + m * P:t * N + (m + 1) * P], c.ident)
    turned = c.pe.mark()
    c.act.wait(turned)
    c.act.act(pT, b1[:, :], ACT.Copy)
    s.free[1] = c.act.mark()
    yield
    c.pe.wait(s.free[1], v_ready, s.free[0])
    for m in range(NT):
        c.pe.mm(b0[:, 0:N], v[:, m, :], pT[:, m * N:(m + 1) * N], start=(m == 0), stop=(m == NT - 1))
    return c.pe.mark()


def values(c, s, out, src, w, ready):
    c.pe.wait(ready, s.weights, s.free[1])
    for t in range(NT):
        c.pe.mm(s.bank[1][:, t * P:(t + 1) * P], src[:, t * P:(t + 1) * P], w)
    made = c.pe.mark()
    c.dve.wait(made)
    c.dve.copy(out, split(s.bank[1][:, 0:N], NT))
    s.free[1] = c.dve.mark()
    return s.free[1]


def cross_attention_1(c, s):
    W = s.W
    normed = yield from layernorm(c, s, s.x[:, :], s.ready, EPS, s.xn[:, :])
    qT, kT = s.kT[:, 0:N], s.kT[:, N:2 * N]
    v = split(s.kT[:, 2 * N:3 * N], NT)
    found = (s.v[:, 0:N], s.v[:, N:2 * N])
    for i, (src_q, src_kv, wq, wk, wv) in enumerate((
            (s.xn[:, :], s.ctx[:, :], "q_c", "k_s", "v_s"), (s.ctx[:, :], s.xn[:, :], "q_s", "k_c", "v_c"))):
        ready = normed if i == 0 else found_ready
        q_ready = project(c, s, qT, W("W" + wq), src_q, ready, W("b" + wq), 0, 0)
        k_ready = project(c, s, kT, W("W" + wk), src_kv, ready, W("b" + wk), 0, 1)
        v_ready = values(c, s, v, src_kv, W("W" + wv), ready)
        yield
        o_done = yield from attention(c, s, qT, kT, v, k_ready, v_ready, D ** -0.5)
        c.act.wait(o_done)
        c.act.act(found[i], s.bank[0][:, 0:N], ACT.Identity, bias=W("b" + wv))
        s.free[0] = found_ready = c.act.mark()
        yield
    half_bias, gate, diff = s.sm[:, 170:171], s.w[:, 0:N], s.w[:, N:2 * N]
    c.pe.wait(found_ready, s.free[0])
    c.pe.mm(s.bank[0][:, 0:N], W("Wg_a"), found[0], start=True, stop=False)
    c.pe.mm(s.bank[0][:, 0:N], W("Wg_b"), found[1], start=False, stop=True)
    z_done = c.pe.mark()
    c.dve.wait(found_ready, s.weights)
    c.dve.ts(half_bias, W("bg"), 0.5, None, ALU.mult)
    c.dve.tt(diff, found[0], found[1], ALU.subtract)
    diff_done = c.dve.mark()
    c.act.wait(z_done, diff_done)
    c.act.act(gate, s.bank[0][:, 0:N], ACT.Tanh, bias=half_bias, scale=0.5)
    s.free[0] = c.act.mark()
    c.dve.wait(s.free[0])
    c.dve.ts(gate, gate, 0.5, 0.5, ALU.mult, ALU.add)
    c.dve.wait(c.dve.mark(), diff_done)
    c.dve.tt(diff, diff, gate, ALU.mult)
    c.dve.wait(c.dve.mark())
    c.dve.tt(diff, diff, found[1], ALU.add)
    c.dve.wait(c.dve.mark(), c.gates_ready)
    c.dve.stt(s.x[:, :], diff, c.gates[:, 1:2], s.x[:, :], ALU.mult, ALU.add)
    s.ready = c.dve.mark()
    yield


def mixture_1(c, s):
    W = s.W
    b0, b1 = s.bank
    normed = yield from layernorm(c, s, s.x[:, :], s.ready, EPS, s.xn[:, :])
    n = NT * E1
    tiles = [s.sm[:, 192 + n * i:192 + n * (i + 1)] for i in range(10)]
    z, work, ordered, square, mean, meansq, tau, a, ones, pick = tiles
    stat, factor = s.sm[:, 172:172 + NT], s.sm[:, 174:174 + NT]
    c.pe.wait(normed, s.weights, s.free[0])
    for t in range(NT):
        c.pe.mm(b0[:, t * E1:(t + 1) * E1], s.xn[:, t * P:(t + 1) * P], W("proj"))
    made = c.pe.mark()

    def then():
        c.dve.wait(c.dve.mark())

    v = c.dve
    v.wait(made)
    v.copy(z, b0[:, 0:n])
    s.free[0] = c.dve.mark()
    v.wait(s.free[0])
    v.reduce(stat, split(z, NT), ALU.add)
    then()
    v.ts(stat, stat, 1.0 / E1, None, ALU.mult)
    then()
    v.tt(split(z, NT), split(z, NT), stretch(stat, E1), ALU.subtract)
    then()
    v.tt(square, z, z, ALU.mult)
    then()
    v.reduce(stat, split(square, NT), ALU.add)
    then()
    v.ts(stat, stat, 1.0 / E1, EPS, ALU.mult, ALU.add)
    var_done = c.dve.mark()
    c.pool.wait(var_done, c.powers_ready)
    c.pool.tt(factor, stat, c.minus_half[:, 0:NT], ALU.pow)
    factor_done = c.pool.mark()
    v.wait(factor_done)
    v.tt(split(z, NT), split(z, NT), stretch(factor, E1), ALU.mult)
    then()
    v.reduce(stat, split(z, NT), ALU.max)
    then()
    v.tt(split(z, NT), split(z, NT), stretch(stat, E1), ALU.subtract)
    then()
    v.ts(z, z, 0.5, None, ALU.mult)
    v.fill(ones, 1.0)
    then()
    for t in range(NT):
        v.top8(ordered[:, t * E1:t * E1 + 8], z[:, t * E1:(t + 1) * E1])
    then()
    for t in range(NT):
        v.drop(work[:, t * E1:(t + 1) * E1], ordered[:, t * E1:t * E1 + 8], z[:, t * E1:(t + 1) * E1])
    then()
    for t in range(NT):
        v.top8(ordered[:, t * E1 + 8:(t + 1) * E1], work[:, t * E1:(t + 1) * E1])
    then()
    v.tt(square, ordered, ordered, ALU.mult)
    then()
    for t in range(NT):
        cols = slice(t * E1, (t + 1) * E1)
        v.scan(mean[:, cols], ones[:, cols], ordered[:, cols])
        v.scan(meansq[:, cols], ones[:, cols], square[:, cols])
    then()
    v.tt(split(mean, NT), split(mean, NT), repeat(c.invk, NT), ALU.mult)
    v.tt(split(meansq, NT), split(meansq, NT), repeat(c.invk, NT), ALU.mult)
    then()
    v.tt(tau, mean, mean, ALU.mult)
    then()
    v.tt(tau, meansq, tau, ALU.subtract)
    then()
    v.tt(split(tau, NT), split(tau, NT), repeat(c.k, NT), ALU.mult)
    then()
    v.ts(tau, tau, -1.0, 1.0, ALU.mult, ALU.add)
    then()
    v.tt(split(tau, NT), split(tau, NT), repeat(c.invk, NT), ALU.mult)
    then()
    v.ts(tau, tau, 0.0, None, ALU.max)
    delta_done = c.dve.mark()
    c.pool.wait(delta_done)
    c.pool.tt(a, tau, c.half[:, 0:n], ALU.pow)
    root_done = c.pool.mark()
    v.wait(root_done)
    v.tt(tau, mean, a, ALU.subtract)
    then()
    v.tt(work, tau, ordered, ALU.is_le)
    then()
    v.reduce(stat, split(work, NT), ALU.add)
    then()
    v.tt(split(pick, NT), repeat(c.k, NT), stretch(stat, E1), ALU.is_equal)
    then()
    v.tt(pick, pick, tau, ALU.mult)
    then()
    v.reduce(stat, split(pick, NT), ALU.add)
    then()
    v.tt(split(a, NT), split(z, NT), stretch(stat, E1), ALU.subtract)
    then()
    v.ts(a, a, 0.0, None, ALU.max)
    then()
    v.tt(a, a, a, ALU.mult)
    a_done = c.dve.mark()
    yield
    c.pe.wait(a_done, s.free[0])
    for t in range(NT):
        c.pe.turn(b0[0:E1, t * P:(t + 1) * P], a[:, t * E1:(t + 1) * E1], c.ident)
    turned = c.pe.mark()
    aT, g = s.w[0:E1, 0:N], s.w[0:R1, BANK:2 * BANK]
    z1, z2 = s.w[0:R1, 2 * BANK:2 * BANK + N], s.w[0:R1, 2 * BANK + N:3 * BANK]
    hT = split(s.v[:, :], O1 // P)
    c.act.wait(turned)
    c.act.act(aT, b0[0:E1, 0:N], ACT.Copy)
    aT_done = c.act.mark()
    yield
    c.pe.wait(aT_done, s.free[1])
    c.pe.mm(b0[0:R1, 0:N], W("C1")[0:E1, :], aT)
    c.pe.mm(b0[0:R1, N:2 * N], W("C2")[0:E1, :], aT)
    c.pe.mm(b1[0:R1, 0:N], W("Win1"), s.xn[:, :])
    made = c.pe.mark()
    c.act.wait(made)
    c.act.act(g, b0[0:R1, :], ACT.Copy)
    g_done = c.act.mark()
    c.dve.wait(g_done)
    c.dve.stt(z1, b1[0:R1, 0:N], W("bin1")[0:R1, :], g[:, 0:N], ALU.add, ALU.mult)
    z1_done = c.dve.mark()
    yield
    c.pe.wait(z1_done)
    made = []
    for j in range(2):
        for i in range(2):
            o = 2 * j + i
            c.pe.mm(s.bank[j][:, i * N:(i + 1) * N], W("Wout1")[0:R1, o * P:(o + 1) * P], z1)
        made.append(c.pe.mark())
    for j in range(2):
        c.act.wait(made[j])
        c.act.act(s.v[:, j * BANK:(j + 1) * BANK], s.bank[j][:, :], ACT.Gelu)
    gelu_done = c.act.mark()
    yield
    c.pe.wait(gelu_done)
    for o in range(O1 // P):
        c.pe.mm(b0[0:R1, 0:N], W("Win2")[:, o * R1:(o + 1) * R1], hT[:, o, :], start=(o == 0), stop=(o == O1 // P - 1))
    made = c.pe.mark()
    c.dve.wait(made)
    c.dve.stt(z2, b0[0:R1, 0:N], W("bin2")[0:R1, :], g[:, N:2 * N], ALU.add, ALU.mult)
    s.free[0] = c.dve.mark()
    yield
    c.pe.wait(s.free[0])
    c.pe.mm(b1[:, 0:N], W("Wout2")[0:R1, :], z2)
    made = c.pe.mark()
    c.dve.wait(made, c.gates_ready)
    c.dve.stt(s.x[:, :], b1[:, 0:N], c.gates[:, B + 1:B + 2], s.x[:, :], ALU.mult, ALU.add)
    s.free[1] = s.ready = c.dve.mark()
    yield


def cross_attention_2(c, s):
    W = s.W
    normed = yield from layernorm(c, s, s.x[:, :], s.ready, EPS, s.xn[:, :])
    qT, kT = s.kT[:, 0:N], s.kT[:, N:2 * N]
    v = split(s.kT[:, 2 * N:3 * N], NT)
    res, out = s.v[:, 0:N], s.v[:, N:2 * N]
    project(c, s, qT, W("Wq"), s.xn[:, :], normed, W("bq"), 0, 0)
    k_ready = project(c, s, kT, W("Wk"), s.ctx[:, :], normed, W("bk"), 0, 1)
    v_ready = values(c, s, v, s.ctx[:, :], W("Wv"), normed)
    yield
    o_done = yield from attention(c, s, qT, kT, v, k_ready, v_ready, D ** -0.5)
    c.dve.wait(o_done)
    c.dve.stt(res, s.bank[0][:, 0:N], W("bv"), s.ctx[:, :], ALU.add, ALU.add)
    s.free[0] = c.dve.mark()
    out_ready = yield from layernorm(c, s, res, s.free[0], EPS_L2, out)
    c.dve.wait(out_ready)
    c.dve.ts(out, out, W("gamma"), W("beta"), ALU.mult, ALU.add)
    c.dve.wait(c.dve.mark())
    c.dve.stt(s.x[:, :], out, c.gates[:, 2:3], s.x[:, :], ALU.mult, ALU.add)
    s.ready = c.dve.mark()
    yield


def top_two(c, s, biased, keep):
    n = NT * E2
    a, b = s.w[:, 0:n * E2], s.w[:, n * E2:2 * n * E2]
    a4, b4 = (x.rearrange("p (t i j) -> p t i j", t=NT, i=E2) for x in (a, b))
    other = split(biased, NT).unsqueeze(2).to_broadcast([P, NT, E2, E2])
    mine = split(biased, NT).unsqueeze(3).to_broadcast([P, NT, E2, E2])
    tri = split(c.tri, E2).unsqueeze(1).to_broadcast([P, NT, E2, E2])
    c.dve.tt(a4, other, mine, ALU.is_gt)
    c.dve.tt(b4, other, mine, ALU.is_equal)
    c.dve.wait(c.dve.mark())
    c.dve.tt(b4, b4, tri, ALU.mult)
    c.dve.wait(c.dve.mark())
    c.dve.tt(a, a, b, ALU.add)
    c.dve.wait(c.dve.mark())
    c.dve.reduce(keep, split(a, n), ALU.add)
    c.dve.wait(c.dve.mark())
    c.dve.ts(keep, keep, K2 - 0.5, None, ALU.is_lt)
    return c.dve.mark()


def mixture_2(c, s):
    W = s.W
    b0, y = s.bank[0], s.bank[1][:, 0:N]
    n = NT * E2
    normed = yield from layernorm(c, s, s.x[:, :], s.ready, EPS, s.xn[:, :])
    score, biased, keep = (s.sm[:, 192 + n * i:192 + n * (i + 1)] for i in range(3))
    least, total, over = (s.sm[:, 176 + NT * i:176 + NT * (i + 1)] for i in range(3))
    c.pe.wait(normed, s.weights, s.free[0])
    for t in range(NT):
        c.pe.mm(b0[:, t * E2:(t + 1) * E2], s.xn[:, t * P:(t + 1) * P], W("gate_w"))
    made = c.pe.mark()
    c.dve.wait(made)
    c.dve.reduce(least, split(b0[:, 0:n], NT), ALU.max, negate=True)
    shift_done = c.dve.mark()
    c.act.wait(shift_done)
    for t in range(NT):
        c.act.act(score[:, t * E2:(t + 1) * E2], b0[:, t * E2:(t + 1) * E2], ACT.Exp, bias=least[:, t:t + 1],
                  total=total[:, t:t + 1])
    s.free[0] = c.act.mark()
    c.dve.wait(s.free[0])
    c.dve.recip(over, total)
    c.dve.wait(c.dve.mark(), s.weights)
    c.dve.tt(split(score, NT), split(score, NT), stretch(over, E2), ALU.mult)
    c.dve.wait(c.dve.mark())
    c.dve.tt(split(biased, NT), split(score, NT), repeat(W("gate_b"), NT), ALU.add)
    c.dve.wait(c.dve.mark())
    keep_done = top_two(c, s, biased, keep)
    c.dve.wait(keep_done)
    c.dve.tt(keep, keep, score, ALU.mult)
    gate_done = c.dve.mark()
    yield
    gT = s.w[:, 2 * BANK:2 * BANK + N]
    c.pool.fill(gT, 0.0)
    zeroed = c.pool.mark()
    c.pe.wait(gate_done)
    for t in range(NT):
        c.pe.turn(b0[0:E2, t * P:(t + 1) * P], keep[:, t * E2:(t + 1) * E2], c.ident)
    turned = c.pe.mark()
    c.act.wait(turned, zeroed)
    c.act.act(gT[0:E2, :], b0[0:E2, 0:N], ACT.Copy)
    gT_done = c.act.mark()
    yield
    c.pe.wait(gT_done)
    spread = []
    for j in range(E2 // 2):
        bank, dst = s.bank[j % 2], (s.kT if j < 2 else s.oT)[:, (j % 2) * BANK:(j % 2 + 1) * BANK]
        c.pe.wait(s.free[j % 2])
        for i in range(2):
            e = 2 * j + i
            c.pe.mm(bank[:, i * N:(i + 1) * N], c.ident[:, e:e + 1].to_broadcast([P, P]), gT)
        made = c.pe.mark()
        if j % 2:
            c.dve.wait(made)
            c.dve.copy(dst, bank[:, :])
            s.free[1] = c.dve.mark()
        else:
            c.act.wait(made)
            c.act.act(dst, bank[:, :], ACT.Copy)
            s.free[0] = c.act.mark()
        spread.append(s.free[j % 2])
        if j == 1:
            yield
    yield
    c.pe.wait(s.free[1])
    c.pe.mm(y, W("b2")[0:E2, :], gT[0:E2, :], start=True, stop=False)
    w1, w3 = split(W("w1"), 2 * (E2 + 1)), split(W("w3"), 2 * (E2 + 1))
    w2 = split(W("w2"), 2 * (E2 + 1))
    b1, b3 = W("b1"), W("b3")
    turns = 2 * (E2 + 1)
    gated, used = [None] * turns, None
    for i in range(turns + 1):
        if i < turns:
            k = i % 2
            t3, prod, silu = (s.w[0:HH2, (3 * k + m) * N:(3 * k + m + 1) * N] for m in range(3))
            if k:
                t3, prod, silu = (s.w[0:HH2, 3 * BANK + m * N:3 * BANK + (m + 1) * N] for m in range(3))
            c.pe.wait(s.free[0], normed)
            c.pe.mm(b0[0:HH2, 0:N], w1[:, i, :], s.xn[:, :])
            c.pe.mm(b0[0:HH2, N:2 * N], w3[:, i, :], s.xn[:, :])
            made = c.pe.mark()
            c.act.wait(made, *([gated[i - 2]] if i >= 2 else []))
            c.act.act(t3, b0[0:HH2, N:2 * N], ACT.Identity, bias=b3[0:HH2, i:i + 1])
            t3_done = c.act.mark()
            c.dve.wait(t3_done)
            c.dve.stt(prod, b0[0:HH2, 0:N], b1[0:HH2, i:i + 1], t3, ALU.add, ALU.mult)
            s.free[0] = c.dve.mark()
            c.act.wait(s.free[0], *([used] if used else []))
            c.act.act(silu, prod, ACT.Silu)
            gated[i] = c.act.mark()
            e = i // 2
            if e < E2:
                rows = (s.kT if e < 4 else s.oT)[0:HH2, (e % 4) * N:(e % 4 + 1) * N]
                c.pool.wait(gated[i], *spread)
                c.pool.settle()
                c.pool.tt(silu, silu, rows, ALU.mult)
                gated[i] = c.pool.mark()
            hidden_i = silu
        if i:
            c.pe.wait(gated[i - 1])
            c.pe.mm(y, w2[0:HH2, i - 1, :], hidden_before, start=False, stop=(i == turns))
            used = c.pe.mark()
        hidden_before = hidden_i
        yield
    yield from update_stream(c, s, y, used, W("sb2"), B + 2, bank=1)


def cross_attention_3(c, s):
    W = s.W
    b0, b1 = s.bank
    normed = yield from layernorm(c, s, s.x[:, :], s.ready, EPS, s.xn[:, :])
    qT, kT = s.kT[:, 0:N], s.kT[:, N:2 * N]
    v = split(s.kT[:, 2 * N:3 * N], NT)
    scale = DH3 ** -0.5
    project(c, s, qT, W("Wq"), s.xn[:, :], normed, W("bq"), 0, 0)
    k_ready = project(c, s, kT, W("Wk"), s.ctx[:, :], normed, W("bk"), 0, 1)
    c.pe.wait(s.free[1])
    for t in range(NT):
        c.pe.mm(b1[:, t * P:(t + 1) * P], s.ctx[:, t * P:(t + 1) * P], W("Wv"))
    made = c.pe.mark()
    c.dve.wait(made)
    c.dve.tt(v, split(b1[:, 0:N], NT), repeat(W("bv"), NT), ALU.add)
    s.free[1] = v_ready = c.dve.mark()
    vz = [s.v[:, :].rearrange("p (h d) -> p h d", h=2 * H3), s.oT[:, :].rearrange("p (h d) -> p h d", h=2 * H3)]
    vz = [x[:, 0:H3, :] for x in vz]
    c.pool.wait(normed)
    for t in range(NT):
        c.pool.fill(vz[t], 0.0)
    zeroed = c.pool.mark()
    yield
    used, held, done = [normed, normed], [None, None], None
    waiting = None
    for h in range(H3 + 1):
        if h < H3:
            kz, e = s.w[:, (h % 2) * N:(h % 2 + 1) * N], s.w[:, (1 + h % 2) * BANK:(2 + h % 2) * BANK]
            least, total, over = (s.sm[:, 184 + 8 * (h % 2) + NT * i:184 + 8 * (h % 2) + NT * (i + 1)] for i in range(3))
            c.pool.wait(k_ready, used[h % 2])
            c.pool.ts(kz, kT, c.headmask[:, h:h + 1], None, ALU.mult)
            kz_done = c.pool.mark()
            c.pe.wait(kz_done, s.free[0])
            for m in range(NT):
                c.pe.mm(b0[:, m * N:(m + 1) * N], kz[:, m * P:(m + 1) * P], qT)
            scored = c.pe.mark()
            c.dve.wait(scored, used[h % 2])
            c.dve.reduce(least, split(b0[:, :], NT), ALU.max, negate=True)
            c.dve.wait(c.dve.mark())
            c.dve.ts(least, least, scale, None, ALU.mult)
            shift_done = c.dve.mark()
            c.act.wait(shift_done, used[h % 2])
            for m in range(NT):
                c.act.act(e[:, m * N:(m + 1) * N], b0[:, m * N:(m + 1) * N], ACT.Exp, bias=least[:, m:m + 1],
                          scale=scale, total=total[:, m:m + 1])
            s.free[0] = c.act.mark()
            c.dve.wait(s.free[0], zeroed, v_ready)
            c.dve.recip(over, total)
            c.dve.wait(c.dve.mark())
            for m in range(NT):
                c.dve.ts(vz[m][:, h, (h % 4) * DH3:(h % 4 + 1) * DH3], v[:, m, h * DH3:(h + 1) * DH3],
                         over[:, m:m + 1], None, ALU.mult)
            now = (h, e, c.dve.mark())
            yield
        if waiting:
            g, e_g, ready = waiting
            rows = slice(32 * (g // 4), 32 * (g // 4) + 32)
            c.pe.wait(ready, s.free[1])
            for m in range(NT):
                c.pe.mm(b1[rows, 0:N], vz[m][:, g, :], e_g[:, m * N:(m + 1) * N], start=(g % 4 == 0 and m == 0),
                        stop=(g % 4 == 3 and m == NT - 1))
            used[g % 2] = done = c.pe.mark()
        waiting = now
    oT = s.w[:, 3 * BANK:3 * BANK + N]
    c.act.wait(done)
    c.act.act(oT, b1[:, 0:N], ACT.Copy)
    s.free[1] = o_kept = c.act.mark()
    yield
    c.pe.wait(o_kept, s.free[0])
    c.pe.mm(b0[:, 0:N], W("Wo"), oT)
    y_done = c.pe.mark()
    yield from update_stream(c, s, b0[:, 0:N], y_done, W("bo"), 3)


def mixture_3(c, s):
    W = s.W
    b0, b1 = s.bank
    n = NT * E3
    normed = yield from layernorm(c, s, s.x[:, :], s.ready, EPS, s.xn[:, :])
    logit, keep, gate = (s.sm[:, 192 + n * i:192 + n * (i + 1)] for i in range(3))
    stat, total, over = (s.sm[:, 176 + NT * i:176 + NT * (i + 1)] for i in range(3))
    c.pe.wait(normed, s.weights, s.free[0])
    for t in range(NT):
        c.pe.mm(b0[:, t * E3:(t + 1) * E3], s.xn[:, t * P:(t + 1) * P], W("gate_w"))
    made = c.pe.mark()
    c.dve.wait(made)
    c.dve.tt(split(logit, NT), split(b0[:, 0:n], NT), repeat(W("gate_b"), NT), ALU.add)
    s.free[0] = c.dve.mark()
    c.dve.wait(s.free[0])
    keep_done = top_two(c, s, logit, keep)
    c.dve.reduce(stat, split(logit, NT), ALU.max)
    c.dve.wait(c.dve.mark(), keep_done)
    c.dve.tt(split(logit, NT), split(logit, NT), stretch(stat, E3), ALU.subtract)
    shifted_done = c.dve.mark()
    c.act.wait(shifted_done)
    c.act.act(gate, logit, ACT.Exp)
    exp_done = c.act.mark()
    c.dve.wait(exp_done)
    c.dve.tt(gate, gate, keep, ALU.mult)
    c.dve.wait(c.dve.mark())
    c.dve.reduce(total, split(gate, NT), ALU.add)
    c.dve.wait(c.dve.mark())
    c.dve.recip(over, total)
    c.dve.wait(c.dve.mark())
    c.dve.tt(split(gate, NT), split(gate, NT), stretch(over, E3), ALU.mult)
    gate_done = c.dve.mark()
    yield
    c.pe.wait(gate_done, s.free[0])
    for t in range(NT):
        c.pe.turn(b0[0:E3, t * P:(t + 1) * P], gate[:, t * E3:(t + 1) * E3], c.ident)
    turned = c.pe.mark()
    gT = s.w[0:E3, BANK:BANK + N]
    c.act.wait(turned)
    c.act.act(gT, b0[0:E3, 0:N], ACT.Copy)
    s.free[0] = gT_done = c.act.mark()
    yield
    for t in range(NT):
        acc = s.w[:, t * P:(t + 1) * P]
        added = gate_done
        for j in range(2):
            c.pe.wait(normed, s.free[j])
            c.pe.mm(s.bank[j][:, :], s.xn[:, t * P:(t + 1) * P], W("expert_w")[:, j * BANK:(j + 1) * BANK])
            made = c.pe.mark()
            for i in range(4):
                e = 4 * j + i
                src, factor = s.bank[j][:, i * P:(i + 1) * P], gate[:, t * E3 + e:t * E3 + e + 1]
                c.dve.wait(made, added)
                if e == 0:
                    c.dve.ts(acc, src, factor, None, ALU.mult)
                else:
                    c.dve.stt(acc, src, factor, acc, ALU.mult, ALU.add)
                added = c.dve.mark()
            s.free[j] = added
        yield
        c.pe.wait(gT_done, *s.free)
        c.pe.mm(b0[:, 0:P], gT[:, t * P:(t + 1) * P], W("expert_b")[0:E3, :])
        c.pe.turn(b1[:, 0:P], s.x[:, t * P:(t + 1) * P], c.ident)
        made = c.pe.mark()
        c.dve.wait(made, added)
        c.dve.tt(acc, acc, b0[:, 0:P], ALU.add)
        s.free[0] = c.dve.mark()
        res = s.w[:, 3 * P + BANK + t * P:4 * P + BANK + t * P]
        c.dve.wait(s.free[0])
        c.dve.stt(res, acc, c.gates[:, B + 3:B + 4], b1[:, 0:P], ALU.mult, ALU.add)
        s.free[1] = s.ready = c.dve.mark()
        c.loads.wait(s.ready)
        dst, sem = c.out[s.b, t * P:(t + 1) * P, :], c.s_out
        c.loads.put(lambda e, dst=dst, res=res: e.dma_start(dst, res).then_inc(sem, 16))
        yield


def build(nc, x_in, ctx_in, gates_in, const_in, packs_in, out):
    with ExitStack() as stack:
        def sb(name, cols):
            return stack.enter_context(nc.sbuf_tensor(name, [P, cols], F32))

        def sem(name):
            return stack.enter_context(nc.semaphore(name))

        c = Chip()
        c.pe, c.act = Tensor(sem("pe_steps")), Scalar(sem("act_steps"))
        c.dve, c.pool = Elementwise(sem("dve_steps")), Elementwise(sem("pool_steps"))
        s_const, s_x, s_out = sem("const_loaded"), sem("x_loaded"), sem("out_stored")
        s_slot = [sem("slot0_loaded"), sem("slot1_loaded")]
        const = sb("constants", CONST.n)
        gates = sb("gate_columns", 2 * B)
        slots = [sb("slot0", SLOT), sb("slot1", SLOT)]
        tables = [sb("rotary0", 4 * NT * DH), sb("rotary1", 4 * NT * DH)]
        powers = sb("powers", 64)
        c.const_ready, c.gates = (s_const, 32), gates
        c.ident, c.mean, c.ones, c.band, c.tri, c.k, c.invk, c.headmask = (
            CONST(const, n) for n in ("ident", "mean", "ones", "band", "tri", "k", "invk", "headmask"))
        c.qcos, c.qsin, c.kcos, c.ksin = (CONST(const, n) for n in ("qcos", "qsin", "kcos", "ksin"))
        c.minus_half, c.half = powers[:, 0:32], powers[:, 32:64]
        c.tables = tables
        c.out, c.s_out = out, s_out

        loads = [0, 0]
        c.loads = Queue(None)

        def load(stage, after=()):
            k = stage % 2
            loads[k] += 16
            c.loads.wait(*after)
            dst, src, s = slots[k][:, 0:STAGES[stage].n], packs_in[stage], s_slot[k]
            c.loads.put(lambda e: e.dma_start(dst, src).then_inc(s, 16))
            return (s, loads[k])

        c.dve.fill(c.minus_half, -0.5)
        c.dve.fill(c.half, 0.5)
        c.powers_ready = c.dve.mark()
        c.act.wait(c.const_ready)
        c.act.act(gates[:, :], gates[:, :], ACT.Tanh)
        c.gates_ready = c.act.mark()

        xin = x_in
        seqs = []
        for b in range(B):
            s = Sequence()
            s.b = b
            s.x, s.ctx, s.xn, s.z, s.zs = (sb(f"{n}{b}", N) for n in ("x", "ctx", "xn", "z", "zs"))
            s.kT, s.v, s.oT = (sb(f"{n}{b}", 4 * N) for n in ("kT", "v", "oT"))
            s.qz = sb(f"qz{b}", 2 * BANK)
            s.w = sb(f"work{b}", 6 * BANK)
            s.sm = sb(f"small{b}", 512)
            s.before = sb(f"window_before{b}", 8 * WINDOW)
            s.bank = [stack.enter_context(nc.psum_tensor(f"bank{b}_{i}", [P, BANK], F32)) for i in range(2)]
            s.free = [c.powers_ready, c.powers_ready]
            c.pool.fill(s.qz[:, :], 0.0)
            c.pool.fill(s.before[:, :], 0.0)
            s.qz_zero = c.pool.mark()
            c.loads.put(lambda e, s=s, b=b: e.dma_start(s.x[:, :], x_in[:, b * N:(b + 1) * N]).then_inc(s_x, 16))
            c.loads.put(lambda e, s=s, b=b: e.dma_start(s.ctx[:, :], ctx_in[:, b * N:(b + 1) * N]).then_inc(s_x, 16))
            s.x_ready = (s_x, 2 * B * 16)
            seqs.append(s)
            if b == 0:
                c.loads.put(lambda e: e.dma_start(const[:, :], const_in).then_inc(s_const, 16))
                c.loads.put(lambda e: e.dma_start(gates[:, :], gates_in).then_inc(s_const, 16))
        weights = {0: load(0), 1: load(1)}
        left = [B] * len(STAGES)

        mask = L0X(slots[0], "mask")
        c.pool.wait(weights[0])
        c.pool.ts(mask, mask, -1.0, 1.0, ALU.mult, ALU.add)
        c.pool.wait(c.pool.mark())
        c.pool.ts(mask, mask, -1e10, None, ALU.mult)
        c.mask_ready = c.pool.mark()

        def rotary(stage):
            k = stage % 2
            sc = split(L0F(slots[k], "scales"), 4)
            c.pool.wait(c.const_ready, weights[stage])
            tab = tables[k][:, :].rearrange("p (a t d) -> p a t d", a=4, t=NT)
            for a, base in enumerate((c.qcos, c.qsin, c.kcos, c.ksin)):
                for t in range(NT):
                    c.pool.tt(tab[:, a, t, :], split(base, NT)[:, t, :], sc[:, a, :], ALU.mult)
            return c.pool.mark()

        c.ready_tables = {}

        def program(s):
            for stage, pack in enumerate(STAGES):
                while stage not in weights:
                    yield
                s.W = lambda name, pack=pack, stage=stage: pack(slots[stage % 2], name)
                s.weights = weights[stage]
                if pack is L0F and stage not in c.ready_tables:
                    c.ready_tables[stage] = rotary(stage)
                if stage == 0:
                    s.ready = s.x_ready
                    yield from cross_attention_0(c, s)
                elif stage <= DEPTH:
                    s.table_ready = c.ready_tables[stage]
                    yield from local_layer(c, s, stage)
                elif pack is MIX1:
                    yield from cross_attention_1(c, s)
                    yield from mixture_1(c, s)
                    yield from cross_attention_2(c, s)
                elif pack is L2F:
                    yield from mixture_2(c, s)
                else:
                    yield from cross_attention_3(c, s)
                    yield from mixture_3(c, s)
                left[stage] -= 1
                if not left[stage] and stage + 2 < len(STAGES):
                    weights[stage + 2] = load(stage + 2, after=[s.ready])

        turns = [program(s) for s in seqs]
        while turns:
            turns = [t for t in turns if next(t, turns) is not turns]

        block = stack.enter_context(nc.Block())

        @block.sync
        def _(e):
            c.loads.play(e)
            e.wait_ge(s_out, B * NT * 16)

        @block.tensor
        def _(e):
            c.pe.play(e)

        @block.scalar
        def _(e):
            c.act.play(e)

        @block.vector
        def _(e):
            c.dve.play(e)

        @block.gpsimd
        def _(e):
            c.pool.play(e)


def constants():
    f = np.float32
    c = {"ident": np.eye(P, dtype=f), "mean": np.full((P, P), 1.0 / P, f), "ones": np.ones((P, P), f)}
    half = np.arange(0, DH, 2, dtype=f)
    freqs = np.arange(N, dtype=f)[:, None] * (f(1.0) / np.power(f(10000.0), half / f(DH)))[None, :]
    base = (half + f(0.4 * DH)) / f(1.4 * DH)
    power = (np.arange(N, dtype=f) - f(N // 2)) / f(WINDOW // 2)
    scale = np.power(base[None, :], power[:, None]).astype(f)
    cos, sin = np.cos(freqs), np.sin(freqs)
    for name, s in (("q", scale * f(QK_SCALE)), ("k", f(1.0) / scale)):
        for part, table in (("cos", np.concatenate([cos * s, cos * s], 1)),
                            ("sin", np.concatenate([-sin * s, sin * s], 1))):
            c[name + part] = table.reshape(NT, P, DH).transpose(1, 0, 2).reshape(P, NT * DH)
    q, k = np.arange(P)[:, None], np.arange(P)[None, :]
    band = np.where((k <= q) & (k >= q - WINDOW), 0.0, MASKED).astype(f)
    second = band.copy()
    before = (q < WINDOW) & (k >= P - WINDOW) & (k - P >= q - WINDOW)
    second[before] = 0.0
    c["band"] = np.concatenate([band, second], 1)
    c["tri"] = np.broadcast_to((np.arange(E2)[None, :] < np.arange(E2)[:, None]).astype(f).reshape(1, -1), (P, E2 * E2))
    ks = np.arange(1, E1 + 1, dtype=f)
    c["k"], c["invk"] = np.broadcast_to(ks, (P, E1)), np.broadcast_to(f(1.0) / ks, (P, E1))
    c["headmask"] = (np.arange(P)[:, None] // DH3 == np.arange(H3)[None, :]).astype(f)
    return c


def packed(columns, arrays):
    out = np.zeros((P, columns.n), np.float32)
    for name, (start, width) in columns.at.items():
        a = arrays[name]
        a = a.reshape(a.shape[0], -1)
        assert a.shape[1] == width, (name, a.shape, width)
        out[:a.shape[0], start:start + width] = a
    return out


def chunked(a, rows=P):
    n = -(-a.shape[0] // rows)
    full = np.zeros((n * rows,) + a.shape[1:], a.dtype)
    full[:a.shape[0]] = a
    return full.reshape(n, rows, -1).transpose(1, 0, 2).reshape(rows, -1)


def column(a):
    return chunked(a.reshape(-1, 1))


def row(a):
    return np.broadcast_to(a.reshape(1, -1), (P, a.size))


def layouts(i):
    heads = lambda w: w.transpose(1, 0, 2).reshape(D, INNER)
    packs = [packed(L0X, {
        "Wq": heads(i["L0_xattn_Wq"]), "Wk": heads(i["L0_xattn_Wk"]), "Wv": heads(i["L0_xattn_Wv"]),
        "Wo": chunked(i["L0_xattn_Wo"].reshape(DH, H0, D).transpose(1, 0, 2).reshape(INNER, D)),
        "mask": chunked(i["mask_SxS2_ff1"]), "bq": column(i["L0_xattn_bq"]), "bk": column(i["L0_xattn_bk"]),
        "bv": column(i["L0_xattn_bv"]), "bo": column(i["L0_xattn_bo"])})]
    for d in range(DEPTH):
        qs, ks = i["L0_ffn_q_scale"][d], i["L0_ffn_k_scale"][d]
        swap = lambda a: np.concatenate([a[DH // 2:], a[:DH // 2]])
        b1 = i["L0_ffn_b1"][d]
        packs.append(packed(L0F, {
            "Wqkv": i["L0_ffn_Wqkv"][d], "Wo": chunked(i["L0_ffn_Wo"][d]), "W1": i["L0_ffn_W1"][d],
            "W2": chunked(i["L0_ffn_W2"][d]), "scales": row(np.concatenate([qs, swap(qs), ks, swap(ks)])),
            "ln_g": column(i["L0_ffn_ln_g"][d]), "ln_b": column(i["L0_ffn_ln_b"][d]),
            "b1": np.concatenate([column(b1[:FF]), column(b1[FF:])], 1), "b2": column(i["L0_ffn_b2"][d])}))
    one = {}
    for n in ("q_c", "k_s", "v_s", "q_s", "k_c", "v_c"):
        one["W" + n], one["b" + n] = i[f"L1_xattn_W{n}"].T, column(i[f"L1_xattn_b{n}"])
    wg = i["L1_xattn_Wg"].T
    one.update({
        "Wg_a": wg[:D], "Wg_b": wg[D:], "bg": column(i["L1_xattn_bg"]), "proj": i["L1_ffn_proj"],
        "C1": i["L1_ffn_C1"], "C2": i["L1_ffn_C2"], "Win1": i["L1_ffn_Win1"][:D], "bin1": i["L1_ffn_Win1"][D:].T,
        "Wout1": i["L1_ffn_Wout1"].T, "Win2": chunked(i["L1_ffn_Win2"][:O1]), "bin2": i["L1_ffn_Win2"][O1:].T,
        "Wout2": i["L1_ffn_Wout2"].T, "gamma": column(i["L2_xattn_gamma"]), "beta": column(i["L2_xattn_beta"])})
    for n in "qkv":
        one["W" + n], one["b" + n] = i["L2_xattn_W" + n], column(i["L2_xattn_b" + n])
    packs.append(packed(MIX1, one))
    two = {}
    for n in "13":
        w = np.concatenate([i[f"L2_ffn_w{n}"], i[f"L2_ffn_sw{n}"][None]], 0)
        b = np.concatenate([i[f"L2_ffn_b{n}"], i[f"L2_ffn_sb{n}"][None]], 0)
        two["w" + n] = w.transpose(1, 0, 2)
        two["b" + n] = b.reshape(2 * (E2 + 1), HH2).T
    w2 = np.concatenate([i["L2_ffn_w2"], i["L2_ffn_sw2"][None]], 0)
    two.update({"w2": w2.reshape(2 * (E2 + 1), HH2, D).transpose(1, 0, 2), "b2": i["L2_ffn_b2"],
                "gate_w": i["L2_ffn_gate_w"].T, "gate_b": row(i["L2_ffn_gate_b"]), "sb2": column(i["L2_ffn_sb2"])})
    packs.append(packed(L2F, two))
    kv, bkv = i["L3_xattn_Wkv"], i["L3_xattn_bkv"]
    packs.append(packed(L3, {
        "Wq": i["L3_xattn_Wq"], "Wk": kv[:, :D], "Wv": kv[:, D:], "Wo": i["L3_xattn_Wo"],
        "bq": column(i["L3_xattn_bq"]), "bk": column(bkv[:D]), "bv": row(bkv[D:]), "bo": column(i["L3_xattn_bo"]),
        "gate_w": i["L3_ffn_gate_w"].T, "gate_b": row(i["L3_ffn_gate_b"]),
        "expert_w": i["L3_ffn_expert_w"].transpose(1, 0, 2), "expert_b": i["L3_ffn_expert_b"]}))
    return packs


def kernel(**inputs):
    import concourse.bacc as bacc
    from concourse.bass_utils import run_bass_kernel_spmd

    i = {name: np.asarray(a) for name, a in inputs.items()}
    arrays = {"x_t": i["x"].transpose(2, 0, 1).reshape(D, B * N),
              "ctx_t": i["ctx_1024"].transpose(2, 0, 1).reshape(D, B * N),
              "gates": np.concatenate([row(i["g_xattn"]), row(i["g_ffn"])], 1),
              "const": packed(CONST, constants())}
    for n, p in enumerate(layouts(i)):
        arrays[f"pack{n}"] = p
    arrays = {n: np.ascontiguousarray(a) for n, a in arrays.items()}
    nc = bacc.Bacc("TRN2", target_bir_lowering=False, num_devices=1)
    aps = {n: nc.dram_tensor(f"in_{n}_dram", a.shape, F32, kind="ExternalInput").ap() for n, a in arrays.items()}
    out = nc.dram_tensor("out_dram", (B, N, D), F32, kind="ExternalOutput").ap()
    build(nc, aps["x_t"], aps["ctx_t"], aps["gates"], aps["const"],
          [aps[f"pack{n}"] for n in range(len(STAGES))], out)
    r = run_bass_kernel_spmd(nc, [{f"in_{n}_dram": a for n, a in arrays.items()}], core_ids=[0])
    return r.results[0]["out_dram"]
```

```python
from contextlib import ExitStack

import numpy as np

import concourse.bass as bass
from concourse import mybir

F32 = mybir.dt.float32
ALU = mybir.AluOpType
ACT = mybir.ActivationFunctionType
AX = mybir.AxisListType

B, N, D = 4, 256, 128
P = 128
NT = N // P
BANK = 512
H0, DH = 16, 64
PAIRS = H0 * DH // P
INNER = H0 * DH
DEPTH, WINDOW = 6, 32
FF = D * 4 * 2 // 3
FFC = [(i, min(P, FF - i)) for i in range(0, FF, P)]
E1, R1, O1 = 16, 64, 512
E2, HID2, K2 = 8, 176, 2
HH2 = HID2 // 2
H3, DH3 = 16, 8
E3 = 8
QK_SCALE = 8.0
MASKED = -1e30
LOWEST = -3.0e38
HOP = 60.0
EPS, EPS_L2 = 1e-5, 1e-6


class Columns:

    def __init__(self, pieces):
        self.at, self.n = {}, 0
        for name, width in pieces:
            self.at[name] = (self.n, width)
            self.n += width

    def __call__(self, tile, name):
        start, width = self.at[name]
        return tile[:, start:start + width]


CONST = Columns([("ident", P), ("mean", P), ("ones", P), ("qcos", NT * DH), ("qsin", NT * DH),
                 ("kcos", NT * DH), ("ksin", NT * DH),
                 ("band", NT * P), ("tri", E2 * E2), ("k", E1), ("invk", E1), ("headmask", H3)])
L0X = Columns([("Wq", INNER), ("Wk", INNER), ("Wv", INNER), ("Wo", PAIRS * D), ("mask", NT * N),
               ("bq", PAIRS), ("bk", PAIRS), ("bv", PAIRS), ("bo", 1)])
L0F = Columns([("Wqkv", 3 * INNER), ("Wo", PAIRS * D), ("W1", 2 * FF), ("W2", len(FFC) * D),
               ("scales", 4 * DH), ("ln_g", 1), ("ln_b", 1), ("b1", 2 * len(FFC)), ("b2", 1)])
MIX1 = Columns([(n, D) for n in ("Wq_c", "Wk_s", "Wv_s", "Wq_s", "Wk_c", "Wv_c", "Wg_a", "Wg_b")]
               + [(n, 1) for n in ("bq_c", "bk_s", "bv_s", "bq_s", "bk_c", "bv_c", "bg")]
               + [("proj", E1), ("C1", R1), ("Win1", R1), ("Wout1", O1), ("C2", R1),
                  ("Win2", O1 // P * R1), ("Wout2", D), ("bin1", 1), ("bin2", 1)]
               + [("Wq", D), ("Wk", D), ("Wv", D), ("bq", 1), ("bk", 1), ("bv", 1),
                  ("gamma", 1), ("beta", 1)])
L2F = Columns([("w1", (E2 + 1) * HID2), ("w3", (E2 + 1) * HID2), ("w2", (E2 + 1) * 2 * D),
               ("b1", (E2 + 1) * 2), ("b3", (E2 + 1) * 2), ("b2", D), ("gate_w", E2),
               ("gate_b", E2), ("sb2", 1)])
L3 = Columns([("Wq", D), ("Wk", D), ("Wv", D), ("Wo", D), ("bq", 1), ("bk", 1), ("bv", D),
              ("bo", 1), ("gate_w", E3), ("gate_b", E3), ("expert_w", E3 * D), ("expert_b", D)])
STAGES = [L0X] + [L0F] * DEPTH + [MIX1, L2F, L3]
SLOT = max(s.n for s in STAGES)


class Mark:

    def __init__(self, sem=None, value=None):
        self.sem, self.value, self.at = sem, value, None


class Stream:

    def __init__(self):
        self.steps, self.last = [], None

    def wait(self, *marks):
        if self.steps and not self.steps[-1][1]:
            self.steps[-1][0] += marks
        else:
            self.steps.append([list(marks), [], None, 0.0])

    def put(self, op, ns=0.0):
        if not self.steps or self.steps[-1][2]:
            self.steps.append([[], [], None, 0.0])
        self.steps[-1][1].append(op)
        self.steps[-1][3] += ns

    def mark(self):
        self.last = self.steps[-1][2] = Mark()
        return self.last

    def settle(self):
        self.wait(SETTLE)

    def load(self, op, sem, value, ns):
        self.put(lambda e: op(e).then_inc(sem, 16), ns)
        self.steps[-1][2] = Mark(sem, value)
        return self.steps[-1][2]


SETTLE = Mark()


class Engine:

    def __init__(self, sem):
        self.sem, self.count, self.ops, self.passed, self.clock = sem, 0, [], {}, 0.0

    def issue(self, step):
        marks, ops, mark, ns = step
        for m in marks:
            sem, value = (self.sem, self.count) if m is SETTLE else (m.sem, m.value)
            if self.passed.get(sem.name, 0) < value:
                self.passed[sem.name] = value
                self.ops.append((sem, value))
        ops = list(ops)
        if mark and not mark.sem:
            last, own = ops.pop(), self.sem
            ops.append(lambda e: last(e).then_inc(own, 1))
            self.count += 1
            mark.sem, mark.value = own, self.count
        self.ops += ops
        self.clock = max([self.clock] + [m.at for m in marks if m is not SETTLE]) + ns
        if mark:
            mark.at = self.clock + HOP

    def play(self, engine):
        for op in self.ops:
            if isinstance(op, tuple):
                engine.wait_ge(*op)
            else:
                op(engine)


def in_order_of_issue(engines, programs):
    at = [[0] * len(engines) for _ in programs]
    while True:
        best = None
        for p, program in enumerate(programs):
            for n, stream in enumerate(program):
                if at[p][n] == len(stream.steps):
                    continue
                ready = 0.0
                for m in stream.steps[at[p][n]][0]:
                    if m is not SETTLE:
                        if m.at is None:
                            break
                        ready = max(ready, m.at)
                else:
                    key = (max(ready, engines[n].clock), ready)
                    if best is None or key < best[0]:
                        best = (key, p, n)
        if best is None:
            break
        _, p, n = best
        engines[n].issue(programs[p][n].steps[at[p][n]])
        at[p][n] += 1
    assert all(at[p][n] == len(s.steps) for p, program in enumerate(programs) for n, s in enumerate(program))


def columns(ap):
    return int(np.prod(ap.shape[1:]))


class Tensor(Stream):
    def mm(self, out, lhsT, rhs, start=True, stop=True):
        self.put(lambda e: e.matmul(out, lhsT, rhs, start=start, stop=stop, skip_group_check=True),
                 1.7 * max(columns(rhs), P) * (1.0 if lhsT.shape[0] == P else 2.0)
                 * (0.55 if columns(lhsT) <= DH else 1.0))

    def turn(self, out, in_, ident):
        rows = in_.shape[0]
        self.put(lambda e: e.transpose(out, in_, ident[0:rows, 0:rows]), 110.0)


class Scalar(Stream):
    def act(self, out, in_, func, bias=0.0, scale=1.0, total=None):
        if total is None:
            self.put(lambda e: e.activation(out, in_, func, bias=bias, scale=scale), 190 + 0.83 * columns(out))
        else:
            self.put(lambda e: e.activation(out, in_, func, bias=bias, scale=scale, accum_out=total),
                     280 + 0.83 * columns(out))


class Elementwise(Stream):

    def __init__(self, per):
        super().__init__()
        self.per = per

    def add(self, op, ap):
        self.put(op, 70 + self.per * columns(ap))

    def tt(self, out, a, b, op):
        self.add(lambda e: e.tensor_tensor(out, a, b, op), out)

    def power(self, out, a, exponent):
        self.put(lambda e: e.tensor_tensor(out, a, exponent, ALU.pow), 170.0 * columns(out))

    def ts(self, out, a, s1, s2, op0, op1=None):
        if op1 is None:
            self.add(lambda e: e.tensor_scalar(out, a, s1, None, op0), out)
        else:
            self.add(lambda e: e.tensor_scalar(out, a, s1, s2, op0, op1), out)

    def copy(self, out, a):
        self.add(lambda e: e.tensor_copy(out, a), out)

    def fill(self, out, value):
        self.add(lambda e: e.memset(out, value), out)

    def stt(self, out, a, s, b, op0, op1):
        self.add(lambda e: e.scalar_tensor_tensor(out=out, in0=a, scalar=s, in1=b, op0=op0, op1=op1), out)

    def reduce(self, out, a, op, negate=False):
        self.add(lambda e: e.tensor_reduce(out, a, AX.X, op, negate=negate), a)

    def add_max(self, out, a, b, largest):
        self.add(lambda e: e.tensor_tensor_reduce(out, a, b, 1.0, LOWEST, ALU.add, ALU.max, largest), out)

    def recip(self, out, a):
        self.add(lambda e: e.reciprocal(out, a), out)

    def top8(self, out, a):
        self.add(lambda e: e.max(out, a), out)

    def drop(self, out, values, a):
        self.add(lambda e: e.match_replace(out, values, a, LOWEST), out)

    def scan(self, out, a, b):
        self.add(lambda e: e.tensor_tensor_scan(out, a, b, 0.0, ALU.mult, ALU.add), out)


def split(ap, n):
    return ap.rearrange("p (n k) -> p n k", n=n)


def stretch(ap, k):
    return ap.unsqueeze(2).to_broadcast([ap.shape[0], ap.shape[1], k])


def repeat(ap, n):
    return ap.unsqueeze(1).to_broadcast([ap.shape[0], n, ap.shape[1]])


class Shared:
    pass


class Program:

    def __init__(self, shared):
        self.shared = shared
        self.pe, self.act, self.dve, self.pool, self.sync = Tensor(), Scalar(), Elementwise(1.04), Elementwise(2.0), Stream()
        self.streams = [self.pe, self.act, self.dve, self.pool, self.sync]


class Sequence:
    pass


def layernorm(c, s, src, ready, eps, out):
    centred, square, diag = s.w[:, 0:N], s.w[:, N:2 * N], s.w[:, 2 * N:3 * N]
    var, rstd = s.sm[:, 0:NT], s.sm[:, NT:2 * NT]
    b0, b1 = s.bank
    c.pe.wait(ready, s.free[0], c.shared.const_ready)
    c.pe.mm(b0[:, 0:N], c.shared.mean, src)
    mean_done = c.pe.mark()
    c.dve.wait(mean_done, ready)
    c.dve.tt(centred, src, b0[:, 0:N], ALU.subtract)
    centred_done = c.dve.mark()
    c.act.wait(centred_done)
    c.act.act(square, centred, ACT.Square)
    square_done = c.act.mark()
    c.pe.wait(square_done, s.free[1])
    for t in range(NT):
        c.pe.mm(b1[:, t:t + 1], square[:, t * P:(t + 1) * P], c.shared.mean[:, 0:1])
    var_done = c.pe.mark()
    c.dve.wait(var_done)
    c.dve.ts(var, b1[:, 0:NT], eps, None, ALU.add)
    s.free[1] = c.dve.mark()
    c.pool.wait(s.free[1], c.shared.powers_ready)
    c.pool.power(rstd, var, c.shared.minus_half[:, 0:NT])
    rstd_done = c.pool.mark()
    c.dve.wait(rstd_done)
    for t in range(NT):
        c.dve.ts(diag[:, t * P:(t + 1) * P], c.shared.ident, rstd[:, t:t + 1], None, ALU.mult)
    diag_done = c.dve.mark()
    c.pe.wait(diag_done)
    for t in range(NT):
        c.pe.mm(b0[:, t * P:(t + 1) * P], c.shared.ones, diag[:, t * P:(t + 1) * P])
    spread = c.pe.mark()
    c.dve.wait(spread)
    c.dve.tt(out, centred, b0[:, 0:N], ALU.mult)
    s.free[0] = c.dve.mark()
    return s.free[0]


def cross_attention_0(c, s):
    b0, b1 = s.bank
    normed = layernorm(c, s, s.x[:, :], s.ready, EPS, s.xn[:, :])
    s.normed = normed
    W = s.W
    qz = s.qz[:, :].rearrange("p (r z n) -> p r z n", r=4, z=2)
    kT = s.kT[:, 0:N]
    v = s.kT[:, N:2 * N].rearrange("p (t d) -> p t d", t=NT)
    mask = split(W("mask"), NT)
    bq8 = s.sm[:, 8:8 + PAIRS]
    c.dve.wait(s.weights)
    c.dve.ts(bq8, W("bq"), 0.125, None, ALU.mult)
    bq8_done = c.dve.mark()
    for pair in range(PAIRS):
        cols = slice(pair * P, (pair + 1) * P)
        c.pe.wait(normed, s.weights, s.x_ready, *s.free)
        c.pe.mm(b0[:, 0:N], W("Wq")[:, cols], s.xn[:, :])
        c.pe.mm(b0[:, N:2 * N], W("Wk")[:, cols], s.ctx[:, :])
        qk_done = c.pe.mark()
        for t in range(NT):
            c.pe.mm(b1[:, t * P:(t + 1) * P], s.ctx[:, t * P:(t + 1) * P], W("Wv")[:, cols])
        v_done = c.pe.mark()
        c.act.wait(qk_done, s.weights, bq8_done, s.qz_zero)
        for z in range(2):
            rows = slice(z * DH, (z + 1) * DH)
            c.act.act(qz[rows, 0:NT, z, :], split(b0[rows, 0:N], NT), ACT.Identity, bias=bq8[rows, pair:pair + 1], scale=0.125)
        c.act.act(kT, b0[:, N:2 * N], ACT.Identity, bias=W("bk")[:, pair:pair + 1])
        qk_kept = c.act.mark()
        c.dve.wait(v_done)
        c.dve.copy(v, b1[:, 0:N].rearrange("p (t d) -> p t d", t=NT))
        v_kept = c.dve.mark()
        most, least, total, over = (s.sm[:, 16 + 4 * i:20 + 4 * i] for i in range(4))
        c.pe.wait(qk_kept, v_kept)
        scored = []
        for z in range(2):
            for t in range(NT):
                c.pe.mm(s.bank[z][:, t * N:(t + 1) * N], qz[:, t, z, :], kT)
            scored.append(c.pe.mark())
        e = [s.w[:, z * BANK:(z + 1) * BANK] for z in range(2)]
        pT = [s.w[:, (2 + z) * BANK:(3 + z) * BANK] for z in range(2)]
        normalised, shift_done, exp_done = [], [], []
        for z in range(2):
            c.dve.wait(scored[z], c.shared.mask_ready)
            for t in range(NT):
                i = 2 * z + t
                c.dve.add_max(e[z][:, t * N:(t + 1) * N], s.bank[z][:, t * N:(t + 1) * N], mask[:, t, :],
                              most[:, i:i + 1])
            c.dve.wait(c.dve.mark())
            c.dve.ts(least[:, 2 * z:2 * z + 2], most[:, 2 * z:2 * z + 2], -1.0, None, ALU.mult)
            shift_done.append(c.dve.mark())
        for z in range(2):
            c.act.wait(shift_done[z])
            for t in range(NT):
                i = 2 * z + t
                c.act.act(e[z][:, t * N:(t + 1) * N], e[z][:, t * N:(t + 1) * N], ACT.Exp,
                          bias=least[:, i:i + 1], total=total[:, i:i + 1])
            exp_done.append(c.act.mark())
        for z in range(2):
            c.dve.wait(exp_done[z])
            c.dve.recip(over[:, 2 * z:2 * z + 2], total[:, 2 * z:2 * z + 2])
            over_done = c.dve.mark()
            c.pool.wait(over_done)
            c.pool.tt(split(e[z], NT), split(e[z], NT), stretch(over[:, 2 * z:2 * z + 2], N), ALU.mult)
            normalised.append(c.pool.mark())
        kept = []
        for z in range(2):
            c.pe.wait(normalised[z])
            for m in range(NT):
                for t in range(NT):
                    c.pe.turn(s.bank[z][:, m * N + t * P:m * N + (t + 1) * P],
                              e[z][:, t * N + m * P:t * N + (m + 1) * P], c.shared.ident)
            turned = c.pe.mark()
            q = c.dve if z else c.act
            q.wait(turned)
            if z:
                c.dve.copy(pT[z], s.bank[z][:, :])
            else:
                c.act.act(pT[z], s.bank[z][:, :], ACT.Copy)
            kept.append(q.mark())
        c.pe.wait(*kept)
        for m in range(NT):
            for z in range(2):
                c.pe.mm(b0[z * DH:(z + 1) * DH, 0:N], v[:, m, z * DH:(z + 1) * DH],
                        pT[z][:, m * N:(m + 1) * N], start=(m == 0), stop=(m == NT - 1))
        o_done = c.pe.mark()
        oT = (s.v if pair < 4 else s.oT)[:, (pair % 4) * N:(pair % 4 + 1) * N]
        c.act.wait(o_done)
        c.act.act(oT, b0[:, 0:N], ACT.Identity, bias=W("bv")[:, pair:pair + 1])
        s.free = [c.act.mark(), kept[1]]
    c.pe.wait(*s.free)
    for pair in range(PAIRS):
        oT = (s.v if pair < 4 else s.oT)[:, (pair % 4) * N:(pair % 4 + 1) * N]
        c.pe.mm(b0[:, 0:N], W("Wo")[:, pair * D:(pair + 1) * D], oT, start=(pair == 0), stop=(pair == PAIRS - 1))
    y_done = c.pe.mark()
    update_stream(c, s, b0[:, 0:N], y_done, W("bo"), 0)


def update_stream(c, s, y, y_done, bias, gate, bank=0):
    tmp = s.w[:, 0:N]
    c.dve.wait(y_done, c.shared.gates_ready, s.weights)
    c.dve.ts(tmp, y, bias, c.shared.gates[:, gate:gate + 1], ALU.add, ALU.mult)
    s.free[bank] = c.dve.mark()
    c.dve.wait(s.free[bank])
    c.dve.tt(s.x[:, :], s.x[:, :], tmp, ALU.add)
    s.ready = c.dve.mark()


def shifted(c, s, ready):
    c.dve.wait(ready)
    c.dve.copy(s.zs[0:DH, :], s.z[0:DH, :])
    c.dve.copy(s.zs[DH:P, 1:N], s.z[DH:P, 0:N - 1])
    return c.dve.mark()


def local_layer(c, s, stage):
    b0, b1 = s.bank
    W = s.W
    if stage == 1:
        z_ready = layernorm(c, s, s.x[:, :], s.ready, EPS, s.z[:, :])
        c.dve.fill(s.zs[DH:P, 0:1], 0.0)
    else:
        z_ready = s.z_ready
    zs_ready = shifted(c, s, z_ready)
    tab = c.shared.tables[stage % 2][:, :].rearrange("p (a t d) -> p a t d", a=4, t=NT)
    qz = s.qz[:, :].rearrange("p (r z n) -> p r z n", r=4, z=2)
    kT = split(s.kT[:, :], 4)
    v = split(s.v[:, :], NT)
    oT = split(s.oT[:, :], 4)
    before = split(s.before[:, :], 8)
    w = [s.w[:, i * BANK:(i + 1) * BANK] for i in range(6)]
    sq_sum, norm, most, least, total, over = (s.sm[:, 64 + 16 * i:80 + 16 * i] for i in range(6))
    heads = 8
    for g in range(H0 // heads):
        for t in range(NT):
            tile = slice(t * P, (t + 1) * P)
            made = []
            for i in range(2):
                c.pe.wait(zs_ready, s.weights, s.free[i])
                c.pe.mm(s.bank[i][:, :], s.zs[:, tile], W("Wqkv")[:, i * INNER + g * BANK:i * INNER + (g + 1) * BANK])
                made.append(c.pe.mark())
            squared = []
            for i in range(2):
                c.act.wait(made[i], *s.free)
                c.act.act(w[i], s.bank[i][:, :], ACT.Square)
                squared.append(c.act.mark())
            for i in range(2):
                c.dve.wait(squared[i])
                c.dve.reduce(sq_sum[:, i * heads:(i + 1) * heads], split(w[i], heads), ALU.add)
            summed = c.dve.mark()
            c.pool.wait(summed, c.shared.powers_ready)
            c.pool.ts(norm, sq_sum, 1e-24, None, ALU.max)
            c.pool.wait(c.pool.mark())
            c.pool.power(norm, norm, c.shared.minus_half[:, 0:2 * heads])
            norm_done = c.pool.mark()
            rotated, sine_done = [], []
            for i in range(2):
                c.dve.wait(norm_done)
                c.dve.tt(split(w[i], heads), split(s.bank[i][:, :], heads), stretch(norm[:, i * heads:(i + 1) * heads], DH),
                         ALU.mult)
                s.free[i] = c.dve.mark()
                c.pool.wait(s.free[i], s.table_ready)
                here, turned, half = split(w[i], heads), split(w[2 + i], heads), DH // 2
                c.pool.tt(turned[:, :, 0:half], here[:, :, half:DH], repeat(tab[:, 2 * i + 1, t, 0:half], heads), ALU.mult)
                c.pool.tt(turned[:, :, half:DH], here[:, :, 0:half], repeat(tab[:, 2 * i + 1, t, half:DH], heads), ALU.mult)
                sine_done.append(c.pool.mark())
            for i in range(2):
                c.dve.wait(s.free[i], s.table_ready)
                c.dve.tt(split(w[4 + i], heads), split(w[i], heads), repeat(tab[:, 2 * i, t, :], heads), ALU.mult)
                cosine_done = c.dve.mark()
            c.pe.wait(s.free[0])
            c.pe.mm(b0[:, :], s.zs[:, tile], W("Wqkv")[:, 2 * INNER + g * BANK:2 * INNER + (g + 1) * BANK])
            v_done = c.pe.mark()
            c.act.wait(v_done)
            c.act.act(v[:, t, :], b0[:, :], ACT.Copy)
            v_kept = c.act.mark()
            for i in range(2):
                c.dve.wait(cosine_done, sine_done[i])
                c.dve.tt(w[4 + i], w[4 + i], w[2 + i], ALU.add)
                rotated.append(c.dve.mark())
            c.pe.wait(rotated[0], s.free[1])
            for r in range(4):
                c.pe.turn(b1[:, r * P:(r + 1) * P], w[4][:, r * P:(r + 1) * P], c.shared.ident)
            turned_q = c.pe.mark()
            c.pe.wait(rotated[1], v_kept)
            for r in range(4):
                c.pe.turn(b0[:, r * P:(r + 1) * P], w[5][:, r * P:(r + 1) * P], c.shared.ident)
            turned_k = c.pe.mark()
            c.act.wait(turned_q, s.qz_zero)
            c.act.act(qz[0:DH, :, 0, :], split(b1[0:DH, :], 4), ACT.Copy)
            q_kept_0 = c.act.mark()
            c.dve.wait(turned_q, s.qz_zero)
            c.dve.copy(qz[DH:P, :, 1, :], split(b1[DH:P, :], 4))
            q_kept_1 = c.dve.mark()
            c.act.wait(turned_k)
            c.act.act(kT[:, :, tile], split(b0[:, :], 4), ACT.Copy)
            k_kept = c.act.mark()
            scored = []
            c.pe.wait(q_kept_0, q_kept_1, k_kept)
            for j in range(2):
                for hh in range(4):
                    r, z = divmod(4 * j + hh, 2)
                    c.pe.mm(s.bank[j][:, hh * P:(hh + 1) * P], qz[:, r, z, :], kT[:, r, tile])
                    if t:
                        c.pe.mm(s.bank[j][0:WINDOW, (hh + 1) * P - WINDOW:(hh + 1) * P], qz[:, r, z, 0:WINDOW],
                                kT[:, r, P - WINDOW:P])
                scored.append(c.pe.mark())
            normalised, shift_done, exp_done = [], [], []
            for j in range(2):
                c.dve.wait(scored[j])
                for hh in range(4):
                    c.dve.add_max(w[j][:, hh * P:(hh + 1) * P], s.bank[j][:, hh * P:(hh + 1) * P],
                                  c.shared.band[:, tile], most[:, 4 * j + hh:4 * j + hh + 1])
                s.free[j] = c.dve.mark()
                c.dve.wait(s.free[j])
                quad = slice(4 * j, 4 * j + 4)
                c.dve.ts(least[:, quad], most[:, quad], -1.0, None, ALU.mult)
                shift_done.append(c.dve.mark())
            for j in range(2):
                c.act.wait(shift_done[j])
                for hh in range(4):
                    i = 4 * j + hh
                    c.act.act(w[j][:, hh * P:(hh + 1) * P], w[j][:, hh * P:(hh + 1) * P], ACT.Exp,
                              bias=least[:, i:i + 1], total=total[:, i:i + 1])
                exp_done.append(c.act.mark())
            for j in range(2):
                quad = slice(4 * j, 4 * j + 4)
                c.dve.wait(exp_done[j])
                c.dve.recip(over[:, quad], total[:, quad])
                over_done = c.dve.mark()
                c.pool.wait(over_done)
                c.pool.tt(split(w[j], 4), split(w[j], 4), stretch(over[:, quad], P), ALU.mult)
                normalised.append(c.pool.mark())
            kept = []
            for j in range(2):
                c.pe.wait(normalised[j], s.free[j])
                for hh in range(4):
                    c.pe.turn(s.bank[j][:, hh * P:(hh + 1) * P], w[j][:, hh * P:(hh + 1) * P], c.shared.ident)
                turned = c.pe.mark()
                q = c.dve if j else c.act
                q.wait(turned)
                if j:
                    c.dve.copy(w[2 + j], s.bank[j][:, :])
                else:
                    c.act.act(w[2 + j], s.bank[j][:, :], ACT.Copy)
                copied = q.mark()
                if t:
                    last, quad = slice(P - WINDOW, P), slice(4 * j, 4 * j + 4)
                    early = split(w[2 + j], 4)[last, :, 0:WINDOW]
                    c.dve.wait(copied, s.qz_zero)
                    c.dve.copy(before[last, quad, :], split(s.bank[j][:, :], 4)[last, :, 0:WINDOW])
                    kept.append(c.dve.mark())
                    c.dve.fill(early, 0.0)
                    kept.append(c.dve.mark())
                else:
                    kept.append(copied)
            c.pe.wait(*kept)
            for h in range(heads):
                r, z = divmod(h, 2)
                j, hh = divmod(h, 4)
                pT = w[2 + j][:, hh * P:(hh + 1) * P]
                rows, vh = slice(z * DH, (z + 1) * DH), slice(h * DH, (h + 1) * DH)
                c.pe.mm(b0[rows, r * P:(r + 1) * P], v[:, t, vh], pT, start=True, stop=(t == 0))
                if t:
                    c.pe.mm(b0[rows, r * P:r * P + WINDOW], v[:, 0, vh], before[:, h, :], start=False, stop=True)
            o_done = c.pe.mark()
            c.act.wait(o_done)
            c.act.act(oT[:, :, tile], split(b0[:, :], 4), ACT.Copy)
            s.free = [c.act.mark(), kept[-1]]
        c.pe.wait(*s.free)
        for r in range(4):
            c.pe.mm(b1[:, 0:N], W("Wo")[:, (4 * g + r) * D:(4 * g + r + 1) * D], oT[:, r, :], start=(r == 0), stop=(r == 3))
        y_done = c.pe.mark()
        c.dve.wait(y_done, zs_ready)
        c.dve.tt(s.z[:, :], s.z[:, :], b1[:, 0:N], ALU.add)
        s.free[1] = z_ready = c.dve.mark()
    zs_ready = shifted(c, s, z_ready)
    normed = layernorm(c, s, s.zs[:, :], zs_ready, EPS, s.xn[:, :])
    c.dve.wait(normed, s.weights)
    c.dve.ts(s.xn[:, :], s.xn[:, :], W("ln_g"), W("ln_b"), ALU.mult, ALU.add)
    normed = c.dve.mark()
    hidden = []
    for i, (start, m) in enumerate(FFC):
        bank = s.bank[i % 2]
        c.pe.wait(normed, s.weights, s.free[i % 2])
        for z in range(2):
            c.pe.mm(bank[0:m, z * N:(z + 1) * N], W("W1")[:, z * FF + start:z * FF + start + m], s.xn[:, :])
        made = c.pe.mark()
        gelu, prod = w[i][0:m, 0:N], w[i][0:m, N:2 * N]
        bias = W("b1")
        c.act.wait(made, normed, s.weights)
        c.act.act(gelu, bank[0:m, N:2 * N], ACT.Gelu, bias=bias[0:m, len(FFC) + i:len(FFC) + i + 1])
        gelu_done = c.act.mark()
        c.dve.wait(gelu_done)
        c.dve.stt(prod, bank[0:m, 0:N], bias[0:m, i:i + 1], gelu, ALU.add, ALU.mult)
        s.free[i % 2] = c.dve.mark()
        hidden.append((prod, s.free[i % 2], m))
    for i, (prod, ready, m) in enumerate(hidden):
        c.pe.wait(ready, s.free[1])
        c.pe.mm(b1[:, 0:N], W("W2")[0:m, i * D:(i + 1) * D], prod, start=(i == 0), stop=(i == len(hidden) - 1))
    y_done = c.pe.mark()
    c.dve.wait(y_done)
    c.dve.stt(s.z[:, :], b1[:, 0:N], W("b2"), s.z[:, :], ALU.add, ALU.add)
    s.free[1] = s.z_ready = s.ready = c.dve.mark()
    if stage == DEPTH:
        c.dve.wait(s.z_ready, c.shared.gates_ready)
        c.dve.stt(s.x[:, :], s.z[:, :], c.shared.gates[:, B:B + 1], s.x[:, :], ALU.mult, ALU.add)
        s.ready = c.dve.mark()


def project(c, s, out, w, src, ready, bias, bank, half=0):
    dst = s.bank[bank][:, half * N:(half + 1) * N]
    c.pe.wait(ready, s.weights, s.free[bank])
    c.pe.mm(dst, w, src)
    made = c.pe.mark()
    c.act.wait(made, s.weights)
    c.act.act(out, dst, ACT.Identity, bias=bias)
    s.free[bank] = c.act.mark()
    return s.free[bank]


def attention(c, s, qT, kT, v, qk_ready, v_ready, scale):
    b0, b1 = s.bank
    e, pT = s.w[:, 0:BANK], s.w[:, BANK:2 * BANK]
    least, total, over = (s.sm[:, 160 + 2 * i:162 + 2 * i] for i in range(3))
    c.pe.wait(qk_ready, s.free[0])
    for t in range(NT):
        c.pe.mm(b0[:, t * N:(t + 1) * N], qT[:, t * P:(t + 1) * P], kT)
    scored = c.pe.mark()
    c.dve.wait(scored)
    c.dve.reduce(least, split(b0[:, :], NT), ALU.max, negate=True)
    c.dve.wait(c.dve.mark())
    c.dve.ts(least, least, scale, None, ALU.mult)
    shift_done = c.dve.mark()
    c.act.wait(shift_done)
    for t in range(NT):
        c.act.act(e[:, t * N:(t + 1) * N], b0[:, t * N:(t + 1) * N], ACT.Exp, bias=least[:, t:t + 1], scale=scale,
                  total=total[:, t:t + 1])
    s.free[0] = c.act.mark()
    c.dve.wait(s.free[0])
    c.dve.recip(over, total)
    over_done = c.dve.mark()
    c.pool.wait(over_done)
    c.pool.tt(split(e, NT), split(e, NT), stretch(over, N), ALU.mult)
    normalised = c.pool.mark()
    c.pe.wait(normalised, s.free[1])
    for m in range(NT):
        for t in range(NT):
            c.pe.turn(b1[:, m * N + t * P:m * N + (t + 1) * P], e[:, t * N + m * P:t * N + (m + 1) * P], c.shared.ident)
    turned = c.pe.mark()
    c.act.wait(turned)
    c.act.act(pT, b1[:, :], ACT.Copy)
    s.free[1] = c.act.mark()
    c.pe.wait(s.free[1], v_ready, s.free[0])
    for m in range(NT):
        c.pe.mm(b0[:, 0:N], v[:, m, :], pT[:, m * N:(m + 1) * N], start=(m == 0), stop=(m == NT - 1))
    return c.pe.mark()


def values(c, s, out, src, w, ready):
    c.pe.wait(ready, s.weights, s.free[1])
    for t in range(NT):
        c.pe.mm(s.bank[1][:, t * P:(t + 1) * P], src[:, t * P:(t + 1) * P], w)
    made = c.pe.mark()
    c.dve.wait(made)
    c.dve.copy(out, split(s.bank[1][:, 0:N], NT))
    s.free[1] = c.dve.mark()
    return s.free[1]


def cross_attention_1(c, s):
    W = s.W
    normed = layernorm(c, s, s.x[:, :], s.ready, EPS, s.xn[:, :])
    qT, kT = s.kT[:, 0:N], s.kT[:, N:2 * N]
    v = split(s.kT[:, 2 * N:3 * N], NT)
    found = (s.v[:, 0:N], s.v[:, N:2 * N])
    for i, (src_q, src_kv, wq, wk, wv) in enumerate((
            (s.xn[:, :], s.ctx[:, :], "q_c", "k_s", "v_s"), (s.ctx[:, :], s.xn[:, :], "q_s", "k_c", "v_c"))):
        ready = normed if i == 0 else found_ready
        q_ready = project(c, s, qT, W("W" + wq), src_q, ready, W("b" + wq), 0, 0)
        k_ready = project(c, s, kT, W("W" + wk), src_kv, ready, W("b" + wk), 0, 1)
        v_ready = values(c, s, v, src_kv, W("W" + wv), ready)
        o_done = attention(c, s, qT, kT, v, k_ready, v_ready, D ** -0.5)
        c.act.wait(o_done)
        c.act.act(found[i], s.bank[0][:, 0:N], ACT.Identity, bias=W("b" + wv))
        s.free[0] = found_ready = c.act.mark()
    half_bias, gate, diff = s.sm[:, 170:171], s.w[:, 0:N], s.w[:, N:2 * N]
    c.pe.wait(found_ready, s.free[0])
    c.pe.mm(s.bank[0][:, 0:N], W("Wg_a"), found[0], start=True, stop=False)
    c.pe.mm(s.bank[0][:, 0:N], W("Wg_b"), found[1], start=False, stop=True)
    z_done = c.pe.mark()
    c.dve.wait(found_ready, s.weights)
    c.dve.ts(half_bias, W("bg"), 0.5, None, ALU.mult)
    c.dve.tt(diff, found[0], found[1], ALU.subtract)
    diff_done = c.dve.mark()
    c.act.wait(z_done, diff_done)
    c.act.act(gate, s.bank[0][:, 0:N], ACT.Tanh, bias=half_bias, scale=0.5)
    s.free[0] = c.act.mark()
    c.dve.wait(s.free[0])
    c.dve.ts(gate, gate, 0.5, 0.5, ALU.mult, ALU.add)
    c.dve.wait(c.dve.mark(), diff_done)
    c.dve.tt(diff, diff, gate, ALU.mult)
    c.dve.wait(c.dve.mark())
    c.dve.tt(diff, diff, found[1], ALU.add)
    c.dve.wait(c.dve.mark(), c.shared.gates_ready)
    c.dve.stt(s.x[:, :], diff, c.shared.gates[:, 1:2], s.x[:, :], ALU.mult, ALU.add)
    s.ready = c.dve.mark()


def mixture_1(c, s):
    W = s.W
    b0, b1 = s.bank
    normed = layernorm(c, s, s.x[:, :], s.ready, EPS, s.xn[:, :])
    n = NT * E1
    tiles = [s.sm[:, 192 + n * i:192 + n * (i + 1)] for i in range(10)]
    z, work, ordered, square, mean, meansq, tau, a, ones, pick = tiles
    stat, factor = s.sm[:, 172:172 + NT], s.sm[:, 174:174 + NT]
    c.pe.wait(normed, s.weights, s.free[0])
    for t in range(NT):
        c.pe.mm(b0[:, t * E1:(t + 1) * E1], s.xn[:, t * P:(t + 1) * P], W("proj"))
    made = c.pe.mark()

    def then():
        c.dve.wait(c.dve.mark())

    v = c.dve
    v.wait(made)
    v.copy(z, b0[:, 0:n])
    s.free[0] = c.dve.mark()
    v.wait(s.free[0])
    v.reduce(stat, split(z, NT), ALU.add)
    then()
    v.ts(stat, stat, 1.0 / E1, None, ALU.mult)
    then()
    v.tt(split(z, NT), split(z, NT), stretch(stat, E1), ALU.subtract)
    then()
    v.tt(square, z, z, ALU.mult)
    then()
    v.reduce(stat, split(square, NT), ALU.add)
    then()
    v.ts(stat, stat, 1.0 / E1, EPS, ALU.mult, ALU.add)
    var_done = c.dve.mark()
    c.pool.wait(var_done, c.shared.powers_ready)
    c.pool.power(factor, stat, c.shared.minus_half[:, 0:NT])
    factor_done = c.pool.mark()
    v.wait(factor_done)
    v.tt(split(z, NT), split(z, NT), stretch(factor, E1), ALU.mult)
    then()
    v.reduce(stat, split(z, NT), ALU.max)
    then()
    v.tt(split(z, NT), split(z, NT), stretch(stat, E1), ALU.subtract)
    then()
    v.ts(z, z, 0.5, None, ALU.mult)
    v.fill(ones, 1.0)
    then()
    for t in range(NT):
        v.top8(ordered[:, t * E1:t * E1 + 8], z[:, t * E1:(t + 1) * E1])
    then()
    for t in range(NT):
        v.drop(work[:, t * E1:(t + 1) * E1], ordered[:, t * E1:t * E1 + 8], z[:, t * E1:(t + 1) * E1])
    then()
    for t in range(NT):
        v.top8(ordered[:, t * E1 + 8:(t + 1) * E1], work[:, t * E1:(t + 1) * E1])
    then()
    v.tt(square, ordered, ordered, ALU.mult)
    then()
    for t in range(NT):
        cols = slice(t * E1, (t + 1) * E1)
        v.scan(mean[:, cols], ones[:, cols], ordered[:, cols])
        v.scan(meansq[:, cols], ones[:, cols], square[:, cols])
    then()
    v.tt(split(mean, NT), split(mean, NT), repeat(c.shared.invk, NT), ALU.mult)
    v.tt(split(meansq, NT), split(meansq, NT), repeat(c.shared.invk, NT), ALU.mult)
    then()
    v.tt(tau, mean, mean, ALU.mult)
    then()
    v.tt(tau, meansq, tau, ALU.subtract)
    then()
    v.tt(split(tau, NT), split(tau, NT), repeat(c.shared.k, NT), ALU.mult)
    then()
    v.ts(tau, tau, -1.0, 1.0, ALU.mult, ALU.add)
    then()
    v.tt(split(tau, NT), split(tau, NT), repeat(c.shared.invk, NT), ALU.mult)
    then()
    v.ts(tau, tau, 0.0, None, ALU.max)
    delta_done = c.dve.mark()
    c.pool.wait(delta_done)
    c.pool.power(a, tau, c.shared.half[:, 0:n])
    root_done = c.pool.mark()
    v.wait(root_done)
    v.tt(tau, mean, a, ALU.subtract)
    then()
    v.tt(work, tau, ordered, ALU.is_le)
    then()
    v.reduce(stat, split(work, NT), ALU.add)
    then()
    v.tt(split(pick, NT), repeat(c.shared.k, NT), stretch(stat, E1), ALU.is_equal)
    then()
    v.tt(pick, pick, tau, ALU.mult)
    then()
    v.reduce(stat, split(pick, NT), ALU.add)
    then()
    v.tt(split(a, NT), split(z, NT), stretch(stat, E1), ALU.subtract)
    then()
    v.ts(a, a, 0.0, None, ALU.max)
    then()
    v.tt(a, a, a, ALU.mult)
    a_done = c.dve.mark()
    c.pe.wait(a_done, s.free[0])
    for t in range(NT):
        c.pe.turn(b0[0:E1, t * P:(t + 1) * P], a[:, t * E1:(t + 1) * E1], c.shared.ident)
    turned = c.pe.mark()
    aT, g = s.w[0:E1, 0:N], s.w[0:R1, BANK:2 * BANK]
    z1, z2 = s.w[0:R1, 2 * BANK:2 * BANK + N], s.w[0:R1, 2 * BANK + N:3 * BANK]
    hT = split(s.v[:, :], O1 // P)
    c.act.wait(turned)
    c.act.act(aT, b0[0:E1, 0:N], ACT.Copy)
    aT_done = c.act.mark()
    c.pe.wait(aT_done, s.free[1])
    c.pe.mm(b0[0:R1, 0:N], W("C1")[0:E1, :], aT)
    c.pe.mm(b0[0:R1, N:2 * N], W("C2")[0:E1, :], aT)
    c.pe.mm(b1[0:R1, 0:N], W("Win1"), s.xn[:, :])
    made = c.pe.mark()
    c.act.wait(made)
    c.act.act(g, b0[0:R1, :], ACT.Copy)
    g_done = c.act.mark()
    c.dve.wait(g_done)
    c.dve.stt(z1, b1[0:R1, 0:N], W("bin1")[0:R1, :], g[:, 0:N], ALU.add, ALU.mult)
    z1_done = c.dve.mark()
    c.pe.wait(z1_done)
    made = []
    for j in range(2):
        for i in range(2):
            o = 2 * j + i
            c.pe.mm(s.bank[j][:, i * N:(i + 1) * N], W("Wout1")[0:R1, o * P:(o + 1) * P], z1)
        made.append(c.pe.mark())
    for j in range(2):
        c.act.wait(made[j])
        c.act.act(s.v[:, j * BANK:(j + 1) * BANK], s.bank[j][:, :], ACT.Gelu)
    gelu_done = c.act.mark()
    c.pe.wait(gelu_done)
    for o in range(O1 // P):
        c.pe.mm(b0[0:R1, 0:N], W("Win2")[:, o * R1:(o + 1) * R1], hT[:, o, :], start=(o == 0), stop=(o == O1 // P - 1))
    made = c.pe.mark()
    c.dve.wait(made)
    c.dve.stt(z2, b0[0:R1, 0:N], W("bin2")[0:R1, :], g[:, N:2 * N], ALU.add, ALU.mult)
    s.free[0] = c.dve.mark()
    c.pe.wait(s.free[0])
    c.pe.mm(b1[:, 0:N], W("Wout2")[0:R1, :], z2)
    made = c.pe.mark()
    c.dve.wait(made, c.shared.gates_ready)
    c.dve.stt(s.x[:, :], b1[:, 0:N], c.shared.gates[:, B + 1:B + 2], s.x[:, :], ALU.mult, ALU.add)
    s.free[1] = s.ready = c.dve.mark()


def cross_attention_2(c, s):
    W = s.W
    normed = layernorm(c, s, s.x[:, :], s.ready, EPS, s.xn[:, :])
    qT, kT = s.kT[:, 0:N], s.kT[:, N:2 * N]
    v = split(s.kT[:, 2 * N:3 * N], NT)
    res, out = s.v[:, 0:N], s.v[:, N:2 * N]
    project(c, s, qT, W("Wq"), s.xn[:, :], normed, W("bq"), 0, 0)
    k_ready = project(c, s, kT, W("Wk"), s.ctx[:, :], normed, W("bk"), 0, 1)
    v_ready = values(c, s, v, s.ctx[:, :], W("Wv"), normed)
    o_done = attention(c, s, qT, kT, v, k_ready, v_ready, D ** -0.5)
    c.dve.wait(o_done)
    c.dve.stt(res, s.bank[0][:, 0:N], W("bv"), s.ctx[:, :], ALU.add, ALU.add)
    s.free[0] = c.dve.mark()
    out_ready = layernorm(c, s, res, s.free[0], EPS_L2, out)
    c.dve.wait(out_ready)
    c.dve.ts(out, out, W("gamma"), W("beta"), ALU.mult, ALU.add)
    c.dve.wait(c.dve.mark())
    c.dve.stt(s.x[:, :], out, c.shared.gates[:, 2:3], s.x[:, :], ALU.mult, ALU.add)
    s.ready = c.dve.mark()


def top_two(c, s, biased, keep):
    n = NT * E2
    a, b = s.w[:, 0:n * E2], s.w[:, n * E2:2 * n * E2]
    a4, b4 = (x.rearrange("p (t i j) -> p t i j", t=NT, i=E2) for x in (a, b))
    other = split(biased, NT).unsqueeze(2).to_broadcast([P, NT, E2, E2])
    mine = split(biased, NT).unsqueeze(3).to_broadcast([P, NT, E2, E2])
    tri = split(c.shared.tri, E2).unsqueeze(1).to_broadcast([P, NT, E2, E2])
    c.dve.tt(a4, other, mine, ALU.is_gt)
    c.dve.tt(b4, other, mine, ALU.is_equal)
    c.dve.wait(c.dve.mark())
    c.dve.tt(b4, b4, tri, ALU.mult)
    c.dve.wait(c.dve.mark())
    c.dve.tt(a, a, b, ALU.add)
    c.dve.wait(c.dve.mark())
    c.dve.reduce(keep, split(a, n), ALU.add)
    c.dve.wait(c.dve.mark())
    c.dve.ts(keep, keep, K2 - 0.5, None, ALU.is_lt)
    return c.dve.mark()


def mixture_2(c, s):
    W = s.W
    b0, y = s.bank[0], s.bank[1][:, 0:N]
    n = NT * E2
    normed = layernorm(c, s, s.x[:, :], s.ready, EPS, s.xn[:, :])
    score, biased, keep = (s.sm[:, 192 + n * i:192 + n * (i + 1)] for i in range(3))
    least, total, over = (s.sm[:, 176 + NT * i:176 + NT * (i + 1)] for i in range(3))
    c.pe.wait(normed, s.weights, s.free[0])
    for t in range(NT):
        c.pe.mm(b0[:, t * E2:(t + 1) * E2], s.xn[:, t * P:(t + 1) * P], W("gate_w"))
    made = c.pe.mark()
    c.dve.wait(made)
    c.dve.reduce(least, split(b0[:, 0:n], NT), ALU.max, negate=True)
    shift_done = c.dve.mark()
    c.act.wait(shift_done)
    for t in range(NT):
        c.act.act(score[:, t * E2:(t + 1) * E2], b0[:, t * E2:(t + 1) * E2], ACT.Exp, bias=least[:, t:t + 1],
                  total=total[:, t:t + 1])
    s.free[0] = c.act.mark()
    c.dve.wait(s.free[0])
    c.dve.recip(over, total)
    c.dve.wait(c.dve.mark(), s.weights)
    c.dve.tt(split(score, NT), split(score, NT), stretch(over, E2), ALU.mult)
    c.dve.wait(c.dve.mark())
    c.dve.tt(split(biased, NT), split(score, NT), repeat(W("gate_b"), NT), ALU.add)
    c.dve.wait(c.dve.mark())
    keep_done = top_two(c, s, biased, keep)
    c.dve.wait(keep_done)
    c.dve.tt(keep, keep, score, ALU.mult)
    gate_done = c.dve.mark()
    gT = s.w[:, 2 * BANK:2 * BANK + N]
    c.pool.fill(gT, 0.0)
    zeroed = c.pool.mark()
    c.pe.wait(gate_done)
    for t in range(NT):
        c.pe.turn(b0[0:E2, t * P:(t + 1) * P], keep[:, t * E2:(t + 1) * E2], c.shared.ident)
    turned = c.pe.mark()
    c.act.wait(turned, zeroed)
    c.act.act(gT[0:E2, :], b0[0:E2, 0:N], ACT.Copy)
    gT_done = c.act.mark()
    c.pe.wait(gT_done)
    spread = []
    for j in range(E2 // 2):
        bank, dst = s.bank[j % 2], (s.kT if j < 2 else s.oT)[:, (j % 2) * BANK:(j % 2 + 1) * BANK]
        c.pe.wait(s.free[j % 2])
        for i in range(2):
            e = 2 * j + i
            c.pe.mm(bank[:, i * N:(i + 1) * N], c.shared.ident[:, e:e + 1].to_broadcast([P, P]), gT)
        made = c.pe.mark()
        if j % 2:
            c.dve.wait(made)
            c.dve.copy(dst, bank[:, :])
            s.free[1] = c.dve.mark()
        else:
            c.act.wait(made)
            c.act.act(dst, bank[:, :], ACT.Copy)
            s.free[0] = c.act.mark()
        spread.append(s.free[j % 2])
    c.pe.wait(s.free[1])
    c.pe.mm(y, W("b2")[0:E2, :], gT[0:E2, :], start=True, stop=False)
    w1, w3 = split(W("w1"), 2 * (E2 + 1)), split(W("w3"), 2 * (E2 + 1))
    w2 = split(W("w2"), 2 * (E2 + 1))
    b1, b3 = W("b1"), W("b3")
    turns = 2 * (E2 + 1)
    gated, used = [None] * turns, None
    for i in range(turns + 1):
        if i < turns:
            k = i % 2
            t3, prod, silu = (s.w[0:HH2, (3 * k + m) * N:(3 * k + m + 1) * N] for m in range(3))
            if k:
                t3, prod, silu = (s.w[0:HH2, 3 * BANK + m * N:3 * BANK + (m + 1) * N] for m in range(3))
            c.pe.wait(s.free[0], normed)
            c.pe.mm(b0[0:HH2, 0:N], w1[:, i, :], s.xn[:, :])
            c.pe.mm(b0[0:HH2, N:2 * N], w3[:, i, :], s.xn[:, :])
            made = c.pe.mark()
            c.act.wait(made, *([gated[i - 2]] if i >= 2 else []))
            c.act.act(t3, b0[0:HH2, N:2 * N], ACT.Identity, bias=b3[0:HH2, i:i + 1])
            t3_done = c.act.mark()
            c.dve.wait(t3_done)
            c.dve.stt(prod, b0[0:HH2, 0:N], b1[0:HH2, i:i + 1], t3, ALU.add, ALU.mult)
            s.free[0] = c.dve.mark()
            c.act.wait(s.free[0], *([used] if used else []))
            c.act.act(silu, prod, ACT.Silu)
            gated[i] = c.act.mark()
            e = i // 2
            if e < E2:
                rows = (s.kT if e < 4 else s.oT)[0:HH2, (e % 4) * N:(e % 4 + 1) * N]
                c.pool.wait(gated[i], *spread)
                c.pool.settle()
                c.pool.tt(silu, silu, rows, ALU.mult)
                gated[i] = c.pool.mark()
            hidden_i = silu
        if i:
            c.pe.wait(gated[i - 1])
            c.pe.mm(y, w2[0:HH2, i - 1, :], hidden_before, start=False, stop=(i == turns))
            used = c.pe.mark()
        hidden_before = hidden_i
    update_stream(c, s, y, used, W("sb2"), B + 2, bank=1)


def cross_attention_3(c, s):
    W = s.W
    b0, b1 = s.bank
    normed = layernorm(c, s, s.x[:, :], s.ready, EPS, s.xn[:, :])
    qT, kT = s.kT[:, 0:N], s.kT[:, N:2 * N]
    v = split(s.kT[:, 2 * N:3 * N], NT)
    scale = DH3 ** -0.5
    project(c, s, qT, W("Wq"), s.xn[:, :], normed, W("bq"), 0, 0)
    k_ready = project(c, s, kT, W("Wk"), s.ctx[:, :], normed, W("bk"), 0, 1)
    c.pe.wait(s.free[1])
    for t in range(NT):
        c.pe.mm(b1[:, t * P:(t + 1) * P], s.ctx[:, t * P:(t + 1) * P], W("Wv"))
    made = c.pe.mark()
    c.dve.wait(made)
    c.dve.tt(v, split(b1[:, 0:N], NT), repeat(W("bv"), NT), ALU.add)
    s.free[1] = v_ready = c.dve.mark()
    vz = [s.v[:, :].rearrange("p (h d) -> p h d", h=2 * H3), s.oT[:, :].rearrange("p (h d) -> p h d", h=2 * H3)]
    vz = [x[:, 0:H3, :] for x in vz]
    c.pool.wait(normed)
    for t in range(NT):
        c.pool.fill(vz[t], 0.0)
    zeroed = c.pool.mark()
    used, held, done = [normed, normed], [None, None], None
    waiting = None
    for h in range(H3 + 1):
        if h < H3:
            kz, e = s.w[:, (h % 2) * N:(h % 2 + 1) * N], s.w[:, (1 + h % 2) * BANK:(2 + h % 2) * BANK]
            least, total, over = (s.sm[:, 184 + 8 * (h % 2) + NT * i:184 + 8 * (h % 2) + NT * (i + 1)] for i in range(3))
            c.pool.wait(k_ready, used[h % 2])
            c.pool.ts(kz, kT, c.shared.headmask[:, h:h + 1], None, ALU.mult)
            kz_done = c.pool.mark()
            c.pe.wait(kz_done, s.free[0])
            for m in range(NT):
                c.pe.mm(b0[:, m * N:(m + 1) * N], kz[:, m * P:(m + 1) * P], qT)
            scored = c.pe.mark()
            c.dve.wait(scored, used[h % 2])
            c.dve.reduce(least, split(b0[:, :], NT), ALU.max, negate=True)
            c.dve.wait(c.dve.mark())
            c.dve.ts(least, least, scale, None, ALU.mult)
            shift_done = c.dve.mark()
            c.act.wait(shift_done, used[h % 2])
            for m in range(NT):
                c.act.act(e[:, m * N:(m + 1) * N], b0[:, m * N:(m + 1) * N], ACT.Exp, bias=least[:, m:m + 1],
                          scale=scale, total=total[:, m:m + 1])
            s.free[0] = c.act.mark()
            c.dve.wait(s.free[0], zeroed, v_ready)
            c.dve.recip(over, total)
            c.dve.wait(c.dve.mark())
            for m in range(NT):
                c.dve.ts(vz[m][:, h, (h % 4) * DH3:(h % 4 + 1) * DH3], v[:, m, h * DH3:(h + 1) * DH3],
                         over[:, m:m + 1], None, ALU.mult)
            now = (h, e, c.dve.mark())
        if waiting:
            g, e_g, ready = waiting
            rows = slice(32 * (g // 4), 32 * (g // 4) + 32)
            c.pe.wait(ready, s.free[1])
            for m in range(NT):
                c.pe.mm(b1[rows, 0:N], vz[m][:, g, :], e_g[:, m * N:(m + 1) * N], start=(g % 4 == 0 and m == 0),
                        stop=(g % 4 == 3 and m == NT - 1))
            used[g % 2] = done = c.pe.mark()
        waiting = now
    oT = s.w[:, 3 * BANK:3 * BANK + N]
    c.act.wait(done)
    c.act.act(oT, b1[:, 0:N], ACT.Copy)
    s.free[1] = o_kept = c.act.mark()
    c.pe.wait(o_kept, s.free[0])
    c.pe.mm(b0[:, 0:N], W("Wo"), oT)
    y_done = c.pe.mark()
    update_stream(c, s, b0[:, 0:N], y_done, W("bo"), 3)


def mixture_3(c, s):
    W = s.W
    b0, b1 = s.bank
    n = NT * E3
    normed = layernorm(c, s, s.x[:, :], s.ready, EPS, s.xn[:, :])
    logit, keep, gate = (s.sm[:, 192 + n * i:192 + n * (i + 1)] for i in range(3))
    stat, total, over = (s.sm[:, 176 + NT * i:176 + NT * (i + 1)] for i in range(3))
    c.pe.wait(normed, s.weights, s.free[0])
    for t in range(NT):
        c.pe.mm(b0[:, t * E3:(t + 1) * E3], s.xn[:, t * P:(t + 1) * P], W("gate_w"))
    made = c.pe.mark()
    c.dve.wait(made)
    c.dve.tt(split(logit, NT), split(b0[:, 0:n], NT), repeat(W("gate_b"), NT), ALU.add)
    s.free[0] = c.dve.mark()
    c.dve.wait(s.free[0])
    keep_done = top_two(c, s, logit, keep)
    c.dve.reduce(stat, split(logit, NT), ALU.max)
    c.dve.wait(c.dve.mark(), keep_done)
    c.dve.tt(split(logit, NT), split(logit, NT), stretch(stat, E3), ALU.subtract)
    shifted_done = c.dve.mark()
    c.act.wait(shifted_done)
    c.act.act(gate, logit, ACT.Exp)
    exp_done = c.act.mark()
    c.dve.wait(exp_done)
    c.dve.tt(gate, gate, keep, ALU.mult)
    c.dve.wait(c.dve.mark())
    c.dve.reduce(total, split(gate, NT), ALU.add)
    c.dve.wait(c.dve.mark())
    c.dve.recip(over, total)
    c.dve.wait(c.dve.mark())
    c.dve.tt(split(gate, NT), split(gate, NT), stretch(over, E3), ALU.mult)
    gate_done = c.dve.mark()
    c.pe.wait(gate_done, s.free[0])
    for t in range(NT):
        c.pe.turn(b0[0:E3, t * P:(t + 1) * P], gate[:, t * E3:(t + 1) * E3], c.shared.ident)
    turned = c.pe.mark()
    gT = s.w[0:E3, BANK:BANK + N]
    c.act.wait(turned)
    c.act.act(gT, b0[0:E3, 0:N], ACT.Copy)
    s.free[0] = gT_done = c.act.mark()
    for t in range(NT):
        acc = s.w[:, t * P:(t + 1) * P]
        added = gate_done
        for j in range(2):
            c.pe.wait(normed, s.free[j])
            c.pe.mm(s.bank[j][:, :], s.xn[:, t * P:(t + 1) * P], W("expert_w")[:, j * BANK:(j + 1) * BANK])
            made = c.pe.mark()
            for i in range(4):
                e = 4 * j + i
                src, factor = s.bank[j][:, i * P:(i + 1) * P], gate[:, t * E3 + e:t * E3 + e + 1]
                c.dve.wait(made, added)
                if e == 0:
                    c.dve.ts(acc, src, factor, None, ALU.mult)
                else:
                    c.dve.stt(acc, src, factor, acc, ALU.mult, ALU.add)
                added = c.dve.mark()
            s.free[j] = added
        c.pe.wait(gT_done, *s.free)
        c.pe.mm(b0[:, 0:P], gT[:, t * P:(t + 1) * P], W("expert_b")[0:E3, :])
        c.pe.turn(b1[:, 0:P], s.x[:, t * P:(t + 1) * P], c.shared.ident)
        made = c.pe.mark()
        c.dve.wait(made, added)
        c.dve.tt(acc, acc, b0[:, 0:P], ALU.add)
        s.free[0] = c.dve.mark()
        res = s.w[:, 3 * P + BANK + t * P:4 * P + BANK + t * P]
        c.dve.wait(s.free[0])
        c.dve.stt(res, acc, c.shared.gates[:, B + 3:B + 4], b1[:, 0:P], ALU.mult, ALU.add)
        s.free[1] = s.ready = c.dve.mark()
        c.sync.wait(s.ready)
        dst, sem = c.shared.out[s.b, t * P:(t + 1) * P, :], c.shared.s_out
        c.sync.put(lambda e, dst=dst, res=res: e.dma_start(dst, res).then_inc(sem, 16))


def build(nc, x_in, ctx_in, gates_in, const_in, packs_in, out):
    with ExitStack() as stack:
        def sb(name, cols):
            return stack.enter_context(nc.sbuf_tensor(name, [P, cols], F32))

        def sem(name):
            return stack.enter_context(nc.semaphore(name))

        h = Shared()
        setup = Program(h)
        s_const, s_out = sem("const_loaded"), sem("out_stored")
        s_slot = [sem("slot0_loaded"), sem("slot1_loaded")]
        const = sb("constants", CONST.n)
        h.gates = sb("gate_columns", 2 * B)
        slots = [sb("slot0", SLOT), sb("slot1", SLOT)]
        h.tables = [sb("rotary0", 4 * NT * DH), sb("rotary1", 4 * NT * DH)]
        powers = sb("powers", 64)
        h.ident, h.mean, h.ones, h.band, h.tri, h.k, h.invk, h.headmask = (
            CONST(const, n) for n in ("ident", "mean", "ones", "band", "tri", "k", "invk", "headmask"))
        rotary = [CONST(const, n) for n in ("qcos", "qsin", "kcos", "ksin")]
        h.minus_half, h.half = powers[:, 0:32], powers[:, 32:64]
        h.out, h.s_out = out, s_out

        seqs = []
        for b in range(B):
            s = Sequence()
            s.b = b
            s.x, s.ctx, s.xn, s.z, s.zs = (sb(f"{n}{b}", N) for n in ("x", "ctx", "xn", "z", "zs"))
            s.kT, s.v, s.oT = (sb(f"{n}{b}", 4 * N) for n in ("kT", "v", "oT"))
            s.qz = sb(f"qz{b}", 2 * BANK)
            s.w = sb(f"work{b}", 6 * BANK)
            s.sm = sb(f"small{b}", 512)
            s.before = sb(f"window_before{b}", 8 * WINDOW)
            s.bank = [stack.enter_context(nc.psum_tensor(f"bank{b}_{i}", [P, BANK], F32)) for i in range(2)]
            s_x = sem(f"x{b}_loaded")
            cols = slice(b * N, (b + 1) * N)
            setup.sync.put(lambda e, s=s, cols=cols, s_x=s_x: e.dma_start(s.x[:, :], x_in[:, cols]).then_inc(s_x, 16))
            s.x_ready = setup.sync.load(lambda e, s=s, cols=cols: e.dma_start(s.ctx[:, :], ctx_in[:, cols]), s_x, 32, 2500.0)
            if b == 0:
                setup.sync.put(lambda e: e.dma_start(const[:, :], const_in).then_inc(s_const, 16))
                h.const_ready = setup.sync.load(lambda e: e.dma_start(h.gates[:, :], gates_in), s_const, 32, 3000.0)
            setup.pool.fill(s.qz[:, :], 0.0)
            setup.pool.fill(s.before[:, :], 0.0)
            s.qz_zero = setup.pool.mark()
            seqs.append(s)
        setup.dve.fill(h.minus_half, -0.5)
        setup.dve.fill(h.half, 0.5)
        h.powers_ready = setup.dve.mark()
        setup.act.wait(h.const_ready)
        setup.act.act(h.gates[:, :], h.gates[:, :], ACT.Tanh)
        h.gates_ready = setup.act.mark()

        weights, done, loader = [], [[] for _ in STAGES], Program(h)
        for stage, pack in enumerate(STAGES):
            if stage >= 2:
                loader.sync.wait()
                loader.sync.steps[-1][0] = done[stage - 2]
            dst, src = slots[stage % 2][:, 0:pack.n], packs_in[stage]
            weights.append(loader.sync.load(lambda e, dst=dst, src=src: e.dma_start(dst, src), s_slot[stage % 2],
                                            16 * (stage // 2 + 1), 15000.0 if stage < 2 else 0.0))

        mask = L0X(slots[0], "mask")
        setup.pool.wait(weights[0])
        setup.pool.ts(mask, mask, -1.0, 1.0, ALU.mult, ALU.add)
        setup.pool.wait(setup.pool.mark())
        setup.pool.ts(mask, mask, -1e10, None, ALU.mult)
        h.mask_ready = setup.pool.mark()

        def rotary_tables(c, stage):
            sc = split(L0F(slots[stage % 2], "scales"), 4)
            tab = h.tables[stage % 2][:, :].rearrange("p (a t d) -> p a t d", a=4, t=NT)
            c.pool.wait(h.const_ready, weights[stage])
            for a, base in enumerate(rotary):
                for t in range(NT):
                    c.pool.tt(tab[:, a, t, :], split(base, NT)[:, t, :], sc[:, a, :], ALU.mult)
            return c.pool.mark()

        table_ready, programs = {}, []
        for s in seqs:
            c = Program(h)
            s.ready, s.free = s.x_ready, [h.powers_ready, h.powers_ready]
            for stage, pack in enumerate(STAGES):
                s.W = lambda name, pack=pack, stage=stage: pack(slots[stage % 2], name)
                s.weights = weights[stage]
                if stage == 0:
                    cross_attention_0(c, s)
                elif stage <= DEPTH:
                    if s.b == 0:
                        table_ready[stage] = rotary_tables(c, stage)
                    s.table_ready = table_ready[stage]
                    local_layer(c, s, stage)
                elif pack is MIX1:
                    cross_attention_1(c, s)
                    mixture_1(c, s)
                    cross_attention_2(c, s)
                elif pack is L2F:
                    mixture_2(c, s)
                else:
                    cross_attention_3(c, s)
                    mixture_3(c, s)
                done[stage].append(s.ready)
            programs.append(c.streams)

        engines = [Engine(sem(n)) for n in ("pe_steps", "act_steps", "dve_steps", "pool_steps", "sync_steps")]
        in_order_of_issue(engines, [setup.streams, loader.streams] + programs)

        block = stack.enter_context(nc.Block())

        @block.tensor
        def _(e):
            engines[0].play(e)

        @block.scalar
        def _(e):
            engines[1].play(e)

        @block.vector
        def _(e):
            engines[2].play(e)

        @block.gpsimd
        def _(e):
            engines[3].play(e)

        @block.sync
        def _(e):
            engines[4].play(e)
            e.wait_ge(s_out, B * NT * 16)


def constants():
    f = np.float32
    c = {"ident": np.eye(P, dtype=f), "mean": np.full((P, P), 1.0 / P, f), "ones": np.ones((P, P), f)}
    half = np.arange(0, DH, 2, dtype=f)
    freqs = np.arange(N, dtype=f)[:, None] * (f(1.0) / np.power(f(10000.0), half / f(DH)))[None, :]
    base = (half + f(0.4 * DH)) / f(1.4 * DH)
    power = (np.arange(N, dtype=f) - f(N // 2)) / f(WINDOW // 2)
    scale = np.power(base[None, :], power[:, None]).astype(f)
    cos, sin = np.cos(freqs), np.sin(freqs)
    for name, s in (("q", scale * f(QK_SCALE)), ("k", f(1.0) / scale)):
        for part, table in (("cos", np.concatenate([cos * s, cos * s], 1)),
                            ("sin", np.concatenate([-sin * s, sin * s], 1))):
            c[name + part] = table.reshape(NT, P, DH).transpose(1, 0, 2).reshape(P, NT * DH)
    q, k = np.arange(P)[:, None], np.arange(P)[None, :]
    band = np.where((k <= q) & (k >= q - WINDOW), 0.0, MASKED).astype(f)
    second = band.copy()
    before = (q < WINDOW) & (k >= P - WINDOW) & (k - P >= q - WINDOW)
    second[before] = 0.0
    c["band"] = np.concatenate([band, second], 1)
    c["tri"] = np.broadcast_to((np.arange(E2)[None, :] < np.arange(E2)[:, None]).astype(f).reshape(1, -1), (P, E2 * E2))
    ks = np.arange(1, E1 + 1, dtype=f)
    c["k"], c["invk"] = np.broadcast_to(ks, (P, E1)), np.broadcast_to(f(1.0) / ks, (P, E1))
    c["headmask"] = (np.arange(P)[:, None] // DH3 == np.arange(H3)[None, :]).astype(f)
    return c


def packed(columns, arrays):
    out = np.zeros((P, columns.n), np.float32)
    for name, (start, width) in columns.at.items():
        a = arrays[name]
        a = a.reshape(a.shape[0], -1)
        assert a.shape[1] == width, (name, a.shape, width)
        out[:a.shape[0], start:start + width] = a
    return out


def chunked(a, rows=P):
    n = -(-a.shape[0] // rows)
    full = np.zeros((n * rows,) + a.shape[1:], a.dtype)
    full[:a.shape[0]] = a
    return full.reshape(n, rows, -1).transpose(1, 0, 2).reshape(rows, -1)


def column(a):
    return chunked(a.reshape(-1, 1))


def row(a):
    return np.broadcast_to(a.reshape(1, -1), (P, a.size))


def layouts(i):
    heads = lambda w: w.transpose(1, 0, 2).reshape(D, INNER)
    packs = [packed(L0X, {
        "Wq": heads(i["L0_xattn_Wq"]), "Wk": heads(i["L0_xattn_Wk"]), "Wv": heads(i["L0_xattn_Wv"]),
        "Wo": chunked(i["L0_xattn_Wo"].reshape(DH, H0, D).transpose(1, 0, 2).reshape(INNER, D)),
        "mask": chunked(i["mask_SxS2_ff1"]), "bq": column(i["L0_xattn_bq"]), "bk": column(i["L0_xattn_bk"]),
        "bv": column(i["L0_xattn_bv"]), "bo": column(i["L0_xattn_bo"])})]
    for d in range(DEPTH):
        qs, ks = i["L0_ffn_q_scale"][d], i["L0_ffn_k_scale"][d]
        swap = lambda a: np.concatenate([a[DH // 2:], a[:DH // 2]])
        b1 = i["L0_ffn_b1"][d]
        packs.append(packed(L0F, {
            "Wqkv": i["L0_ffn_Wqkv"][d], "Wo": chunked(i["L0_ffn_Wo"][d]), "W1": i["L0_ffn_W1"][d],
            "W2": chunked(i["L0_ffn_W2"][d]), "scales": row(np.concatenate([qs, swap(qs), ks, swap(ks)])),
            "ln_g": column(i["L0_ffn_ln_g"][d]), "ln_b": column(i["L0_ffn_ln_b"][d]),
            "b1": np.concatenate([column(b1[:FF]), column(b1[FF:])], 1), "b2": column(i["L0_ffn_b2"][d])}))
    one = {}
    for n in ("q_c", "k_s", "v_s", "q_s", "k_c", "v_c"):
        one["W" + n], one["b" + n] = i[f"L1_xattn_W{n}"].T, column(i[f"L1_xattn_b{n}"])
    wg = i["L1_xattn_Wg"].T
    one.update({
        "Wg_a": wg[:D], "Wg_b": wg[D:], "bg": column(i["L1_xattn_bg"]), "proj": i["L1_ffn_proj"],
        "C1": i["L1_ffn_C1"], "C2": i["L1_ffn_C2"], "Win1": i["L1_ffn_Win1"][:D], "bin1": i["L1_ffn_Win1"][D:].T,
        "Wout1": i["L1_ffn_Wout1"].T, "Win2": chunked(i["L1_ffn_Win2"][:O1]), "bin2": i["L1_ffn_Win2"][O1:].T,
        "Wout2": i["L1_ffn_Wout2"].T, "gamma": column(i["L2_xattn_gamma"]), "beta": column(i["L2_xattn_beta"])})
    for n in "qkv":
        one["W" + n], one["b" + n] = i["L2_xattn_W" + n], column(i["L2_xattn_b" + n])
    packs.append(packed(MIX1, one))
    two = {}
    for n in "13":
        w = np.concatenate([i[f"L2_ffn_w{n}"], i[f"L2_ffn_sw{n}"][None]], 0)
        b = np.concatenate([i[f"L2_ffn_b{n}"], i[f"L2_ffn_sb{n}"][None]], 0)
        two["w" + n] = w.transpose(1, 0, 2)
        two["b" + n] = b.reshape(2 * (E2 + 1), HH2).T
    w2 = np.concatenate([i["L2_ffn_w2"], i["L2_ffn_sw2"][None]], 0)
    two.update({"w2": w2.reshape(2 * (E2 + 1), HH2, D).transpose(1, 0, 2), "b2": i["L2_ffn_b2"],
                "gate_w": i["L2_ffn_gate_w"].T, "gate_b": row(i["L2_ffn_gate_b"]), "sb2": column(i["L2_ffn_sb2"])})
    packs.append(packed(L2F, two))
    kv, bkv = i["L3_xattn_Wkv"], i["L3_xattn_bkv"]
    packs.append(packed(L3, {
        "Wq": i["L3_xattn_Wq"], "Wk": kv[:, :D], "Wv": kv[:, D:], "Wo": i["L3_xattn_Wo"],
        "bq": column(i["L3_xattn_bq"]), "bk": column(bkv[:D]), "bv": row(bkv[D:]), "bo": column(i["L3_xattn_bo"]),
        "gate_w": i["L3_ffn_gate_w"].T, "gate_b": row(i["L3_ffn_gate_b"]),
        "expert_w": i["L3_ffn_expert_w"].transpose(1, 0, 2), "expert_b": i["L3_ffn_expert_b"]}))
    return packs


def kernel(**inputs):
    import concourse.bacc as bacc
    from concourse.bass_utils import run_bass_kernel_spmd

    i = {name: np.asarray(a) for name, a in inputs.items()}
    arrays = {"x_t": i["x"].transpose(2, 0, 1).reshape(D, B * N),
              "ctx_t": i["ctx_1024"].transpose(2, 0, 1).reshape(D, B * N),
              "gates": np.concatenate([row(i["g_xattn"]), row(i["g_ffn"])], 1),
              "const": packed(CONST, constants())}
    for n, p in enumerate(layouts(i)):
        arrays[f"pack{n}"] = p
    arrays = {n: np.ascontiguousarray(a) for n, a in arrays.items()}
    nc = bacc.Bacc("TRN2", target_bir_lowering=False, num_devices=1)
    aps = {n: nc.dram_tensor(f"in_{n}_dram", a.shape, F32, kind="ExternalInput").ap() for n, a in arrays.items()}
    out = nc.dram_tensor("out_dram", (B, N, D), F32, kind="ExternalOutput").ap()
    build(nc, aps["x_t"], aps["ctx_t"], aps["gates"], aps["const"],
          [aps[f"pack{n}"] for n in range(len(STAGES))], out)
    r = run_bass_kernel_spmd(nc, [{f"in_{n}_dram": a for n, a in arrays.items()}], core_ids=[0])
    return r.results[0]["out_dram"]
```

```python
from contextlib import ExitStack

import numpy as np

import concourse.bass as bass
from concourse import mybir

F32 = mybir.dt.float32
ALU = mybir.AluOpType
ACT = mybir.ActivationFunctionType
AX = mybir.AxisListType

B, N, D = 4, 256, 128
P = 128
NT = N // P
BANK = 512
H0, DH = 16, 64
PAIRS = H0 * DH // P
INNER = H0 * DH
DEPTH, WINDOW = 6, 32
EARLY = DH
FF = D * 4 * 2 // 3
FFC = [(i, min(P, FF - i)) for i in range(0, FF, P)]
E1, R1, O1 = 16, 64, 512
E2, HID2, K2 = 8, 176, 2
HT2 = -(-(E2 + 1) * HID2 // P)
H3, DH3 = 16, 8
E3 = 8
QK_SCALE = 8.0
MASKED = -1e30
LOWEST = -3.0e38
HOP = 100.0
EPS, EPS_L2 = 1e-5, 1e-6


class Columns:

    def __init__(self, pieces):
        self.at, self.n = {}, 0
        for name, width in pieces:
            self.at[name] = (self.n, width)
            self.n += width

    def __call__(self, tile, name):
        start, width = self.at[name]
        return tile[:, start:start + width]


CONST = Columns([("ident", P), ("mean", P), ("ones", P), ("qcos", NT * DH), ("qsin", NT * DH),
                 ("kcos", NT * DH), ("ksin", NT * DH),
                 ("band", NT * P), ("tri", E2 * E2), ("k", E1), ("invk", E1), ("headmask", H3)])
L0X = Columns([("Wq", INNER), ("Wk", INNER), ("Wv", INNER), ("Wo", PAIRS * D), ("mask", NT * N),
               ("bq", PAIRS), ("bk", PAIRS), ("bv", PAIRS), ("bo", 1)])
L0F = Columns([("Wqkv", 3 * INNER), ("Wo", PAIRS * D), ("W1", 2 * FF), ("W2", len(FFC) * D),
               ("scales", 4 * DH), ("ln_g", 1), ("ln_b", 1), ("b1", 2 * len(FFC)), ("b2", 1)])
MIX1 = Columns([(n, D) for n in ("Wq_c", "Wk_s", "Wv_s", "Wq_s", "Wk_c", "Wv_c", "Wg_a", "Wg_b")]
               + [(n, 1) for n in ("bq_c", "bk_s", "bv_s", "bq_s", "bk_c", "bv_c", "bg")]
               + [("proj", E1), ("C1", R1), ("Win1", R1), ("Wout1", O1), ("C2", R1),
                  ("Win2", O1 // P * R1), ("Wout2", D), ("bin1", 1), ("bin2", 1)]
               + [("Wq", D), ("Wk", D), ("Wv", D), ("bq", 1), ("bk", 1), ("bv", 1),
                  ("gamma", 1), ("beta", 1)])
L2F = Columns([("w1", (E2 + 1) * HID2), ("w3", (E2 + 1) * HID2), ("w2", HT2 * D), ("pick", HT2 * P),
               ("b1", HT2), ("b3", HT2), ("b2", D), ("gate_w", E2), ("gate_b", E2)])
L3 = Columns([("Wq", D), ("Wk", D), ("Wv", D), ("Wo", D), ("bq", 1), ("bk", 1), ("bv", D),
              ("bo", 1), ("gate_w", E3), ("gate_b", E3), ("expert_w", E3 * D), ("expert_b", D)])
STAGES = [L0X] + [L0F] * DEPTH + [MIX1, L2F, L3]
SLOTS = [max(s.n for s in STAGES[i::2]) for i in range(2)]


class Mark:

    def __init__(self, sem=None, value=None):
        self.sem, self.value, self.at = sem, value, None


class Stream:

    def __init__(self):
        self.steps = []

    def wait(self, *marks):
        if self.steps and not self.steps[-1][1]:
            self.steps[-1][0] += marks
        else:
            self.steps.append([list(marks), [], None, 0.0])

    def put(self, op, ns=0.0):
        if not self.steps or self.steps[-1][2]:
            self.steps.append([[], [], None, 0.0])
        self.steps[-1][1].append(op)
        self.steps[-1][3] += ns

    def mark(self):
        self.steps[-1][2] = Mark()
        return self.steps[-1][2]

    def load(self, op, sem, value, ns):
        self.put(lambda e: op(e).then_inc(sem, 16), ns)
        self.steps[-1][2] = Mark(sem, value)
        return self.steps[-1][2]


class Engine:

    def __init__(self, sem):
        self.sem, self.count, self.ops, self.passed, self.clock = sem, 0, [], {}, 0.0

    def issue(self, step):
        marks, ops, mark, ns = step
        for m in marks:
            if self.passed.get(m.sem.name, 0) < m.value:
                self.passed[m.sem.name] = m.value
                self.ops.append((m.sem, m.value))
        ops = list(ops)
        if mark and not mark.sem:
            last, own = ops.pop(), self.sem
            ops.append(lambda e: last(e).then_inc(own, 1))
            self.count += 1
            mark.sem, mark.value = own, self.count
        self.ops += ops
        self.clock = max([self.clock] + [m.at for m in marks]) + ns
        if mark:
            mark.at = self.clock + HOP

    def play(self, engine):
        for op in self.ops:
            if isinstance(op, tuple):
                engine.wait_ge(*op)
            else:
                op(engine)


def in_order_of_issue(engines, programs):
    at = [[0] * len(engines) for _ in programs]
    while True:
        best = None
        for p, program in enumerate(programs):
            for n, stream in enumerate(program):
                if at[p][n] == len(stream.steps):
                    continue
                ready = 0.0
                for m in stream.steps[at[p][n]][0]:
                    if m.at is None:
                        break
                    ready = max(ready, m.at)
                else:
                    key = (max(ready, engines[n].clock), stream.steps[at[p][n]][3], ready)
                    if best is None or key < best[0]:
                        best = (key, p, n)
        if best is None:
            break
        _, p, n = best
        engines[n].issue(programs[p][n].steps[at[p][n]])
        at[p][n] += 1
    assert all(at[p][n] == len(s.steps) for p, program in enumerate(programs) for n, s in enumerate(program))


def columns(ap):
    return int(np.prod(ap.shape[1:]))


class Tensor(Stream):
    def mm(self, out, lhsT, rhs, start=True, stop=True):
        n, m = columns(rhs), columns(lhsT)
        ns = 20 + 0.83 * n if m <= DH and n >= m else 1.65 * n if n >= P else 420.0
        self.put(lambda e: e.matmul(out, lhsT, rhs, start=start, stop=stop, skip_group_check=True), ns)

    def turn(self, out, in_, ident):
        rows = in_.shape[0]
        self.put(lambda e: e.transpose(out, in_, ident[0:rows, 0:rows]), 110.0)


class Scalar(Stream):
    def act(self, out, in_, func, bias=0.0, scale=1.0, total=None):
        extra = {} if total is None else {"accum_out": total}
        operands = (total is not None) + (not isinstance(bias, float)) + (not isinstance(scale, float))
        self.put(lambda e: e.activation(out, in_, func, bias=bias, scale=scale, **extra),
                 (97 if self.steps and self.steps[-1][1] else 190) + 93 * operands + 0.83 * columns(out))


class Elementwise(Stream):

    def __init__(self, per):
        super().__init__()
        self.per = per

    def add(self, op, ap):
        self.put(op, 70 + self.per * columns(ap))

    def tt(self, out, a, b, op):
        self.add(lambda e: e.tensor_tensor(out, a, b, op), out)

    def power(self, out, a, exponent):
        self.put(lambda e: e.tensor_tensor(out, a, exponent, ALU.pow), 170.0 * columns(out))

    def ts(self, out, a, s1, s2, op0, op1=None):
        if op1 is None:
            self.add(lambda e: e.tensor_scalar(out, a, s1, None, op0), out)
        else:
            self.add(lambda e: e.tensor_scalar(out, a, s1, s2, op0, op1), out)

    def copy(self, out, a):
        self.add(lambda e: e.tensor_copy(out, a), out)

    def fill(self, out, value):
        self.add(lambda e: e.memset(out, value), out)

    def stt(self, out, a, s, b, op0, op1):
        self.add(lambda e: e.scalar_tensor_tensor(out=out, in0=a, scalar=s, in1=b, op0=op0, op1=op1), out)

    def reduce(self, out, a, op, negate=False):
        self.add(lambda e: e.tensor_reduce(out, a, AX.X, op, negate=negate), a)

    def add_max(self, out, a, b, largest):
        self.add(lambda e: e.tensor_tensor_reduce(out, a, b, 1.0, LOWEST, ALU.add, ALU.max, largest), out)

    def recip(self, out, a):
        self.add(lambda e: e.reciprocal(out, a), out)

    def top8(self, out, a):
        self.add(lambda e: e.max(out, a), out)

    def drop(self, out, values, a):
        self.add(lambda e: e.match_replace(out, values, a, LOWEST), out)

    def scan(self, out, a, b):
        self.add(lambda e: e.tensor_tensor_scan(out, a, b, 0.0, ALU.mult, ALU.add), out)


def split(ap, n):
    return ap.rearrange("p (n k) -> p n k", n=n)


def stretch(ap, k):
    return ap.unsqueeze(2).to_broadcast([ap.shape[0], ap.shape[1], k])


def repeat(ap, n):
    return ap.unsqueeze(1).to_broadcast([ap.shape[0], n, ap.shape[1]])


class Shared:
    pass


class Program:

    def __init__(self, shared):
        self.shared = shared
        self.pe, self.act, self.dve, self.pool, self.sync = Tensor(), Scalar(), Elementwise(1.04), Elementwise(2.0), Stream()
        self.streams = [self.pe, self.act, self.dve, self.pool, self.sync]


class Sequence:
    pass


def layernorm(c, s, src, ready, eps, out):
    centred, square, diag = s.w[:, 0:N], s.w[:, N:2 * N], s.w[:, 2 * N:3 * N]
    var, rstd = s.sm[:, 0:NT], s.sm[:, NT:2 * NT]
    b0, b1 = s.bank
    c.pe.wait(ready, s.free[0], c.shared.const_ready)
    c.pe.mm(b0[:, 0:N], c.shared.mean, src)
    mean_done = c.pe.mark()
    c.dve.wait(mean_done, ready)
    c.dve.tt(centred, src, b0[:, 0:N], ALU.subtract)
    centred_done = c.dve.mark()
    c.dve.wait(centred_done)
    c.dve.tt(square, centred, centred, ALU.mult)
    square_done = c.dve.mark()
    c.pe.wait(square_done, s.free[1])
    for t in range(NT):
        c.pe.mm(b1[:, t * P:(t + 1) * P], square[:, t * P:(t + 1) * P], c.shared.mean)
    var_done = c.pe.mark()
    c.dve.wait(var_done)
    c.dve.ts(var, b1[:, 0:N:P], eps, None, ALU.add)
    s.free[1] = c.dve.mark()
    c.pool.wait(s.free[1], c.shared.powers_ready)
    c.pool.power(rstd, var, c.shared.minus_half[:, 0:NT])
    rstd_done = c.pool.mark()
    c.dve.wait(rstd_done)
    for t in range(NT):
        c.dve.ts(diag[:, t * P:(t + 1) * P], c.shared.ident, rstd[:, t:t + 1], None, ALU.mult)
    diag_done = c.dve.mark()
    c.pe.wait(diag_done)
    for t in range(NT):
        c.pe.mm(b0[:, t * P:(t + 1) * P], c.shared.ones, diag[:, t * P:(t + 1) * P])
    spread = c.pe.mark()
    c.dve.wait(spread)
    c.dve.tt(out, centred, b0[:, 0:N], ALU.mult)
    s.free[0] = c.dve.mark()
    return s.free[0]


def cross_attention_0(c, s):
    b0, b1 = s.bank
    normed = layernorm(c, s, s.x[:, :], s.ready, EPS, s.xn[:, :])
    s.normed = normed
    W = s.W
    qz = s.qz[:, :].rearrange("p (r z n) -> p r z n", r=4, z=2)
    kT = s.kT[:, 0:N]
    v = s.kT[:, N:2 * N].rearrange("p (t d) -> p t d", t=NT)
    mask = split(W("mask"), NT)
    bq8 = s.sm[:, 8:8 + PAIRS]
    c.dve.wait(s.weights)
    c.dve.ts(bq8, W("bq"), 0.125, None, ALU.mult)
    bq8_done = c.dve.mark()
    for pair in range(PAIRS):
        cols = slice(pair * P, (pair + 1) * P)
        c.pe.wait(normed, s.weights, s.x_ready, *s.free)
        c.pe.mm(b0[:, 0:N], W("Wq")[:, cols], s.xn[:, :])
        c.pe.mm(b0[:, N:2 * N], W("Wk")[:, cols], s.ctx[:, :])
        qk_done = c.pe.mark()
        for t in range(NT):
            c.pe.mm(b1[:, t * P:(t + 1) * P], s.ctx[:, t * P:(t + 1) * P], W("Wv")[:, cols])
        v_done = c.pe.mark()
        c.act.wait(qk_done, s.weights, bq8_done, s.qz_zero)
        for z in range(2):
            rows = slice(z * DH, (z + 1) * DH)
            c.act.act(qz[rows, 0:NT, z, :], split(b0[rows, 0:N], NT), ACT.Identity, bias=bq8[rows, pair:pair + 1], scale=0.125)
        c.act.act(kT, b0[:, N:2 * N], ACT.Identity, bias=W("bk")[:, pair:pair + 1])
        qk_kept = c.act.mark()
        c.dve.wait(v_done)
        c.dve.copy(v, b1[:, 0:N].rearrange("p (t d) -> p t d", t=NT))
        v_kept = c.dve.mark()
        most, least, total, over = (s.sm[:, 16 + 4 * i:20 + 4 * i] for i in range(4))
        c.pe.wait(qk_kept, v_kept)
        scored = []
        for z in range(2):
            for t in range(NT):
                c.pe.mm(s.bank[z][:, t * N:(t + 1) * N], qz[:, t, z, :], kT)
            scored.append(c.pe.mark())
        e = [s.w[:, z * BANK:(z + 1) * BANK] for z in range(2)]
        pT = [s.w[:, (2 + z) * BANK:(3 + z) * BANK] for z in range(2)]
        normalised, shift_done, exp_done = [], [], []
        for z in range(2):
            c.dve.wait(scored[z], c.shared.mask_ready)
            for t in range(NT):
                i = 2 * z + t
                c.dve.add_max(e[z][:, t * N:(t + 1) * N], s.bank[z][:, t * N:(t + 1) * N], mask[:, t, :],
                              most[:, i:i + 1])
            c.dve.wait(c.dve.mark())
            c.dve.ts(least[:, 2 * z:2 * z + 2], most[:, 2 * z:2 * z + 2], -1.0, None, ALU.mult)
            shift_done.append(c.dve.mark())
        for z in range(2):
            c.act.wait(shift_done[z])
            for t in range(NT):
                i = 2 * z + t
                c.act.act(e[z][:, t * N:(t + 1) * N], e[z][:, t * N:(t + 1) * N], ACT.Exp,
                          bias=least[:, i:i + 1], total=total[:, i:i + 1])
            exp_done.append(c.act.mark())
        for z in range(2):
            c.dve.wait(exp_done[z])
            c.dve.recip(over[:, 2 * z:2 * z + 2], total[:, 2 * z:2 * z + 2])
            over_done = c.dve.mark()
            c.pool.wait(over_done)
            c.pool.tt(split(e[z], NT), split(e[z], NT), stretch(over[:, 2 * z:2 * z + 2], N), ALU.mult)
            normalised.append(c.pool.mark())
        kept = []
        for z in range(2):
            c.pe.wait(normalised[z])
            for m in range(NT):
                for t in range(NT):
                    c.pe.turn(s.bank[z][:, m * N + t * P:m * N + (t + 1) * P],
                              e[z][:, t * N + m * P:t * N + (m + 1) * P], c.shared.ident)
            turned = c.pe.mark()
            q = c.dve if z else c.act
            q.wait(turned)
            if z:
                c.dve.copy(pT[z], s.bank[z][:, :])
            else:
                c.act.act(pT[z], s.bank[z][:, :], ACT.Copy)
            kept.append(q.mark())
        c.pe.wait(*kept)
        for m in range(NT):
            for z in range(2):
                c.pe.mm(b0[z * DH:(z + 1) * DH, 0:N], v[:, m, z * DH:(z + 1) * DH],
                        pT[z][:, m * N:(m + 1) * N], start=(m == 0), stop=(m == NT - 1))
        o_done = c.pe.mark()
        oT = (s.v if pair < 4 else s.oT)[:, (pair % 4) * N:(pair % 4 + 1) * N]
        c.act.wait(o_done)
        c.act.act(oT, b0[:, 0:N], ACT.Identity, bias=W("bv")[:, pair:pair + 1])
        s.free = [c.act.mark(), kept[1]]
    c.pe.wait(*s.free)
    for pair in range(PAIRS):
        oT = (s.v if pair < 4 else s.oT)[:, (pair % 4) * N:(pair % 4 + 1) * N]
        c.pe.mm(b0[:, 0:N], W("Wo")[:, pair * D:(pair + 1) * D], oT, start=(pair == 0), stop=(pair == PAIRS - 1))
    y_done = c.pe.mark()
    update_stream(c, s, b0[:, 0:N], y_done, W("bo"), 0)


def update_stream(c, s, y, y_done, bias, gate, bank=0):
    tmp = s.w[:, 0:N]
    c.dve.wait(y_done, c.shared.gates_ready, s.weights)
    c.dve.ts(tmp, y, bias, c.shared.gates[:, gate:gate + 1], ALU.add, ALU.mult)
    s.free[bank] = c.dve.mark()
    c.dve.wait(s.free[bank])
    c.dve.tt(s.x[:, :], s.x[:, :], tmp, ALU.add)
    s.ready = c.dve.mark()


def shifted(c, s, ready):
    c.dve.wait(ready)
    c.dve.copy(s.zs[0:DH, :], s.z[0:DH, :])
    c.dve.copy(s.zs[DH:P, 1:N], s.z[DH:P, 0:N - 1])
    return c.dve.mark()


def local_heads(c, s, stage, half, zs_ready):
    W, bank = s.W, s.bank[half]
    part = slice(half * BANK, (half + 1) * BANK)
    heads, pairs = 4, 2
    tab = c.shared.tables[stage % 2][:, :].rearrange("p (a k t d) -> p a k t d", a=2, k=2, t=NT)
    qz = s.qz[:, part].rearrange("p (r z n) -> p r z n", r=pairs, z=2)
    kT = split(s.kT[:, part], pairs)
    v = split(s.v[:, part], NT)
    oT = split(s.oT[:, part], pairs)
    before = split(s.before[:, half * heads * EARLY:(half + 1) * heads * EARLY], heads)
    w = [s.w[:, (3 * half + i) * BANK:(3 * half + i + 1) * BANK] for i in range(3)]
    small = s.sm[:, 64 + 32 * half:96 + 32 * half]
    sq_sum, norm = small[:, 0:8], small[:, 8:16]
    most, total, over = (small[:, 16 + 4 * i:20 + 4 * i] for i in range(3))
    qk = lambda a, lo=0, hi=DH: a.rearrange("p (k h d) -> p k h d", k=2, h=heads)[:, :, :, lo:hi]
    out_done = None
    for first in (half * 2 * heads, half * 2 * heads + heads):
        for t in range(NT):
            tile = slice(t * P, (t + 1) * P)
            spread = lambda a, lo=0, hi=DH: tab[:, a, :, t, lo:hi].unsqueeze(2).to_broadcast([P, 2, heads, hi - lo])
            c.pe.wait(zs_ready, s.weights, s.free[half])
            for k in range(2):
                c.pe.mm(bank[:, k * N:(k + 1) * N], s.zs[:, tile],
                        W("Wqkv")[:, k * INNER + first * DH:k * INNER + (first + heads) * DH])
            made = c.pe.mark()
            c.act.wait(made, s.free[half])
            c.act.act(w[0], bank[:, :], ACT.Square)
            squared = c.act.mark()
            c.dve.wait(made, squared, s.table_ready)
            c.dve.tt(qk(w[1]), qk(bank[:, :]), spread(0), ALU.mult)
            c.dve.tt(qk(w[2], 0, DH // 2), qk(bank[:, :], DH // 2, DH), spread(1, 0, DH // 2), ALU.mult)
            c.dve.tt(qk(w[2], DH // 2, DH), qk(bank[:, :], 0, DH // 2), spread(1, DH // 2, DH), ALU.mult)
            products = c.dve.mark()
            c.dve.reduce(sq_sum, split(w[0], 2 * heads), ALU.add)
            summed = c.dve.mark()
            c.pool.wait(summed, c.shared.powers_ready)
            c.pool.ts(norm, sq_sum, 1e-24, None, ALU.max)
            c.pool.wait(c.pool.mark())
            c.pool.power(norm, norm, c.shared.minus_half[:, 0:2 * heads])
            norm_done = c.pool.mark()
            c.pe.wait(products)
            c.pe.mm(bank[:, 0:N], s.zs[:, tile], W("Wqkv")[:, 2 * INNER + first * DH:2 * INNER + (first + heads) * DH])
            v_done = c.pe.mark()
            c.act.wait(v_done)
            c.act.act(v[:, t, :], bank[:, 0:N], ACT.Copy)
            v_kept = c.act.mark()
            c.dve.wait(products)
            c.dve.tt(w[1], w[1], w[2], ALU.add)
            added = c.dve.mark()
            c.pool.wait(added, norm_done)
            c.pool.tt(split(w[1], 2 * heads), split(w[1], 2 * heads), stretch(norm, DH), ALU.mult)
            normed = c.pool.mark()
            c.pe.wait(normed, v_kept)
            for r in range(2 * pairs):
                c.pe.turn(bank[:, r * P:(r + 1) * P], w[1][:, r * P:(r + 1) * P], c.shared.ident)
            turned = c.pe.mark()
            c.act.wait(turned, s.qz_zero)
            for z in range(2):
                rows = slice(z * DH, (z + 1) * DH)
                c.act.act(qz[rows, :, z, :], split(bank[rows, 0:N], pairs), ACT.Copy)
            c.act.act(kT[:, :, tile], split(bank[:, N:2 * N], pairs), ACT.Copy)
            qk_kept = c.act.mark()
            c.pe.wait(qk_kept)
            for h in range(heads):
                r, z = divmod(h, 2)
                c.pe.mm(bank[:, h * P:(h + 1) * P], qz[:, r, z, :], kT[:, r, tile])
            if t:
                for h in range(heads):
                    r, z = divmod(h, 2)
                    c.pe.mm(bank[0:WINDOW, (h + 1) * P - WINDOW:(h + 1) * P], qz[:, r, z, 0:WINDOW], kT[:, r, P - WINDOW:P])
            scored = c.pe.mark()
            c.dve.wait(scored)
            for h in range(heads):
                c.dve.add_max(w[0][:, h * P:(h + 1) * P], bank[:, h * P:(h + 1) * P], c.shared.band[:, tile],
                              most[:, h:h + 1])
            score_kept = c.dve.mark()
            c.pool.wait(score_kept)
            c.pool.tt(split(w[0], heads), split(w[0], heads), stretch(most, P), ALU.subtract)
            shift_done = c.pool.mark()
            c.act.wait(shift_done)
            for h in range(heads):
                c.act.act(w[0][:, h * P:(h + 1) * P], w[0][:, h * P:(h + 1) * P], ACT.Exp, total=total[:, h:h + 1])
            exp_done = c.act.mark()
            c.dve.wait(exp_done)
            c.dve.recip(over, total)
            c.dve.wait(c.dve.mark())
            c.dve.tt(split(w[0], heads), split(w[0], heads), stretch(over, P), ALU.mult)
            normalised = c.dve.mark()
            c.pe.wait(normalised, score_kept)
            for h in range(heads):
                c.pe.turn(bank[:, h * P:(h + 1) * P], w[0][:, h * P:(h + 1) * P], c.shared.ident)
            turned = c.pe.mark()
            c.act.wait(turned)
            c.act.act(w[2], bank[:, :], ACT.Copy)
            kept = c.act.mark()
            if t:
                last = slice(P - WINDOW, P)
                c.dve.wait(kept, s.qz_zero)
                c.dve.copy(before[last, :, 0:WINDOW], split(bank[:, :], heads)[last, :, 0:WINDOW])
                c.dve.fill(split(w[2], heads)[last, :, 0:WINDOW], 0.0)
                kept = c.dve.mark()
            c.pe.wait(kept)
            for h in range(heads):
                r, z = divmod(h, 2)
                c.pe.mm(bank[z * DH:(z + 1) * DH, r * P:(r + 1) * P], v[:, t, h * DH:(h + 1) * DH],
                        w[2][:, h * P:(h + 1) * P], start=True, stop=(t == 0))
                if t:
                    c.pe.mm(bank[z * DH:(z + 1) * DH, r * P:r * P + EARLY], v[:, 0, h * DH:(h + 1) * DH], before[:, h, :],
                            start=False, stop=True)
            o_done = c.pe.mark()
            c.act.wait(o_done, *([out_done] if out_done else []))
            c.act.act(oT[:, :, tile], split(bank[:, 0:N], pairs), ACT.Copy)
            s.free[half] = c.act.mark()
        if out_done is None:
            c.pe.wait(s.free[half])
            project_out(c, s, bank[:, 0:N], oT, first, True, True)
            out_done = c.pe.mark()
            c.dve.wait(out_done, zs_ready, *s.z_added)
            c.dve.tt(s.z[:, :], s.z[:, :], bank[:, 0:N], ALU.add)
            s.free[half] = c.dve.mark()
            s.z_added.append(s.free[half])


def project_out(c, s, out, oT, first, start, stop):
    for r in range(2):
        pair = first // 2 + r
        c.pe.mm(out, s.W("Wo")[:, pair * D:(pair + 1) * D], oT[:, r, :], start=(start and r == 0), stop=(stop and r == 1))


def local_layer(c, s, stage):
    b0, b1 = s.bank
    W = s.W
    w = [s.w[:, i * BANK:(i + 1) * BANK] for i in range(6)]
    if stage == 1:
        z_ready = layernorm(c, s, s.x[:, :], s.ready, EPS, s.z[:, :])
        c.dve.fill(s.zs[DH:P, 0:1], 0.0)
    else:
        z_ready = s.z_ready
    zs_ready = shifted(c, s, z_ready)
    s.z_added = []
    local_heads(c, s, stage, 0, zs_ready)
    local_heads(s.beside, s, stage, 1, zs_ready)
    c.pe.wait(*s.free)
    for half in range(2):
        project_out(c, s, b0[:, 0:N], split(s.oT[:, half * BANK:(half + 1) * BANK], 2), half * 8 + 4, half == 0, half == 1)
    y_done = c.pe.mark()
    c.dve.wait(y_done, *s.z_added)
    c.dve.tt(s.z[:, :], s.z[:, :], b0[:, 0:N], ALU.add)
    s.free[0] = z_ready = c.dve.mark()
    zs_ready = shifted(c, s, z_ready)
    normed = layernorm(c, s, s.zs[:, :], zs_ready, EPS, s.xn[:, :])
    c.dve.wait(normed, s.weights)
    c.dve.ts(s.xn[:, :], s.xn[:, :], W("ln_g"), W("ln_b"), ALU.mult, ALU.add)
    normed = c.dve.mark()
    hidden = []
    for i, (start, m) in enumerate(FFC):
        bank = s.bank[i % 2]
        c.pe.wait(normed, s.weights, s.free[i % 2])
        for z in range(2):
            c.pe.mm(bank[0:m, z * N:(z + 1) * N], W("W1")[:, z * FF + start:z * FF + start + m], s.xn[:, :])
        made = c.pe.mark()
        gelu, prod = w[i][0:m, 0:N], w[i][0:m, N:2 * N]
        bias = W("b1")
        c.act.wait(made, normed, s.weights)
        c.act.act(gelu, bank[0:m, N:2 * N], ACT.Gelu, bias=bias[0:m, len(FFC) + i:len(FFC) + i + 1])
        gelu_done = c.act.mark()
        c.dve.wait(gelu_done)
        c.dve.stt(prod, bank[0:m, 0:N], bias[0:m, i:i + 1], gelu, ALU.add, ALU.mult)
        s.free[i % 2] = c.dve.mark()
        hidden.append((prod, s.free[i % 2], m))
    for i, (prod, ready, m) in enumerate(hidden):
        c.pe.wait(ready, s.free[1])
        c.pe.mm(b1[:, 0:N], W("W2")[0:m, i * D:(i + 1) * D], prod, start=(i == 0), stop=(i == len(hidden) - 1))
    y_done = c.pe.mark()
    c.dve.wait(y_done)
    c.dve.stt(s.z[:, :], b1[:, 0:N], W("b2"), s.z[:, :], ALU.add, ALU.add)
    s.free[1] = s.z_ready = s.ready = c.dve.mark()
    if stage == DEPTH:
        c.dve.wait(s.z_ready, c.shared.gates_ready)
        c.dve.stt(s.x[:, :], s.z[:, :], c.shared.gates[:, B:B + 1], s.x[:, :], ALU.mult, ALU.add)
        s.ready = c.dve.mark()


def project(c, s, out, w, src, ready, bias, bank, half=0):
    dst = s.bank[bank][:, half * N:(half + 1) * N]
    c.pe.wait(ready, s.weights, s.free[bank])
    c.pe.mm(dst, w, src)
    made = c.pe.mark()
    c.act.wait(made, s.weights)
    c.act.act(out, dst, ACT.Identity, bias=bias)
    s.free[bank] = c.act.mark()
    return s.free[bank]


def attention(c, s, qT, kT, v, qk_ready, v_ready, scale):
    b0, b1 = s.bank
    e, pT = s.w[:, 0:BANK], s.w[:, BANK:2 * BANK]
    least, total, over = (s.sm[:, 160 + 2 * i:162 + 2 * i] for i in range(3))
    c.pe.wait(qk_ready, s.free[0])
    for t in range(NT):
        c.pe.mm(b0[:, t * N:(t + 1) * N], qT[:, t * P:(t + 1) * P], kT)
    scored = c.pe.mark()
    c.dve.wait(scored)
    c.dve.reduce(least, split(b0[:, :], NT), ALU.max, negate=True)
    c.dve.wait(c.dve.mark())
    c.dve.ts(least, least, scale, None, ALU.mult)
    shift_done = c.dve.mark()
    c.act.wait(shift_done)
    for t in range(NT):
        c.act.act(e[:, t * N:(t + 1) * N], b0[:, t * N:(t + 1) * N], ACT.Exp, bias=least[:, t:t + 1], scale=scale,
                  total=total[:, t:t + 1])
    s.free[0] = c.act.mark()
    c.dve.wait(s.free[0])
    c.dve.recip(over, total)
    over_done = c.dve.mark()
    c.dve.wait(over_done)
    c.dve.tt(split(e, NT), split(e, NT), stretch(over, N), ALU.mult)
    normalised = c.dve.mark()
    c.pe.wait(normalised, s.free[1])
    for m in range(NT):
        for t in range(NT):
            c.pe.turn(b1[:, m * N + t * P:m * N + (t + 1) * P], e[:, t * N + m * P:t * N + (m + 1) * P], c.shared.ident)
    turned = c.pe.mark()
    c.act.wait(turned)
    c.act.act(pT, b1[:, :], ACT.Copy)
    s.free[1] = c.act.mark()
    c.pe.wait(s.free[1], v_ready, s.free[0])
    for m in range(NT):
        c.pe.mm(b0[:, 0:N], v[:, m, :], pT[:, m * N:(m + 1) * N], start=(m == 0), stop=(m == NT - 1))
    return c.pe.mark()


def values(c, s, out, src, w, ready):
    c.pe.wait(ready, s.weights, s.free[1])
    for t in range(NT):
        c.pe.mm(s.bank[1][:, t * P:(t + 1) * P], src[:, t * P:(t + 1) * P], w)
    made = c.pe.mark()
    c.dve.wait(made)
    c.dve.copy(out, split(s.bank[1][:, 0:N], NT))
    s.free[1] = c.dve.mark()
    return s.free[1]


def cross_attention_1(c, s):
    W = s.W
    normed = layernorm(c, s, s.x[:, :], s.ready, EPS, s.xn[:, :])
    qT, kT = s.kT[:, 0:N], s.kT[:, N:2 * N]
    v = split(s.kT[:, 2 * N:3 * N], NT)
    found = (s.v[:, 0:N], s.v[:, N:2 * N])
    for i, (src_q, src_kv, wq, wk, wv) in enumerate((
            (s.xn[:, :], s.ctx[:, :], "q_c", "k_s", "v_s"), (s.ctx[:, :], s.xn[:, :], "q_s", "k_c", "v_c"))):
        ready = normed if i == 0 else found_ready
        q_ready = project(c, s, qT, W("W" + wq), src_q, ready, W("b" + wq), 0, 0)
        k_ready = project(c, s, kT, W("W" + wk), src_kv, ready, W("b" + wk), 0, 1)
        v_ready = values(c, s, v, src_kv, W("W" + wv), ready)
        o_done = attention(c, s, qT, kT, v, k_ready, v_ready, D ** -0.5)
        c.act.wait(o_done)
        c.act.act(found[i], s.bank[0][:, 0:N], ACT.Identity, bias=W("b" + wv))
        s.free[0] = found_ready = c.act.mark()
    half_bias, gate, diff = s.sm[:, 170:171], s.w[:, 0:N], s.w[:, N:2 * N]
    c.pe.wait(found_ready, s.free[0])
    c.pe.mm(s.bank[0][:, 0:N], W("Wg_a"), found[0], start=True, stop=False)
    c.pe.mm(s.bank[0][:, 0:N], W("Wg_b"), found[1], start=False, stop=True)
    z_done = c.pe.mark()
    c.dve.wait(found_ready, s.weights)
    c.dve.ts(half_bias, W("bg"), 0.5, None, ALU.mult)
    c.dve.tt(diff, found[0], found[1], ALU.subtract)
    diff_done = c.dve.mark()
    c.act.wait(z_done, diff_done)
    c.act.act(gate, s.bank[0][:, 0:N], ACT.Tanh, bias=half_bias, scale=0.5)
    s.free[0] = c.act.mark()
    c.dve.wait(s.free[0])
    c.dve.ts(gate, gate, 0.5, 0.5, ALU.mult, ALU.add)
    c.dve.wait(c.dve.mark(), diff_done)
    c.dve.tt(diff, diff, gate, ALU.mult)
    c.dve.wait(c.dve.mark())
    c.dve.tt(diff, diff, found[1], ALU.add)
    c.dve.wait(c.dve.mark(), c.shared.gates_ready)
    c.dve.stt(s.x[:, :], diff, c.shared.gates[:, 1:2], s.x[:, :], ALU.mult, ALU.add)
    s.ready = c.dve.mark()


def mixture_1(c, s):
    W = s.W
    b0, b1 = s.bank
    normed = layernorm(c, s, s.x[:, :], s.ready, EPS, s.xn[:, :])
    n = NT * E1
    tiles = [s.sm[:, 192 + n * i:192 + n * (i + 1)] for i in range(10)]
    z, work, ordered, square, mean, meansq, tau, a, ones, pick = tiles
    stat, factor = s.sm[:, 172:172 + NT], s.sm[:, 174:174 + NT]
    c.pe.wait(normed, s.weights, s.free[0])
    for t in range(NT):
        c.pe.mm(b0[:, t * E1:(t + 1) * E1], s.xn[:, t * P:(t + 1) * P], W("proj"))
    made = c.pe.mark()

    def then():
        c.dve.wait(c.dve.mark())

    v = c.dve
    v.wait(made)
    v.copy(z, b0[:, 0:n])
    s.free[0] = c.dve.mark()
    v.wait(s.free[0])
    v.reduce(stat, split(z, NT), ALU.add)
    then()
    v.ts(stat, stat, 1.0 / E1, None, ALU.mult)
    then()
    v.tt(split(z, NT), split(z, NT), stretch(stat, E1), ALU.subtract)
    then()
    v.tt(square, z, z, ALU.mult)
    then()
    v.reduce(stat, split(square, NT), ALU.add)
    then()
    v.ts(stat, stat, 1.0 / E1, EPS, ALU.mult, ALU.add)
    var_done = c.dve.mark()
    c.pool.wait(var_done, c.shared.powers_ready)
    c.pool.power(factor, stat, c.shared.minus_half[:, 0:NT])
    factor_done = c.pool.mark()
    v.wait(factor_done)
    v.tt(split(z, NT), split(z, NT), stretch(factor, E1), ALU.mult)
    then()
    v.reduce(stat, split(z, NT), ALU.max)
    then()
    v.tt(split(z, NT), split(z, NT), stretch(stat, E1), ALU.subtract)
    then()
    v.ts(z, z, 0.5, None, ALU.mult)
    v.fill(ones, 1.0)
    then()
    for t in range(NT):
        v.top8(ordered[:, t * E1:t * E1 + 8], z[:, t * E1:(t + 1) * E1])
    then()
    for t in range(NT):
        v.drop(work[:, t * E1:(t + 1) * E1], ordered[:, t * E1:t * E1 + 8], z[:, t * E1:(t + 1) * E1])
    then()
    for t in range(NT):
        v.top8(ordered[:, t * E1 + 8:(t + 1) * E1], work[:, t * E1:(t + 1) * E1])
    then()
    v.tt(square, ordered, ordered, ALU.mult)
    then()
    for t in range(NT):
        cols = slice(t * E1, (t + 1) * E1)
        v.scan(mean[:, cols], ones[:, cols], ordered[:, cols])
        v.scan(meansq[:, cols], ones[:, cols], square[:, cols])
    then()
    v.tt(split(mean, NT), split(mean, NT), repeat(c.shared.invk, NT), ALU.mult)
    v.tt(split(meansq, NT), split(meansq, NT), repeat(c.shared.invk, NT), ALU.mult)
    then()
    v.tt(tau, mean, mean, ALU.mult)
    then()
    v.tt(tau, meansq, tau, ALU.subtract)
    then()
    v.tt(split(tau, NT), split(tau, NT), repeat(c.shared.k, NT), ALU.mult)
    then()
    v.ts(tau, tau, -1.0, 1.0, ALU.mult, ALU.add)
    then()
    v.tt(split(tau, NT), split(tau, NT), repeat(c.shared.invk, NT), ALU.mult)
    then()
    v.ts(tau, tau, 0.0, None, ALU.max)
    delta_done = c.dve.mark()
    c.pool.wait(delta_done)
    c.pool.power(a, tau, c.shared.half[:, 0:n])
    root_done = c.pool.mark()
    v.wait(root_done)
    v.tt(tau, mean, a, ALU.subtract)
    then()
    v.tt(work, tau, ordered, ALU.is_le)
    then()
    v.reduce(stat, split(work, NT), ALU.add)
    then()
    v.tt(split(pick, NT), repeat(c.shared.k, NT), stretch(stat, E1), ALU.is_equal)
    then()
    v.tt(pick, pick, tau, ALU.mult)
    then()
    v.reduce(stat, split(pick, NT), ALU.add)
    then()
    v.tt(split(a, NT), split(z, NT), stretch(stat, E1), ALU.subtract)
    then()
    v.ts(a, a, 0.0, None, ALU.max)
    then()
    v.tt(a, a, a, ALU.mult)
    a_done = c.dve.mark()
    c.pe.wait(a_done, s.free[0])
    for t in range(NT):
        c.pe.turn(b0[0:E1, t * P:(t + 1) * P], a[:, t * E1:(t + 1) * E1], c.shared.ident)
    turned = c.pe.mark()
    aT, g = s.w[0:E1, 0:N], s.w[0:R1, BANK:2 * BANK]
    z1, z2 = s.w[0:R1, 2 * BANK:2 * BANK + N], s.w[0:R1, 2 * BANK + N:3 * BANK]
    hT = split(s.v[:, :], O1 // P)
    c.act.wait(turned)
    c.act.act(aT, b0[0:E1, 0:N], ACT.Copy)
    aT_done = c.act.mark()
    c.pe.wait(aT_done, s.free[1])
    c.pe.mm(b0[0:R1, 0:N], W("C1")[0:E1, :], aT)
    c.pe.mm(b0[0:R1, N:2 * N], W("C2")[0:E1, :], aT)
    c.pe.mm(b1[0:R1, 0:N], W("Win1"), s.xn[:, :])
    made = c.pe.mark()
    c.act.wait(made)
    c.act.act(g, b0[0:R1, :], ACT.Copy)
    g_done = c.act.mark()
    c.dve.wait(g_done)
    c.dve.stt(z1, b1[0:R1, 0:N], W("bin1")[0:R1, :], g[:, 0:N], ALU.add, ALU.mult)
    z1_done = c.dve.mark()
    c.pe.wait(z1_done)
    made = []
    for j in range(2):
        for i in range(2):
            o = 2 * j + i
            c.pe.mm(s.bank[j][:, i * N:(i + 1) * N], W("Wout1")[0:R1, o * P:(o + 1) * P], z1)
        made.append(c.pe.mark())
    for j in range(2):
        c.act.wait(made[j])
        c.act.act(s.v[:, j * BANK:(j + 1) * BANK], s.bank[j][:, :], ACT.Gelu)
    gelu_done = c.act.mark()
    c.pe.wait(gelu_done)
    for o in range(O1 // P):
        c.pe.mm(b0[0:R1, 0:N], W("Win2")[:, o * R1:(o + 1) * R1], hT[:, o, :], start=(o == 0), stop=(o == O1 // P - 1))
    made = c.pe.mark()
    c.dve.wait(made)
    c.dve.stt(z2, b0[0:R1, 0:N], W("bin2")[0:R1, :], g[:, N:2 * N], ALU.add, ALU.mult)
    s.free[0] = c.dve.mark()
    c.pe.wait(s.free[0])
    c.pe.mm(b1[:, 0:N], W("Wout2")[0:R1, :], z2)
    made = c.pe.mark()
    c.dve.wait(made, c.shared.gates_ready)
    c.dve.stt(s.x[:, :], b1[:, 0:N], c.shared.gates[:, B + 1:B + 2], s.x[:, :], ALU.mult, ALU.add)
    s.free[1] = s.ready = c.dve.mark()


def cross_attention_2(c, s):
    W = s.W
    normed = layernorm(c, s, s.x[:, :], s.ready, EPS, s.xn[:, :])
    qT, kT = s.kT[:, 0:N], s.kT[:, N:2 * N]
    v = split(s.kT[:, 2 * N:3 * N], NT)
    res, out = s.v[:, 0:N], s.v[:, N:2 * N]
    project(c, s, qT, W("Wq"), s.xn[:, :], normed, W("bq"), 0, 0)
    k_ready = project(c, s, kT, W("Wk"), s.ctx[:, :], normed, W("bk"), 0, 1)
    v_ready = values(c, s, v, s.ctx[:, :], W("Wv"), normed)
    o_done = attention(c, s, qT, kT, v, k_ready, v_ready, D ** -0.5)
    c.dve.wait(o_done)
    c.dve.stt(res, s.bank[0][:, 0:N], W("bv"), s.ctx[:, :], ALU.add, ALU.add)
    s.free[0] = c.dve.mark()
    out_ready = layernorm(c, s, res, s.free[0], EPS_L2, out)
    c.dve.wait(out_ready)
    c.dve.ts(out, out, W("gamma"), W("beta"), ALU.mult, ALU.add)
    c.dve.wait(c.dve.mark())
    c.dve.stt(s.x[:, :], out, c.shared.gates[:, 2:3], s.x[:, :], ALU.mult, ALU.add)
    s.ready = c.dve.mark()


def top_two(c, s, biased, keep):
    n = NT * E2
    a, b = s.w[:, 0:n * E2], s.w[:, n * E2:2 * n * E2]
    a4, b4 = (x.rearrange("p (t i j) -> p t i j", t=NT, i=E2) for x in (a, b))
    other = split(biased, NT).unsqueeze(2).to_broadcast([P, NT, E2, E2])
    mine = split(biased, NT).unsqueeze(3).to_broadcast([P, NT, E2, E2])
    tri = split(c.shared.tri, E2).unsqueeze(1).to_broadcast([P, NT, E2, E2])
    c.dve.tt(a4, other, mine, ALU.is_gt)
    c.dve.tt(b4, other, mine, ALU.is_equal)
    c.dve.wait(c.dve.mark())
    c.dve.tt(b4, b4, tri, ALU.mult)
    c.dve.wait(c.dve.mark())
    c.dve.tt(a, a, b, ALU.add)
    c.dve.wait(c.dve.mark())
    c.dve.reduce(keep, split(a, n), ALU.add)
    c.dve.wait(c.dve.mark())
    c.dve.ts(keep, keep, K2 - 0.5, None, ALU.is_lt)
    return c.dve.mark()


def mixture_2(c, s):
    W = s.W
    b0, y = s.bank[0], s.bank[1][:, 0:N]
    n = NT * E2
    normed = layernorm(c, s, s.x[:, :], s.ready, EPS, s.xn[:, :])
    score, biased, keep = (s.sm[:, 192 + n * i:192 + n * (i + 1)] for i in range(3))
    least, total, over = (s.sm[:, 176 + NT * i:176 + NT * (i + 1)] for i in range(3))
    c.pe.wait(normed, s.weights, s.free[0])
    for t in range(NT):
        c.pe.mm(b0[:, t * E2:(t + 1) * E2], s.xn[:, t * P:(t + 1) * P], W("gate_w"))
    made = c.pe.mark()
    c.dve.wait(made)
    c.dve.reduce(least, split(b0[:, 0:n], NT), ALU.max, negate=True)
    shift_done = c.dve.mark()
    c.act.wait(shift_done)
    for t in range(NT):
        c.act.act(score[:, t * E2:(t + 1) * E2], b0[:, t * E2:(t + 1) * E2], ACT.Exp, bias=least[:, t:t + 1],
                  total=total[:, t:t + 1])
    s.free[0] = c.act.mark()
    c.dve.wait(s.free[0])
    c.dve.recip(over, total)
    c.dve.wait(c.dve.mark(), s.weights)
    c.dve.tt(split(score, NT), split(score, NT), stretch(over, E2), ALU.mult)
    c.dve.wait(c.dve.mark())
    c.dve.tt(split(biased, NT), split(score, NT), repeat(W("gate_b"), NT), ALU.add)
    c.dve.wait(c.dve.mark())
    keep_done = top_two(c, s, biased, keep)
    c.dve.wait(keep_done)
    c.dve.tt(keep, keep, score, ALU.mult)
    gate_done = c.dve.mark()
    gT = s.w[:, 5 * BANK:5 * BANK + N]
    c.pool.wait(normed)
    c.pool.fill(gT, 1.0)
    filled = c.pool.mark()
    c.pe.wait(gate_done)
    for t in range(NT):
        c.pe.turn(b0[0:E2, t * P:(t + 1) * P], keep[:, t * E2:(t + 1) * E2], c.shared.ident)
    turned = c.pe.mark()
    c.act.wait(turned, filled)
    c.act.act(gT[0:E2, :], b0[0:E2, 0:N], ACT.Copy)
    gT_done = c.act.mark()
    homes = [s.kT[:, :BANK], s.kT[:, BANK:], s.oT[:, :BANK], s.oT[:, BANK:], s.v[:, :BANK], s.v[:, BANK:], s.qz[:, :BANK]]
    pick, rows_ready = split(W("pick"), HT2), []
    c.pe.wait(gT_done)
    for j, home in enumerate(homes):
        bank, tiles = s.bank[j % 2], range(2 * j, min(2 * j + 2, HT2))
        c.pe.wait(s.free[j % 2])
        for i in tiles:
            c.pe.mm(bank[:, (i % 2) * N:(i % 2 + 1) * N], pick[:, i, :], gT)
        made = c.pe.mark()
        q = c.dve if j % 2 else c.act
        q.wait(made)
        if j % 2:
            c.dve.copy(home[:, 0:len(tiles) * N], bank[:, 0:len(tiles) * N])
        else:
            c.act.act(home[:, 0:len(tiles) * N], bank[:, 0:len(tiles) * N], ACT.Copy)
        s.free[j % 2] = q.mark()
        rows_ready.append(s.free[j % 2])
    c.pe.wait(s.free[1], gT_done)
    c.pe.mm(y, W("b2"), gT, start=True, stop=False)
    w2, b1, b3 = split(W("w2"), HT2), W("b1"), W("b3")
    hidden, used = [], []
    for i in range(HT2 + 1):
        if i < HT2:
            m = min(P, (E2 + 1) * HID2 - i * P)
            t3, prod, silu = (s.w[0:m, (3 * (i % 3) + n) * N:(3 * (i % 3) + n + 1) * N] for n in range(3))
            c.pe.wait(s.free[0], normed)
            c.pe.mm(b0[0:m, 0:N], W("w1")[:, i * P:i * P + m], s.xn[:, :])
            c.pe.mm(b0[0:m, N:2 * N], W("w3")[:, i * P:i * P + m], s.xn[:, :])
            made = c.pe.mark()
            c.dve.wait(made, *used[i - 3:i - 2] if i >= 3 else [])
            c.dve.ts(t3, b0[0:m, N:2 * N], b3[0:m, i:i + 1], None, ALU.add)
            t3_done = c.dve.mark()
            c.dve.wait(t3_done)
            c.dve.stt(prod, b0[0:m, 0:N], b1[0:m, i:i + 1], t3, ALU.add, ALU.mult)
            s.free[0] = c.dve.mark()
            c.act.wait(s.free[0])
            c.act.act(silu, prod, ACT.Silu)
            silu_done = c.act.mark()
            c.dve.wait(silu_done, rows_ready[i // 2])
            c.dve.tt(silu, silu, homes[i // 2][0:m, (i % 2) * N:(i % 2 + 1) * N], ALU.mult)
            hidden.append((silu, m, c.dve.mark()))
        if i:
            rows, m, ready = hidden[i - 1]
            c.pe.wait(ready)
            c.pe.mm(y, w2[0:m, i - 1, :], rows, start=False, stop=(i == HT2))
            used.append(c.pe.mark())
    c.dve.wait(used[-1], c.shared.gates_ready)
    c.dve.stt(s.x[:, :], y, c.shared.gates[:, B + 2:B + 3], s.x[:, :], ALU.mult, ALU.add)
    s.free[1] = s.ready = c.dve.mark()


def cross_attention_3(c, s):
    W = s.W
    b0, b1 = s.bank
    normed = layernorm(c, s, s.x[:, :], s.ready, EPS, s.xn[:, :])
    qT, kT = s.kT[:, 0:N], s.kT[:, N:2 * N]
    v = split(s.kT[:, 2 * N:3 * N], NT)
    scale = DH3 ** -0.5
    project(c, s, qT, W("Wq"), s.xn[:, :], normed, W("bq"), 0, 0)
    k_ready = project(c, s, kT, W("Wk"), s.ctx[:, :], normed, W("bk"), 0, 1)
    c.pe.wait(s.free[1])
    for t in range(NT):
        c.pe.mm(b1[:, t * P:(t + 1) * P], s.ctx[:, t * P:(t + 1) * P], W("Wv"))
    made = c.pe.mark()
    c.dve.wait(made)
    c.dve.tt(v, split(b1[:, 0:N], NT), repeat(W("bv"), NT), ALU.add)
    s.free[1] = v_ready = c.dve.mark()
    vz = [s.v[:, :].rearrange("p (h d) -> p h d", h=2 * H3), s.oT[:, :].rearrange("p (h d) -> p h d", h=2 * H3)]
    vz = [x[:, 0:H3, :] for x in vz]
    c.pool.wait(normed)
    for t in range(NT):
        c.pool.fill(vz[t], 0.0)
    zeroed = c.pool.mark()
    used, held, done = [normed, normed], [None, None], None
    waiting = None
    for h in range(H3 + 1):
        if h < H3:
            kz, e = s.w[:, (h % 2) * N:(h % 2 + 1) * N], s.w[:, (1 + h % 2) * BANK:(2 + h % 2) * BANK]
            least, total, over = (s.sm[:, 184 + 8 * (h % 2) + NT * i:184 + 8 * (h % 2) + NT * (i + 1)] for i in range(3))
            c.pool.wait(k_ready, used[h % 2])
            c.pool.ts(kz, kT, c.shared.headmask[:, h:h + 1], None, ALU.mult)
            kz_done = c.pool.mark()
            c.pe.wait(kz_done, s.free[0])
            for m in range(NT):
                c.pe.mm(b0[:, m * N:(m + 1) * N], kz[:, m * P:(m + 1) * P], qT)
            scored = c.pe.mark()
            c.dve.wait(scored, used[h % 2])
            c.dve.reduce(least, split(b0[:, :], NT), ALU.max, negate=True)
            c.dve.wait(c.dve.mark())
            c.dve.ts(least, least, scale, None, ALU.mult)
            shift_done = c.dve.mark()
            c.act.wait(shift_done, used[h % 2])
            for m in range(NT):
                c.act.act(e[:, m * N:(m + 1) * N], b0[:, m * N:(m + 1) * N], ACT.Exp, bias=least[:, m:m + 1],
                          scale=scale, total=total[:, m:m + 1])
            s.free[0] = c.act.mark()
            c.dve.wait(s.free[0], zeroed, v_ready)
            c.dve.recip(over, total)
            c.dve.wait(c.dve.mark())
            for m in range(NT):
                c.dve.ts(vz[m][:, h, (h % 4) * DH3:(h % 4 + 1) * DH3], v[:, m, h * DH3:(h + 1) * DH3],
                         over[:, m:m + 1], None, ALU.mult)
            now = (h, e, c.dve.mark())
        if waiting:
            g, e_g, ready = waiting
            rows = slice(32 * (g // 4), 32 * (g // 4) + 32)
            c.pe.wait(ready, s.free[1])
            for m in range(NT):
                c.pe.mm(b1[rows, 0:N], vz[m][:, g, :], e_g[:, m * N:(m + 1) * N], start=(g % 4 == 0 and m == 0),
                        stop=(g % 4 == 3 and m == NT - 1))
            used[g % 2] = done = c.pe.mark()
        waiting = now
    oT = s.w[:, 3 * BANK:3 * BANK + N]
    c.act.wait(done)
    c.act.act(oT, b1[:, 0:N], ACT.Copy)
    s.free[1] = o_kept = c.act.mark()
    c.pe.wait(o_kept, s.free[0])
    c.pe.mm(b0[:, 0:N], W("Wo"), oT)
    y_done = c.pe.mark()
    update_stream(c, s, b0[:, 0:N], y_done, W("bo"), 3)


def mixture_3(c, s):
    W = s.W
    b0, b1 = s.bank
    n = NT * E3
    normed = layernorm(c, s, s.x[:, :], s.ready, EPS, s.xn[:, :])
    logit, keep, gate = (s.sm[:, 192 + n * i:192 + n * (i + 1)] for i in range(3))
    stat, total, over = (s.sm[:, 176 + NT * i:176 + NT * (i + 1)] for i in range(3))
    c.pe.wait(normed, s.weights, s.free[0])
    for t in range(NT):
        c.pe.mm(b0[:, t * E3:(t + 1) * E3], s.xn[:, t * P:(t + 1) * P], W("gate_w"))
    made = c.pe.mark()
    c.dve.wait(made)
    c.dve.tt(split(logit, NT), split(b0[:, 0:n], NT), repeat(W("gate_b"), NT), ALU.add)
    s.free[0] = c.dve.mark()
    c.dve.wait(s.free[0])
    keep_done = top_two(c, s, logit, keep)
    c.dve.reduce(stat, split(logit, NT), ALU.max)
    c.dve.wait(c.dve.mark(), keep_done)
    c.dve.tt(split(logit, NT), split(logit, NT), stretch(stat, E3), ALU.subtract)
    shifted_done = c.dve.mark()
    c.act.wait(shifted_done)
    c.act.act(gate, logit, ACT.Exp)
    exp_done = c.act.mark()
    c.dve.wait(exp_done)
    c.dve.tt(gate, gate, keep, ALU.mult)
    c.dve.wait(c.dve.mark())
    c.dve.reduce(total, split(gate, NT), ALU.add)
    c.dve.wait(c.dve.mark())
    c.dve.recip(over, total)
    c.dve.wait(c.dve.mark())
    c.dve.tt(split(gate, NT), split(gate, NT), stretch(over, E3), ALU.mult)
    gate_done = c.dve.mark()
    c.pe.wait(gate_done, s.free[0])
    for t in range(NT):
        c.pe.turn(b0[0:E3, t * P:(t + 1) * P], gate[:, t * E3:(t + 1) * E3], c.shared.ident)
    turned = c.pe.mark()
    gT = s.w[0:E3, BANK:BANK + N]
    c.act.wait(turned)
    c.act.act(gT, b0[0:E3, 0:N], ACT.Copy)
    s.free[0] = gT_done = c.act.mark()
    for t in range(NT):
        acc = s.w[:, t * P:(t + 1) * P]
        added = gate_done
        for j in range(2):
            c.pe.wait(normed, s.free[j])
            c.pe.mm(s.bank[j][:, :], s.xn[:, t * P:(t + 1) * P], W("expert_w")[:, j * BANK:(j + 1) * BANK])
            made = c.pe.mark()
            for i in range(4):
                e = 4 * j + i
                src, factor = s.bank[j][:, i * P:(i + 1) * P], gate[:, t * E3 + e:t * E3 + e + 1]
                c.dve.wait(made, added)
                if e == 0:
                    c.dve.ts(acc, src, factor, None, ALU.mult)
                else:
                    c.dve.stt(acc, src, factor, acc, ALU.mult, ALU.add)
                added = c.dve.mark()
            s.free[j] = added
        c.pe.wait(gT_done, *s.free)
        c.pe.mm(b0[:, 0:P], gT[:, t * P:(t + 1) * P], W("expert_b")[0:E3, :])
        c.pe.turn(b1[:, 0:P], s.x[:, t * P:(t + 1) * P], c.shared.ident)
        made = c.pe.mark()
        c.dve.wait(made, added)
        c.dve.tt(acc, acc, b0[:, 0:P], ALU.add)
        s.free[0] = c.dve.mark()
        res = s.w[:, 3 * P + BANK + t * P:4 * P + BANK + t * P]
        c.dve.wait(s.free[0])
        c.dve.stt(res, acc, c.shared.gates[:, B + 3:B + 4], b1[:, 0:P], ALU.mult, ALU.add)
        s.free[1] = s.ready = c.dve.mark()
        c.sync.wait(s.ready)
        dst, sem = c.shared.out[s.b, t * P:(t + 1) * P, :], c.shared.s_out
        c.sync.put(lambda e, dst=dst, res=res: e.dma_start(dst, res).then_inc(sem, 16))


def build(nc, x_in, ctx_in, gates_in, const_in, packs_in, out):
    with ExitStack() as stack:
        def sb(name, cols):
            return stack.enter_context(nc.sbuf_tensor(name, [P, cols], F32))

        def sem(name):
            return stack.enter_context(nc.semaphore(name))

        h = Shared()
        setup = Program(h)
        s_const, s_out = sem("const_loaded"), sem("out_stored")
        s_slot = [sem("slot0_loaded"), sem("slot1_loaded")]
        const = sb("constants", CONST.n)
        h.gates = sb("gate_columns", 2 * B)
        slots = [sb("slot0", SLOTS[0]), sb("slot1", SLOTS[1])]
        h.tables = [sb("rotary0", 4 * NT * DH), sb("rotary1", 4 * NT * DH)]
        powers = sb("powers", 64)
        h.ident, h.mean, h.ones, h.band, h.tri, h.k, h.invk, h.headmask = (
            CONST(const, n) for n in ("ident", "mean", "ones", "band", "tri", "k", "invk", "headmask"))
        rotary = [CONST(const, n) for n in ("qcos", "kcos", "qsin", "ksin")]
        h.minus_half, h.half = powers[:, 0:32], powers[:, 32:64]
        h.out, h.s_out = out, s_out

        seqs = []
        for b in range(B):
            s = Sequence()
            s.b = b
            s.x, s.ctx, s.xn, s.z, s.zs = (sb(f"{n}{b}", N) for n in ("x", "ctx", "xn", "z", "zs"))
            s.kT, s.v, s.oT = (sb(f"{n}{b}", 4 * N) for n in ("kT", "v", "oT"))
            s.qz = sb(f"qz{b}", 2 * BANK)
            s.w = sb(f"work{b}", 6 * BANK)
            s.sm = sb(f"small{b}", 512)
            s.before = sb(f"window_before{b}", 8 * EARLY)
            s.bank = [stack.enter_context(nc.psum_tensor(f"bank{b}_{i}", [P, BANK], F32)) for i in range(2)]
            s_x = sem(f"x{b}_loaded")
            cols = slice(b * N, (b + 1) * N)
            setup.sync.put(lambda e, s=s, cols=cols, s_x=s_x: e.dma_start(s.x[:, :], x_in[:, cols]).then_inc(s_x, 16))
            s.x_ready = setup.sync.load(lambda e, s=s, cols=cols: e.dma_start(s.ctx[:, :], ctx_in[:, cols]), s_x, 32, 2500.0)
            if b == 0:
                setup.sync.put(lambda e: e.dma_start(const[:, :], const_in).then_inc(s_const, 16))
                h.const_ready = setup.sync.load(lambda e: e.dma_start(h.gates[:, :], gates_in), s_const, 32, 3000.0)
            setup.pool.fill(s.qz[:, :], 0.0)
            setup.pool.fill(s.before[:, :], 0.0)
            s.qz_zero = setup.pool.mark()
            seqs.append(s)
        setup.dve.fill(h.minus_half, -0.5)
        setup.dve.fill(h.half, 0.5)
        h.powers_ready = setup.dve.mark()
        setup.act.wait(h.const_ready)
        setup.act.act(h.gates[:, :], h.gates[:, :], ACT.Tanh)
        h.gates_ready = setup.act.mark()

        weights, done, loader = [], [[] for _ in STAGES], Program(h)
        for stage, pack in enumerate(STAGES):
            if stage >= 2:
                loader.sync.wait()
                loader.sync.steps[-1][0] = done[stage - 2]
            dst, src = slots[stage % 2][:, 0:pack.n], packs_in[stage]
            weights.append(loader.sync.load(lambda e, dst=dst, src=src: e.dma_start(dst, src), s_slot[stage % 2],
                                            16 * (stage // 2 + 1), 15000.0 if stage < 2 else 0.0))

        mask = L0X(slots[0], "mask")
        setup.pool.wait(weights[0])
        setup.pool.ts(mask, mask, -1.0, 1.0, ALU.mult, ALU.add)
        setup.pool.wait(setup.pool.mark())
        setup.pool.ts(mask, mask, -1e10, None, ALU.mult)
        h.mask_ready = setup.pool.mark()

        def rotary_tables(c, stage):
            sc = split(L0F(slots[stage % 2], "scales"), 4)
            tab = h.tables[stage % 2][:, :].rearrange("p (a t d) -> p a t d", a=4, t=NT)
            c.pool.wait(h.const_ready, weights[stage])
            for a, base in enumerate(rotary):
                for t in range(NT):
                    c.pool.tt(tab[:, a, t, :], split(base, NT)[:, t, :], sc[:, a, :], ALU.mult)
            return c.pool.mark()

        table_ready, programs = {}, []
        for s in seqs:
            c, s.beside = Program(h), Program(h)
            s.ready, s.free = s.x_ready, [h.powers_ready, h.powers_ready]
            for stage, pack in enumerate(STAGES):
                s.W = lambda name, pack=pack, stage=stage: pack(slots[stage % 2], name)
                s.weights = weights[stage]
                if stage == 0:
                    cross_attention_0(c, s)
                elif stage <= DEPTH:
                    if s.b == 0:
                        table_ready[stage] = rotary_tables(c, stage)
                    s.table_ready = table_ready[stage]
                    local_layer(c, s, stage)
                elif pack is MIX1:
                    cross_attention_1(c, s)
                    mixture_1(c, s)
                    cross_attention_2(c, s)
                elif pack is L2F:
                    mixture_2(c, s)
                else:
                    cross_attention_3(c, s)
                    mixture_3(c, s)
                done[stage].append(s.ready)
            programs += [c.streams, s.beside.streams]

        engines = [Engine(sem(n)) for n in ("pe_steps", "act_steps", "dve_steps", "pool_steps", "sync_steps")]
        in_order_of_issue(engines, [setup.streams, loader.streams] + programs)

        block = stack.enter_context(nc.Block())

        @block.tensor
        def _(e):
            engines[0].play(e)

        @block.scalar
        def _(e):
            engines[1].play(e)

        @block.vector
        def _(e):
            engines[2].play(e)

        @block.gpsimd
        def _(e):
            engines[3].play(e)

        @block.sync
        def _(e):
            engines[4].play(e)
            e.wait_ge(s_out, B * NT * 16)


def constants():
    f = np.float32
    c = {"ident": np.eye(P, dtype=f), "mean": np.full((P, P), 1.0 / P, f), "ones": np.ones((P, P), f)}
    half = np.arange(0, DH, 2, dtype=f)
    freqs = np.arange(N, dtype=f)[:, None] * (f(1.0) / np.power(f(10000.0), half / f(DH)))[None, :]
    base = (half + f(0.4 * DH)) / f(1.4 * DH)
    power = (np.arange(N, dtype=f) - f(N // 2)) / f(WINDOW // 2)
    scale = np.power(base[None, :], power[:, None]).astype(f)
    cos, sin = np.cos(freqs), np.sin(freqs)
    for name, s in (("q", scale * f(QK_SCALE)), ("k", f(1.0) / scale)):
        for part, table in (("cos", np.concatenate([cos * s, cos * s], 1)),
                            ("sin", np.concatenate([-sin * s, sin * s], 1))):
            c[name + part] = table.reshape(NT, P, DH).transpose(1, 0, 2).reshape(P, NT * DH)
    q, k = np.arange(P)[:, None], np.arange(P)[None, :]
    band = np.where((k <= q) & (k >= q - WINDOW), 0.0, MASKED).astype(f)
    second = band.copy()
    before = (q < WINDOW) & (k >= P - WINDOW) & (k - P >= q - WINDOW)
    second[before] = 0.0
    c["band"] = np.concatenate([band, second], 1)
    c["tri"] = np.broadcast_to((np.arange(E2)[None, :] < np.arange(E2)[:, None]).astype(f).reshape(1, -1), (P, E2 * E2))
    ks = np.arange(1, E1 + 1, dtype=f)
    c["k"], c["invk"] = np.broadcast_to(ks, (P, E1)), np.broadcast_to(f(1.0) / ks, (P, E1))
    c["headmask"] = (np.arange(P)[:, None] // DH3 == np.arange(H3)[None, :]).astype(f)
    return c


def packed(columns, arrays):
    out = np.zeros((P, columns.n), np.float32)
    for name, (start, width) in columns.at.items():
        a = arrays[name]
        a = a.reshape(a.shape[0], -1)
        assert a.shape[1] == width, (name, a.shape, width)
        out[:a.shape[0], start:start + width] = a
    return out


def chunked(a, rows=P):
    n = -(-a.shape[0] // rows)
    full = np.zeros((n * rows,) + a.shape[1:], a.dtype)
    full[:a.shape[0]] = a
    return full.reshape(n, rows, -1).transpose(1, 0, 2).reshape(rows, -1)


def column(a):
    return chunked(a.reshape(-1, 1))


def row(a):
    return np.broadcast_to(a.reshape(1, -1), (P, a.size))


def layouts(i):
    heads = lambda w: w.transpose(1, 0, 2).reshape(D, INNER)
    packs = [packed(L0X, {
        "Wq": heads(i["L0_xattn_Wq"]), "Wk": heads(i["L0_xattn_Wk"]), "Wv": heads(i["L0_xattn_Wv"]),
        "Wo": chunked(i["L0_xattn_Wo"].reshape(DH, H0, D).transpose(1, 0, 2).reshape(INNER, D)),
        "mask": chunked(i["mask_SxS2_ff1"]), "bq": column(i["L0_xattn_bq"]), "bk": column(i["L0_xattn_bk"]),
        "bv": column(i["L0_xattn_bv"]), "bo": column(i["L0_xattn_bo"])})]
    for d in range(DEPTH):
        qs, ks = i["L0_ffn_q_scale"][d], i["L0_ffn_k_scale"][d]
        swap = lambda a: np.concatenate([a[DH // 2:], a[:DH // 2]])
        b1 = i["L0_ffn_b1"][d]
        packs.append(packed(L0F, {
            "Wqkv": i["L0_ffn_Wqkv"][d], "Wo": chunked(i["L0_ffn_Wo"][d]), "W1": i["L0_ffn_W1"][d],
            "W2": chunked(i["L0_ffn_W2"][d]), "scales": row(np.concatenate([qs, ks, swap(qs), swap(ks)])),
            "ln_g": column(i["L0_ffn_ln_g"][d]), "ln_b": column(i["L0_ffn_ln_b"][d]),
            "b1": np.concatenate([column(b1[:FF]), column(b1[FF:])], 1), "b2": column(i["L0_ffn_b2"][d])}))
    one = {}
    for n in ("q_c", "k_s", "v_s", "q_s", "k_c", "v_c"):
        one["W" + n], one["b" + n] = i[f"L1_xattn_W{n}"].T, column(i[f"L1_xattn_b{n}"])
    wg = i["L1_xattn_Wg"].T
    one.update({
        "Wg_a": wg[:D], "Wg_b": wg[D:], "bg": column(i["L1_xattn_bg"]), "proj": i["L1_ffn_proj"],
        "C1": i["L1_ffn_C1"], "C2": i["L1_ffn_C2"], "Win1": i["L1_ffn_Win1"][:D], "bin1": i["L1_ffn_Win1"][D:].T,
        "Wout1": i["L1_ffn_Wout1"].T, "Win2": chunked(i["L1_ffn_Win2"][:O1]), "bin2": i["L1_ffn_Win2"][O1:].T,
        "Wout2": i["L1_ffn_Wout2"].T, "gamma": column(i["L2_xattn_gamma"]), "beta": column(i["L2_xattn_beta"])})
    for n in "qkv":
        one["W" + n], one["b" + n] = i["L2_xattn_W" + n], column(i["L2_xattn_b" + n])
    packs.append(packed(MIX1, one))
    two = {}
    for n in "13":
        w = np.concatenate([i[f"L2_ffn_w{n}"], i[f"L2_ffn_sw{n}"][None]], 0)
        b = np.concatenate([i[f"L2_ffn_b{n}"], i[f"L2_ffn_sb{n}"][None]], 0)
        two["w" + n], two["b" + n] = w.transpose(1, 0, 2), column(b)
    w2 = np.concatenate([i["L2_ffn_w2"], i["L2_ffn_sw2"][None]], 0)
    b2 = np.concatenate([i["L2_ffn_b2"], i["L2_ffn_sb2"][None]], 0)
    pick = np.arange(P)[:, None] == np.arange(HT2 * P)[None, :] // HID2
    two.update({"w2": chunked(w2.reshape(-1, D)), "pick": (pick & (np.arange(P)[:, None] <= E2)).astype(np.float32),
                "b2": b2, "gate_w": i["L2_ffn_gate_w"].T, "gate_b": row(i["L2_ffn_gate_b"])})
    packs.append(packed(L2F, two))
    kv, bkv = i["L3_xattn_Wkv"], i["L3_xattn_bkv"]
    packs.append(packed(L3, {
        "Wq": i["L3_xattn_Wq"], "Wk": kv[:, :D], "Wv": kv[:, D:], "Wo": i["L3_xattn_Wo"],
        "bq": column(i["L3_xattn_bq"]), "bk": column(bkv[:D]), "bv": row(bkv[D:]), "bo": column(i["L3_xattn_bo"]),
        "gate_w": i["L3_ffn_gate_w"].T, "gate_b": row(i["L3_ffn_gate_b"]),
        "expert_w": i["L3_ffn_expert_w"].transpose(1, 0, 2), "expert_b": i["L3_ffn_expert_b"]}))
    return packs


def kernel(**inputs):
    import concourse.bacc as bacc
    from concourse.bass_utils import run_bass_kernel_spmd

    i = {name: np.asarray(a) for name, a in inputs.items()}
    arrays = {"x_t": i["x"].transpose(2, 0, 1).reshape(D, B * N),
              "ctx_t": i["ctx_1024"].transpose(2, 0, 1).reshape(D, B * N),
              "gates": np.concatenate([row(i["g_xattn"]), row(i["g_ffn"])], 1),
              "const": packed(CONST, constants())}
    for n, p in enumerate(layouts(i)):
        arrays[f"pack{n}"] = p
    arrays = {n: np.ascontiguousarray(a) for n, a in arrays.items()}
    nc = bacc.Bacc("TRN2", target_bir_lowering=False, num_devices=1)
    aps = {n: nc.dram_tensor(f"in_{n}_dram", a.shape, F32, kind="ExternalInput").ap() for n, a in arrays.items()}
    out = nc.dram_tensor("out_dram", (B, N, D), F32, kind="ExternalOutput").ap()
    build(nc, aps["x_t"], aps["ctx_t"], aps["gates"], aps["const"],
          [aps[f"pack{n}"] for n in range(len(STAGES))], out)
    r = run_bass_kernel_spmd(nc, [{f"in_{n}_dram": a for n, a in arrays.items()}], core_ids=[0])
    return r.results[0]["out_dram"]
```
